# Optimizing a Trainium2 kernel written in Bass

```python
import numpy as np
import jax
import jax.numpy as jnp

def _softmax(x, axis=-1):
    return jax.nn.softmax(x, axis=axis)

def _gelu(x):
    return jax.nn.gelu(x, approximate=True)

def _silu(x):
    return jax.nn.silu(x)

def _sigmoid(x):
    return jax.nn.sigmoid(x)

def _layernorm(x, axis=-1, eps=1e-05):
    m = jnp.mean(x, axis=axis, keepdims=True)
    v = jnp.var(x, axis=axis, keepdims=True)
    return (x - m) / jnp.sqrt(v + eps)

def _scatter_add(tgt, idx, src, axis=0):
    return tgt.at[idx].add(src)

def _segment_sum(src, seg, n):
    return jax.ops.segment_sum(src, seg, n)
kernel_name = 'mk_vit_tower_postln_d1_tok_img768_r4_ba472e'

def setup_inputs(seed: int=0):
    np.random.seed(seed)
    _w = jnp.asarray

    def _rec_inputs():
        import jax
        import jax.numpy as jnp
        _rk = jax.random.key(seed)
        x = -0.000356955 + 1 * jax.random.normal(jax.random.fold_in(_rk, 1), (16, 3, 112, 112), jnp.float32)
        return x
    x = _rec_inputs()

    def _L0_tok_setup():
        import jax, jax.numpy as jnp
        import numpy as np
        IMG = 224
        PATCH = 16
        C_IN = 3
        EMB = 192
        B = 128
        K = PATCH * PATCH * C_IN

        def _patchify(x):
            Bn, C, H, Wd = x.shape
            nH, nW = (H // PATCH, Wd // PATCH)
            x = x.reshape(Bn, C, nH, PATCH, nW, PATCH)
            x = x.transpose(0, 2, 4, 3, 5, 1)
            return x.reshape(Bn, nH * nW, PATCH * PATCH * C)
        key = jax.random.key(seed)
        k1, k2 = jax.random.split(key)
        x = jax.random.normal(k1, (B, C_IN, IMG, IMG), dtype=jnp.float32)
        W = jax.random.normal(k2, (EMB, K), dtype=jnp.float32) * (1.0 / np.sqrt(K))
        b = jnp.zeros((EMB,), dtype=jnp.float32)
        return {'x': x, 'W': W, 'b': b}
    _L0_tok_all = _L0_tok_setup()
    _L0_tok_in = {k: v for k, v in _L0_tok_all.items() if k in ('W', 'b')}
    del _L0_tok_all

    def _L0_attn_setup():
        import jax, jax.numpy as jnp
        import numpy as np

        def _rotate_half(x):
            a, b = jnp.split(x, 2, axis=-1)
            return jnp.concatenate([-b, a], axis=-1)

        def _rope_tables(L, d, dtype):
            inv = 1.0 / 10000.0 ** (jnp.arange(0, d, 2, dtype=jnp.float32) / d)
            ang = jnp.arange(L, dtype=jnp.float32)[:, None] * inv[None, :]
            cos = jnp.repeat(jnp.cos(ang), 2, axis=-1)[None, :, None, :].astype(dtype)
            sin = jnp.repeat(jnp.sin(ang), 2, axis=-1)[None, :, None, :].astype(dtype)
            return (cos, sin)

        def _forward(X, Wq, Wk, Wv, Wu, Wg, Wo, prior_mu, prior_log_tau):
            B, L, D = X.shape
            h = prior_mu.shape[2]
            d = D // h
            eps = 1e-12
            q = (X @ Wq.T).reshape(B, L, h, d)
            k = (X @ Wk.T).reshape(B, L, h, d)
            v = (X @ Wv.T).reshape(B, L, h, d)
            u = (X @ Wu.T).reshape(B, L, h, d)
            gate = (X @ Wg.T).reshape(B, L, h, 3)
            t = jnp.arange(1, L + 1, dtype=X.dtype).reshape(1, L, 1, 1)
            log_tau = jnp.exp(jnp.clip(prior_log_tau, -50.0, 30.0))
            u_sum = jnp.cumsum(u, axis=1)
            bar_u = (log_tau * prior_mu + u_sum) / (log_tau + t)
            s_i = -jnp.sum(u * bar_u, axis=-1, keepdims=True) / np.float32(np.sqrt(d))
            cos, sin = _rope_tables(L, d, X.dtype)
            q = q * cos + _rotate_half(q) * sin
            k = k * cos + _rotate_half(k) * sin
            q = q / jnp.maximum(jnp.linalg.norm(q, axis=-1, keepdims=True), eps)
            k = k / jnp.maximum(jnp.linalg.norm(k, axis=-1, keepdims=True), eps)
            s_max = jax.lax.stop_gradient(jnp.max(s_i, axis=1, keepdims=True))
            exp_s = jnp.exp(s_i - s_max)
            E_t = jnp.cumsum(exp_s, axis=1)
            P_t = jnp.cumsum(s_i, axis=1)
            kv = jnp.einsum('blhd,blhe->blhde', k, v)
            F_t = jnp.cumsum(exp_s[..., None] * kv, axis=1)
            G_t = jnp.cumsum(s_i[..., None] * kv, axis=1)
            H_t = jnp.cumsum(kv, axis=1)
            sig1 = jax.nn.sigmoid(gate[..., 0:1])
            sigh = jax.nn.sigmoid(gate[..., 1:2])
            alpha = sigh / (E_t + eps)
            beta = (sig1 - sigh) / t
            gamma = -((beta * P_t + sigh) / t)
            M = alpha[..., None] * F_t + beta[..., None] * G_t + gamma[..., None] * H_t
            out = jnp.einsum('blhd,blhde->blhe', q, M)
            mu = jnp.mean(out, axis=-1, keepdims=True)
            var = jnp.mean(jnp.square(out - mu), axis=-1, keepdims=True)
            out = (out - mu) / jnp.sqrt(var + 1e-05)
            return out.reshape(B, L, D) @ Wo.T
        key = jax.random.key(seed)
        ks = jax.random.split(key, 7)
        B, L, D, h = (1, 256, 192, 12)
        d = D // h
        s = 0.02
        return {'X': jax.random.normal(ks[0], (B, L, D), jnp.float32), 'Wq': jax.random.normal(ks[1], (D, D), jnp.float32) * s, 'Wk': jax.random.normal(ks[2], (D, D), jnp.float32) * s, 'Wv': jax.random.normal(ks[3], (D, D), jnp.float32) * s, 'Wu': jax.random.normal(ks[4], (D, D), jnp.float32) * s, 'Wg': jax.random.normal(ks[5], (3 * h, D), jnp.float32) * s, 'Wo': jax.random.normal(ks[6], (D, D), jnp.float32) * s, 'prior_mu': jnp.zeros((1, 1, h, d), jnp.float32), 'prior_log_tau': jnp.zeros((1, 1, h, 1), jnp.float32)}
    _L0_attn_all = _L0_attn_setup()
    _L0_attn_in = {k: v for k, v in _L0_attn_all.items() if k in ('Wq', 'Wk', 'Wv', 'Wu', 'Wg', 'Wo', 'prior_mu', 'prior_log_tau')}
    del _L0_attn_all

    def _L0_ffn_setup():
        import math
        import jax, jax.numpy as jnp
        import numpy as np
        B, L, D = (8, 1024, 192)
        E = 16
        TOP_K = 2
        F_EXP = 4 * D
        F_SH = F_EXP * 2 // 4
        key = jax.random.key(seed)
        ks = jax.random.split(key, 8)
        s = lambda fan_in: 1.0 / math.sqrt(fan_in)
        return {'hidden_states': jax.random.normal(ks[0], (B, L, D), jnp.float32), 'gate_weight': jax.random.uniform(ks[1], (E, D), jnp.float32, -s(D), s(D)), 'Wg': jax.random.uniform(ks[2], (E, F_EXP, D), jnp.float32, -s(D), s(D)), 'Wu': jax.random.uniform(ks[3], (E, F_EXP, D), jnp.float32, -s(D), s(D)), 'Wd': jax.random.uniform(ks[4], (E, D, F_EXP), jnp.float32, -s(F_EXP), s(F_EXP)), 'Ws_g': jax.random.uniform(ks[5], (F_SH, D), jnp.float32, -s(D), s(D)), 'Ws_u': jax.random.uniform(ks[6], (F_SH, D), jnp.float32, -s(D), s(D)), 'Ws_d': jax.random.uniform(ks[7], (D, F_SH), jnp.float32, -s(F_SH), s(F_SH))}
    _L0_ffn_all = _L0_ffn_setup()
    _L0_ffn_in = {k: v for k, v in _L0_ffn_all.items() if k in ('gate_weight', 'Wg', 'Wu', 'Wd', 'Ws_g', 'Ws_u', 'Ws_d')}
    del _L0_ffn_all
    return {'x': x, 'L0_tok_W': _L0_tok_in['W'], 'L0_tok_b': _L0_tok_in['b'], 'L0_attn_Wq': _L0_attn_in['Wq'], 'L0_attn_Wk': _L0_attn_in['Wk'], 'L0_attn_Wv': _L0_attn_in['Wv'], 'L0_attn_Wu': _L0_attn_in['Wu'], 'L0_attn_Wg': _L0_attn_in['Wg'], 'L0_attn_Wo': _L0_attn_in['Wo'], 'L0_attn_prior_mu': _L0_attn_in['prior_mu'], 'L0_attn_prior_log_tau': _L0_attn_in['prior_log_tau'], 'L0_ffn_gate_weight': _L0_ffn_in['gate_weight'], 'L0_ffn_Wg': _L0_ffn_in['Wg'], 'L0_ffn_Wu': _L0_ffn_in['Wu'], 'L0_ffn_Wd': _L0_ffn_in['Wd'], 'L0_ffn_Ws_g': _L0_ffn_in['Ws_g'], 'L0_ffn_Ws_u': _L0_ffn_in['Ws_u'], 'L0_ffn_Ws_d': _L0_ffn_in['Ws_d']}

def reference(x, L0_tok_W, L0_tok_b, L0_attn_Wq, L0_attn_Wk, L0_attn_Wv, L0_attn_Wu, L0_attn_Wg, L0_attn_Wo, L0_attn_prior_mu, L0_attn_prior_log_tau, L0_ffn_gate_weight, L0_ffn_Wg, L0_ffn_Wu, L0_ffn_Wd, L0_ffn_Ws_g, L0_ffn_Ws_u, L0_ffn_Ws_d):
    import jax
    import jax.numpy as jnp

    def _L0_tok_ref(x, W, b):
        import jax, jax.numpy as jnp
        import numpy as np
        IMG = 224
        PATCH = 16
        C_IN = 3
        EMB = 192
        B = 128
        K = PATCH * PATCH * C_IN

        def _patchify(x):
            Bn, C, H, Wd = x.shape
            nH, nW = (H // PATCH, Wd // PATCH)
            x = x.reshape(Bn, C, nH, PATCH, nW, PATCH)
            x = x.transpose(0, 2, 4, 3, 5, 1)
            return x.reshape(Bn, nH * nW, PATCH * PATCH * C)
        patches = _patchify(x)
        return jnp.einsum('bnk,ek->bne', patches, W) + b

    def _L0_attn_ref(X, Wq, Wk, Wv, Wu, Wg, Wo, prior_mu, prior_log_tau):
        import jax, jax.numpy as jnp
        import numpy as np

        def _rotate_half(x):
            a, b = jnp.split(x, 2, axis=-1)
            return jnp.concatenate([-b, a], axis=-1)

        def _rope_tables(L, d, dtype):
            inv = 1.0 / 10000.0 ** (jnp.arange(0, d, 2, dtype=jnp.float32) / d)
            ang = jnp.arange(L, dtype=jnp.float32)[:, None] * inv[None, :]
            cos = jnp.repeat(jnp.cos(ang), 2, axis=-1)[None, :, None, :].astype(dtype)
            sin = jnp.repeat(jnp.sin(ang), 2, axis=-1)[None, :, None, :].astype(dtype)
            return (cos, sin)

        def _forward(X, Wq, Wk, Wv, Wu, Wg, Wo, prior_mu, prior_log_tau):
            B, L, D = X.shape
            h = prior_mu.shape[2]
            d = D // h
            eps = 1e-12
            q = (X @ Wq.T).reshape(B, L, h, d)
            k = (X @ Wk.T).reshape(B, L, h, d)
            v = (X @ Wv.T).reshape(B, L, h, d)
            u = (X @ Wu.T).reshape(B, L, h, d)
            gate = (X @ Wg.T).reshape(B, L, h, 3)
            t = jnp.arange(1, L + 1, dtype=X.dtype).reshape(1, L, 1, 1)
            log_tau = jnp.exp(jnp.clip(prior_log_tau, -50.0, 30.0))
            u_sum = jnp.cumsum(u, axis=1)
            bar_u = (log_tau * prior_mu + u_sum) / (log_tau + t)
            s_i = -jnp.sum(u * bar_u, axis=-1, keepdims=True) / np.float32(np.sqrt(d))
            cos, sin = _rope_tables(L, d, X.dtype)
            q = q * cos + _rotate_half(q) * sin
            k = k * cos + _rotate_half(k) * sin
            q = q / jnp.maximum(jnp.linalg.norm(q, axis=-1, keepdims=True), eps)
            k = k / jnp.maximum(jnp.linalg.norm(k, axis=-1, keepdims=True), eps)
            s_max = jax.lax.stop_gradient(jnp.max(s_i, axis=1, keepdims=True))
            exp_s = jnp.exp(s_i - s_max)
            E_t = jnp.cumsum(exp_s, axis=1)
            P_t = jnp.cumsum(s_i, axis=1)
            kv = jnp.einsum('blhd,blhe->blhde', k, v)
            F_t = jnp.cumsum(exp_s[..., None] * kv, axis=1)
            G_t = jnp.cumsum(s_i[..., None] * kv, axis=1)
            H_t = jnp.cumsum(kv, axis=1)
            sig1 = jax.nn.sigmoid(gate[..., 0:1])
            sigh = jax.nn.sigmoid(gate[..., 1:2])
            alpha = sigh / (E_t + eps)
            beta = (sig1 - sigh) / t
            gamma = -((beta * P_t + sigh) / t)
            M = alpha[..., None] * F_t + beta[..., None] * G_t + gamma[..., None] * H_t
            out = jnp.einsum('blhd,blhde->blhe', q, M)
            mu = jnp.mean(out, axis=-1, keepdims=True)
            var = jnp.mean(jnp.square(out - mu), axis=-1, keepdims=True)
            out = (out - mu) / jnp.sqrt(var + 1e-05)
            return out.reshape(B, L, D) @ Wo.T
        return _forward(X, Wq, Wk, Wv, Wu, Wg, Wo, prior_mu, prior_log_tau)

    def _L0_ffn_ref(hidden_states, gate_weight, Wg, Wu, Wd, Ws_g, Ws_u, Ws_d):
        import math
        import jax, jax.numpy as jnp
        import numpy as np
        B, L, D = (8, 1024, 192)
        E = 16
        TOP_K = 2
        F_EXP = 4 * D
        F_SH = F_EXP * 2 // 4
        b, l, d = hidden_states.shape
        n = b * l
        x = hidden_states.reshape(n, d)
        scores = jax.nn.sigmoid(x @ gate_weight.T)
        capacity = math.ceil(n / E * TOP_K)
        topk_score, topk_ids = jax.lax.top_k(scores.T, capacity)
        xg = x[topk_ids]
        gate = jax.nn.silu(jnp.einsum('ecd,efd->ecf', xg, Wg))
        up = jnp.einsum('ecd,efd->ecf', xg, Wu)
        out = jnp.einsum('ecf,edf->ecd', gate * up, Wd)
        out = out * topk_score[..., None]
        y = jnp.zeros((n, d), x.dtype).at[topk_ids.reshape(-1)].add(out.reshape(-1, d))
        y = y.reshape(b, l, d)
        shared = jax.nn.silu(hidden_states @ Ws_g.T) * (hidden_states @ Ws_u.T) @ Ws_d.T
        return y + shared
    h = _L0_tok_ref(x, L0_tok_W, L0_tok_b)
    h = _layernorm(h + _L0_attn_ref(h, L0_attn_Wq, L0_attn_Wk, L0_attn_Wv, L0_attn_Wu, L0_attn_Wg, L0_attn_Wo, L0_attn_prior_mu, L0_attn_prior_log_tau), axis=-1)
    h = _layernorm(h + _L0_ffn_ref(h, L0_ffn_gate_weight, L0_ffn_Wg, L0_ffn_Wu, L0_ffn_Wd, L0_ffn_Ws_g, L0_ffn_Ws_u, L0_ffn_Ws_d), axis=-1)
    return h

_drawn_inputs = setup_inputs


def setup_inputs(seed=0):
    import zlib

    import numpy as np

    out = dict(_drawn_inputs(seed))
    spreads = {'L0_tok_b': (0.0, 0.1),
     'L0_attn_prior_mu': (0.0, 0.8),
     'L0_attn_prior_log_tau': (0.0, 0.8)}
    factors = {'L0_attn_Wg': 7.687}
    for name, (base, spread) in spreads.items():
        noise = np.random.default_rng([zlib.crc32(name.encode()), seed]).standard_normal(out[name].shape)
        drawn = base * np.exp(spread * noise) if base else spread * noise
        out[name] = jnp.asarray(drawn.astype(out[name].dtype))
    for name, factor in factors.items():
        out[name] = (out[name] * factor).astype(out[name].dtype)
    return out
```

```python
from contextlib import ExitStack

import concourse.bass as bass
from concourse import mybir

ALU = mybir.AluOpType
ACT = mybir.ActivationFunctionType
AX_X = mybir.AxisListType.X
F32 = mybir.dt.float32
I32 = mybir.dt.int32
U32 = mybir.dt.uint32
F32R = mybir.dt.float32r

IMAGES, PATCH, SIDE = 16, 16, 7
L = SIDE * SIDE
TOKENS = IMAGES * L
PIX = 3 * PATCH * PATCH
D = 192
H, DH = 12, 16
TT = 2 * L
NT = TOKENS // TT
KX = PIX // 128
DK = D // 2
E = 16
CAP = -(-TOKENS * 2 // E)
F = 4 * D
FK = F // 128
FS = F // 2
FSK = FS // 128
HALF = TOKENS // 2
ROUNDS = -(-CAP // 8)
YT = 112
NY = TOKENS // YT
CH = 256
NCH = F // CH
G6 = 6
EPS = 1e-5
RING = 4
SMALL = 4

C_ID, C_TRI, C_REV = 0, 128, 128 + TT
C_COS = C_REV + CAP
C_SIN = C_COS + DH
C_HM = C_SIN + DH
C_T = C_HM + G6
C_RT = C_T + 1
C_ONE = C_RT + 1
C_N = C_ONE + 128
P_B, P_MU, P_TAU, P_N = 0, D, 2 * D, 2 * D + H
QK, VU = 2 * D, 2 * D + 2 * H


def build(nc, x, w_patch, w_proj, w_o, params, consts, w_gate, w_gu, w_d, ws_gu, ws_d, out):
    h1_dram = nc.dram_tensor("h1_rows", (TOKENS, D), F32, kind="Internal").ap()
    y_dram = nc.dram_tensor("y_rows", (TOKENS, D), F32, kind="Internal").ap()
    with ExitStack() as ctx:
        def sb(name, shape, dt=F32):
            return ctx.enter_context(nc.sbuf_tensor(name, shape, dt))

        def sem(name):
            return ctx.enter_context(nc.semaphore(name))

        bank = [ctx.enter_context(nc.psum_tensor(f"bank{i}", [128, 512], F32)) for i in range(8)]

        cst = sb("cst", [128, C_N])
        wgate_sb = sb("wgate_sb", [DK, 2, 2 * E])
        h1 = sb("h1", [TT, NT, D])
        h1T = sb("h1T", [DK, 2, TOKENS])
        wgu_sb = sb("wgu_sb", [DK, 2, 2, 2 * F])
        wd_sb = sb("wd_sb", [128, RING, FK, D])
        wsgu_sb = sb("wsgu_sb", [DK, 2, 2 * FS])
        wsd_sb = sb("wsd_sb", [128, FSK, D])
        silu_s = sb("silu_s", [128, 2, HALF])
        hsT = sb("hsT", [128, FSK, TOKENS])

        attention = ctx.enter_context(ExitStack())

        def sa(name, shape, dt=F32):
            return attention.enter_context(nc.sbuf_tensor(name, shape, dt))

        par = sa("par", [TT, P_N])
        wo_sb = sa("wo_sb", [DK, 2, D])
        h0 = sa("h0", [TT, NT, D])
        qk = sa("qk", [TT, NT, QK])
        norm2 = sa("norm2", [TT, NT, 2 * H])
        rnorm = sa("rnorm", [TT, NT, 2 * H])
        vug = sa("vug", [TT, NT, VU])
        s_raw = sa("s_raw", [TT, NT, H])
        es_s = sa("es_s", [TT, 2, NT * H])
        tau = sa("tau", [TT, 3, H])
        mu_row = sa("mu_row", [1, D])
        wv_mean = sa("wv_mean", [DK, 2, H])
        sT = sa("sT", [NT * H, 3, TT])
        s_max = sa("s_max", [NT * H, 2])
        gates = sa("gates", [TT, 3, NT, 2 * H])
        coef = sa("coef", [TT, NT * H, 3])
        vcoef = sa("vcoef", [TT, NT * H, 3])
        small = sa("small", [TT, 4, NT * H])

        projections = attention.enter_context(ExitStack())

        def sproj(name, shape, dt=F32):
            return projections.enter_context(nc.sbuf_tensor(name, shape, dt))

        x_sb = sproj("x_sb", [128, NT, KX * TT])
        wp_sb = sproj("wp_sb", [128, KX * D])
        wproj_sb = sproj("wproj_sb", [DK, 2, QK + VU])
        wproj_hi = sproj("wproj_hi", [DK, 2, QK + VU], F32R)
        wproj_lo = sproj("wproj_lo", [DK, 2, QK + VU], F32R)
        h0T_hi = sproj("h0T_hi", [DK, 2, 2 * TT], F32R)
        h0T_lo = sproj("h0T_lo", [DK, 2, 2 * TT], F32R)
        rope_a = sproj("rope_a", [TT, 2, QK])
        rope_b = sproj("rope_b", [TT, 2, QK])
        squares = sproj("squares", [TT, 2, QK])
        u_bar = sproj("u_bar", [TT, 2, D])
        projections.close()

        v3 = sa("v3", [TT, 2, (H + 1) * 3 * DH])
        qkT = sa("qkT", [DK, 2, 4 * TT])
        q_exp = sa("q_exp", [DK, 2, 2, G6 * TT])
        pT = sa("pT", [TT, 2, H * TT])
        mix = sa("mix", [TT, 2, H * 3 * DH])
        o_sum = sa("o_sum", [TT, 2, D])
        o_att = sa("o_att", [TT, SMALL, D])
        o_sq = sa("o_sq", [TT, 2, D])
        o_var = sa("o_var", [TT, SMALL, 3 * H])
        o_n = sa("o_n", [TT, SMALL, D])
        oT = sa("oT", [DK, 2, 2 * TT])
        r1 = sa("r1", [TT, SMALL, D])
        bn1 = sa("bn1", [TT, SMALL, 6])
        mv1 = sa("mv1", [TT, SMALL, 4])
        attention.close()

        w_hi = sb("w_hi", [DK, 2, 2, 2 * F], F32R)
        w_lo = sb("w_lo", [DK, 2, 2, 2 * F], F32R)
        rank_in = sb("rank_in", [64, HALF])
        top_val = sb("top_val", [48, 8 * ROUNDS])
        top_idx = sb("top_idx", [48, 8 * ROUNDS], U32)
        top_row = sb("top_row", [48, CAP])
        top_T = sb("top_T", [CAP, 2, 48])
        pick = sb("pick", [CAP, 5, E])
        row_i = sb("row_i", [CAP, E], I32)
        score = sb("score", [CAP, E])
        xg = sb("xg", [CAP, RING, D])
        x_hi = sb("x_hi", [DK, 2, 2 * CAP], F32R)
        x_lo = sb("x_lo", [DK, 2, 2 * CAP], F32R)
        silu_g = sb("silu_g", [CAP, NCH, CH])
        hid = sb("hid", [CAP, 2, F])
        hidT = sb("hidT", [128, FK, CAP])
        o_exp = sb("o_exp", [CAP, 2, D])
        y_base = sb("y_base", [TT, 2, NT, D])
        y = sb("y", [YT, NY, D])
        bn2 = sb("bn2", [YT, NY, 6])
        mv2 = sb("mv2", [YT, NY, 2])
        std2 = sb("std2", [YT, 3, NY])
        y_n = sb("y_n", [YT, NY, D])

        consts_in, wp_in, proj_in, rest_in = (sem(n) for n in ("consts_in", "wp_in", "proj_in", "rest_in"))
        x_in = [sem(f"x_in{j}") for j in range(NT)]
        h1_out = sem("h1_out")
        embed_done, h0_ready, h0T_psum, h0T_ready = (sem(n) for n in (
            "embed_done", "h0_ready", "h0T_psum", "h0T_ready"))
        qk_psum, vug_psum, qk_ready, qk_read, vug_ready, usum_done, s_ready, sq_ready, n2_ready = (sem(n) for n in (
            "qk_psum", "vug_psum", "qk_ready", "qk_read", "vug_ready", "usum_done", "s_ready", "sq_ready", "n2_ready"))
        tau_clip, tau_exp, tau_ready, wv_ready = (sem(n) for n in ("tau_clip", "tau_exp", "tau_ready", "wv_ready"))
        s_all, sT_psum, sT_sub, sT_exp, es_psum, es_ready, cum_done, coef_ready, gate_exp, norm_sqrt, vcoef_ready = (
            sem(n) for n in ("s_all", "sT_psum", "sT_sub", "sT_exp", "es_psum", "es_ready", "cum_done",
                             "coef_ready", "gate_exp", "norm_sqrt", "vcoef_ready"))
        qkT_psum, qkT_ready, q_exp_ready, score_done, p_ready, v3_ready, att_psum, mix_ready, osum_ready = (
            sem(n) for n in ("qkT_psum", "qkT_ready", "q_exp_ready", "score_done", "p_ready", "v3_ready",
                             "att_psum", "mix_ready", "osum_ready"))
        att_ready, osq_ready, ovar_ready, ostd_ready, on_ready, oT_psum, oT_ready, wo_done = (sem(n) for n in (
            "att_ready", "osq_ready", "ovar_ready", "ostd_ready", "on_ready", "oT_psum", "oT_ready", "wo_done"))
        r1_var, r1_std, r1_ready, h1_ready, h1T_psum, h1T_ready = (sem(n) for n in (
            "r1_var", "r1_std", "r1_ready", "h1_ready", "h1T_psum", "h1T_ready"))
        wo_in, wproj_hi_ready, wproj_lo_ready, h0T_hi_ready, q_exp_pool, v3_zero = (sem(n) for n in (
            "wo_in", "wproj_hi_ready", "wproj_lo_ready", "h0T_hi_ready", "q_exp_pool", "v3_zero"))
        ws_in = sem("ws_in")
        wgu_in = [sem(f"wgu_in{n}") for n in range(2)]
        wd_in = [sem(f"wd_in{n}") for n in range(RING)]
        xg_in = [sem(f"xg_in{n}") for n in range(RING)]
        logit_psum, logit_ready, shared_gu, silu_s_ready, hs_ready, top_ready, top_psum, topT_ready, rev_psum = (
            sem(n) for n in ("logit_psum", "logit_ready", "shared_gu", "silu_s_ready", "hs_ready", "top_ready",
                             "top_psum", "topT_ready", "rev_psum"))
        pick_ready, row_ready, score_ready, shared_y, base_ready, base_added, base_out, y_add, y_in = (
            sem(n) for n in ("pick_ready", "row_ready", "score_ready", "shared_y", "base_ready", "base_added",
                             "base_out", "y_add", "y_in"))
        x_psum, x_hi_ready, x_lo_ready, w_hi_ready, w_lo_ready, w_lo0_ready = (sem(n) for n in (
            "x_psum", "x_hi_ready", "x_lo_ready", "w_hi_ready", "w_lo_ready", "w_lo0_ready"))
        gu_done, silu_ready, h_ready, turn_a, turn_b, turned_a, turned_b, down_done, out_ready = (
            sem(n) for n in ("gu_done", "silu_ready", "h_ready", "turn_a", "turn_b", "turned_a", "turned_b",
                             "down_done", "out_ready"))
        y_var, y_std, y_norm, y_out = (sem(n) for n in ("y_var", "y_std", "y_norm", "y_out"))
        v_order, p_order = sem("v_order"), sem("p_order")

        ident = cst[:, C_ID:C_ID + 128]
        tri = cst[0:TT, C_TRI:C_TRI + TT]
        rev = cst[0:CAP, C_REV:C_REV + CAP]
        ones_row = cst[0:1, C_ONE:C_ONE + TT]

        def heads(ap, n=H):
            return ap.rearrange("p (h e) -> p h e", h=n)

        def spread_q(eng, j, g):
            eng.wait_ge(qkT_ready, j + 1)
            if j >= 2:
                eng.wait_ge(score_done, 4 * (j - 1))
            return eng.tensor_tensor(q_exp[:, j % 2, g, :].rearrange("p (h t) -> p h t", h=G6),
                                     qkT[:, j % 2, g * TT:(g + 1) * TT].rearrange("p (o t) -> p o t", o=1)
                                     .broadcast_to([DK, G6, TT]),
                                     cst[0:DK, C_HM:C_HM + G6].rearrange("p (h o) -> p h o", o=1)
                                     .broadcast_to([DK, G6, TT]), ALU.mult)

        def over_experts(eng, step):
            for e in range(RING - 1):
                step(e, e)
            with eng.Fori(0, E // RING - 1) as i:
                for k in range(RING - 1, 2 * RING - 1):
                    step(i * RING + k, k % RING)
            for e in range(E - 1, E + 1):
                step(e, e % RING)

        def known(e, least=None, most=None):
            return not isinstance(e, int) or ((least is None or e >= least) and (most is None or e <= most))

        block = ctx.enter_context(nc.Block())

        @block.sync
        def _(sp):
            sp.dma_start(wp_sb[:, :], w_patch).then_inc(wp_in, 16)
            for j in range(NT):
                sp.dma_start(x_sb[:, j, :], x[j]).then_inc(x_in[j], 16)
                if j == 0:
                    sp.dma_start(wproj_sb[:, :, :], w_proj).then_inc(proj_in, 16)
            sp.dma_start(wo_sb[:, :, :], w_o).then_inc(wo_in, 16)
            sp.dma_start(wgate_sb[:, :, :], w_gate).then_inc(rest_in, 16)
            sp.dma_start(wsgu_sb[:, :, :], ws_gu).then_inc(ws_in, 16)
            sp.dma_start(wsd_sb[:, :, :], ws_d).then_inc(ws_in, 16)
            for e in range(2):
                sp.dma_start(wgu_sb[:, e, :, :], w_gu[e]).then_inc(wgu_in[e], 16)
            for e in range(RING):
                sp.dma_start(wd_sb[:, e, :, :], w_d[e]).then_inc(wd_in[e], 16)
            for j in range(NT):
                sp.wait_ge(h1_ready, j + 1)
                sp.dma_start(h1_dram[j * TT:(j + 1) * TT, :], h1[:, j, :]).then_inc(h1_out, 16)
            sp.wait_ge(base_added, 1)
            sp.dma_start(y_dram.rearrange("(j p) d -> p j d", j=NT), y_base[:, 1, :, :]).then_inc(base_out, 16)

            def load_gu(e, k):
                sp.wait_ge(w_lo_ready, (e - 2) * NCH if known(e, 3) else 0)
                sp.dma_start(wgu_sb[:, k % 2, :, :], w_gu[e]).then_inc(wgu_in[k % 2], 16)

            def load_d(e, k):
                sp.wait_ge(down_done, e - RING + 1)
                sp.dma_start(wd_sb[:, k, :, :], w_d[e]).then_inc(wd_in[k], 16)

            sp.wait_ge(w_lo0_ready, 1)
            sp.dma_start(wgu_sb[:, 0, :, :], w_gu[2]).then_inc(wgu_in[0], 16)
            load_gu(3, 3)
            with sp.Fori(0, E // RING - 1) as i:
                for k in range(RING):
                    load_gu(i * RING + RING + k, k)
                    load_d(i * RING + RING + k, k)
            sp.wait_ge(y_add, 16 * E)
            sp.dma_start(y[:, :, :], y_dram.rearrange("(p t) d -> p t d", t=NY)).then_inc(y_in, 16)
            out_rows = out.rearrange("(p t) d -> p t d", t=NY)
            for part in (slice(0, 4), slice(4, NY)):
                sp.wait_ge(y_norm, part.stop)
                sp.dma_start(out_rows[:, part, :], y_n[:, part, :]).then_inc(y_out, 16)
            sp.wait_ge(y_out, 32)

        @block.tensor
        def _(pe):
            def embed(j):
                pe.wait_ge(x_in[j], 16)
                if j >= 2:
                    pe.wait_ge(h0_ready, j - 1)
                for c in range(KX):
                    last = pe.matmul(bank[j % 2][0:TT, 0:D], x_sb[:, j, c * TT:(c + 1) * TT],
                                     wp_sb[:, c * D:(c + 1) * D], start=(c == 0), stop=(c == KX - 1))
                last.then_inc(embed_done, 1)

            def turn_h0(j):
                pe.wait_ge(h0_ready, j + 1)
                if j >= 1:
                    pe.wait_ge(h0T_ready, j)
                for c in range(2):
                    last = pe.transpose(bank[2][0:DK, c * TT:(c + 1) * TT], h0[:, j, c * DK:(c + 1) * DK],
                                        ident[0:TT, 0:TT])
                last.then_inc(h0T_psum, 1)

            def project(j):
                pe.wait_ge(h0T_ready, j + 1)
                if j >= 2:
                    pe.wait_ge(qk_read, j - 1)
                    pe.wait_ge(vug_ready, j - 1)
                for b, c0, n, done in ((3, 0, QK, qk_psum), (4, QK, VU, vug_psum)):
                    b += 3 * (j % 2)
                    parts = [(x, w, c) for c in range(2)
                             for x, w in ((h0T_hi, wproj_hi), (h0T_hi, wproj_lo), (h0T_lo, wproj_hi))]
                    for m, (x, w, c) in enumerate(parts):
                        last = pe.matmul(bank[b][0:TT, 0:n], x[:, j % 2, c * TT:(c + 1) * TT], w[:, c, c0:c0 + n],
                                         start=(m == 0), stop=(m == len(parts) - 1))
                    last.then_inc(done, 1)

            def sum_u(j):
                pe.wait_ge(vug_ready, j + 1)
                if j >= 1:
                    pe.wait_ge(s_ready, j)
                pe.matmul(bank[5][0:TT, 0:D], tri, vug[:, j, D:2 * D], start=True, stop=False)
                pe.matmul(bank[5][0:TT, 0:D], ones_row, mu_row[:, :], start=False, stop=True).then_inc(usum_done, 1)

            pe.wait_ge(consts_in, 32)
            pe.wait_ge(wp_in, 16)
            embed(0)
            embed(1)
            for j in range(NT):
                turn_h0(j)
                if j + 2 < NT:
                    embed(j + 2)
                if j == 0:
                    pe.wait_ge(wproj_lo_ready, 1)
                project(j)
                if j == 0:
                    pe.wait_ge(tau_ready, 2)
                if j >= 1:
                    sum_u(j - 1)
            sum_u(NT - 1)

            def turn_qk(j):
                if j < 1:
                    pe.wait_ge(qk_read, NT)
                pe.wait_ge(qk_ready, j + 1)
                if j >= 1:
                    pe.wait_ge(qkT_ready, j)
                for c in range(4):
                    last = pe.transpose(bank[3][0:DK, c * TT:(c + 1) * TT], qk[:, j, c * DK:(c + 1) * DK],
                                        ident[0:TT, 0:TT])
                last.then_inc(qkT_psum, 1)

            def scores(j):
                pe.wait_ge(qkT_ready, j + 1)
                if j == 0:
                    pe.wait_ge(h0_ready, NT)
                for g in range(4):
                    pe.wait_ge(q_exp_ready if g < 2 else q_exp_pool, j + 1)
                    n = 4 * j + g
                    if n >= 2:
                        pe.wait_ge(p_ready, n - 1)
                    pe.matmul(bank[n % 2][0:TT, 0:3 * TT], qkT[:, j % 2, (2 + g // 2) * TT:(3 + g // 2) * TT],
                              q_exp[:, j % 2, g // 2, (g % 2) * 3 * TT:(g % 2 + 1) * 3 * TT],
                              start=True, stop=True).then_inc(score_done, 1)

            def attend(j):
                pe.wait_ge(p_ready, 4 * (j + 1))
                pe.wait_ge(v3_ready, j + 1)
                if j == 0:
                    pe.wait_ge(s_ready, NT)
                if j >= 1:
                    pe.wait_ge(mix_ready, 2 * j)
                for h in range(H):
                    at = (h % G6) * 3 * DH
                    last = pe.matmul(bank[4 + h // G6][0:TT, at:at + 6 * DH],
                                     pT[:, j % 2, h * TT:(h + 1) * TT], v3[:, j % 2, h * 3 * DH:(h + 2) * 3 * DH],
                                     start=True, stop=True)
                    if h % G6 == G6 - 1:
                        last.then_inc(att_psum, 1)

            def turn_o(j):
                pe.wait_ge(on_ready, j + 1)
                if j >= 1:
                    pe.wait_ge(oT_ready, j)
                for c in range(2):
                    last = pe.transpose(bank[6][0:DK, c * TT:(c + 1) * TT], o_n[:, j % SMALL, c * DK:(c + 1) * DK],
                                        ident[0:TT, 0:TT])
                last.then_inc(oT_psum, 1)

            def project_o(j):
                pe.wait_ge(oT_ready, j + 1)
                if j >= 1:
                    pe.wait_ge(r1_ready, j)
                for c in range(2):
                    last = pe.matmul(bank[7][0:TT, 0:D], oT[:, j % 2, c * TT:(c + 1) * TT], wo_sb[:, c, :],
                                     start=(c == 0), stop=(c == 1))
                last.then_inc(wo_done, 1)

            def turn_h1(j):
                pe.wait_ge(h1_ready, j + 1)
                if j >= 1:
                    pe.wait_ge(h1T_ready, j)
                for c in range(2):
                    last = pe.transpose(bank[2][0:DK, c * TT:(c + 1) * TT], h1[:, j, c * DK:(c + 1) * DK],
                                        ident[0:TT, 0:TT])
                last.then_inc(h1T_psum, 1)

            def shared(m):
                n, f = divmod(m, FSK)
                if m >= 2:
                    pe.wait_ge(hs_ready, m - 1)
                for b, f0 in ((0, f * 128), (3, FS + f * 128)):
                    for c in range(2):
                        last = pe.matmul(bank[b + m % 2][:, 0:HALF], wsgu_sb[:, c, f0:f0 + 128],
                                         h1T[:, c, n * HALF:(n + 1) * HALF], start=(c == 0), stop=(c == 1))
                last.then_inc(shared_gu, 1)

            turn_qk(0)
            pe.wait_ge(s_all, 1)
            pe.transpose(bank[5][0:NT * H, 0:TT], es_s[:, 1, :], ident[0:TT, 0:TT]).then_inc(sT_psum, 1)
            scores(0)
            turn_qk(1)
            pe.wait_ge(sT_exp, 1)
            pe.transpose(bank[7][0:TT, 0:NT * H], sT[:, 2, :], ident[0:NT * H, 0:NT * H]).then_inc(es_psum, 1)
            scores(1)
            turn_qk(2)
            pe.wait_ge(es_ready, 1)
            pe.matmul(bank[6][0:TT, 0:2 * NT * H], tri, es_s[:, :, :].rearrange("p a b -> p (a b)"),
                      start=True, stop=True).then_inc(cum_done, 1)
            pe.wait_ge(wo_in, 16)
            for i in range(1, NT + 7):
                if 2 <= i < NT:
                    scores(i)
                if 0 <= i - 1 < NT:
                    attend(i - 1)
                if 3 <= i + 2 < NT:
                    turn_qk(i + 2)
                if 0 <= i - 3 < NT:
                    if i == 3:
                        pe.wait_ge(coef_ready, 1)
                    turn_o(i - 3)
                if 0 <= i - 4 < NT:
                    project_o(i - 4)
                if 0 <= i - 6 < NT:
                    turn_h1(i - 6)
            pe.wait_ge(rest_in, 16)
            pe.wait_ge(h1T_ready, NT)
            for n in range(2):
                for c in range(2):
                    last = pe.matmul(bank[5][32 * n:32 * n + 32, 0:HALF], wgate_sb[:, c, :],
                                     h1T[:, c, n * HALF:(n + 1) * HALF], start=(c == 0), stop=(c == 1))
            last.then_inc(logit_psum, 1)
            pe.wait_ge(ws_in, 32)
            for m in range(2 * FSK):
                shared(m)
            pe.wait_ge(hs_ready, 2 * FSK)
            for j in range(NT):
                if j >= 2:
                    pe.wait_ge(base_ready, j - 1)
                for f in range(FSK):
                    last = pe.matmul(bank[6 + j % 2][0:TT, 0:D], hsT[:, f, j * TT:(j + 1) * TT], wsd_sb[:, f, :],
                                     start=(f == 0), stop=(f == FSK - 1))
                last.then_inc(shared_y, 1)
            pe.wait_ge(top_ready, 1)
            pe.transpose(bank[5][0:CAP, 0:48], top_val[:, 0:CAP], ident[0:48, 0:48])
            pe.transpose(bank[5][0:CAP, 48:96], top_row[:, :], ident[0:48, 0:48]).then_inc(top_psum, 1)
            pe.wait_ge(topT_ready, 1)
            pe.matmul(bank[2][0:CAP, 0:2 * E], rev, top_T[:, :, 32:48], start=True, stop=True).then_inc(rev_psum, 1)

            def turn_x(e, k):
                pe.wait_ge(xg_in[k], (e - k) * (16 // RING) + 16)
                if known(e, 1):
                    pe.wait_ge(x_lo_ready, e)
                for c in range(2):
                    last = pe.transpose(bank[6][0:DK, c * CAP:(c + 1) * CAP], xg[:, k, c * DK:(c + 1) * DK],
                                        ident[0:CAP, 0:CAP])
                last.then_inc(x_psum, 1)

            def gate_up(e, k, c):
                if known(e, 1):
                    pe.wait_ge(h_ready, e * NCH - NCH + c + 1)
                    pe.wait_ge(w_lo_ready, e * NCH - NCH + c + 1)
                parts = [(x, w, n) for n in range(2) for x, w in ((x_hi, w_hi), (x_hi, w_lo), (x_lo, w_hi))]
                for m, (x, w, n) in enumerate(parts):
                    last = pe.matmul(bank[c][0:CAP, 0:2 * CH], x[:, k % 2, n * CAP:(n + 1) * CAP],
                                     w[:, k % 2, n, c * 2 * CH:(c + 1) * 2 * CH],
                                     start=(m == 0), stop=(m == len(parts) - 1))
                last.then_inc(gu_done, 1)

            def turn_hidden(e, k, tiles, b, done):
                for n, c in enumerate(tiles):
                    last = pe.transpose(bank[b][:, n * CAP:(n + 1) * CAP], hid[:, k % 2, c * 128:(c + 1) * 128],
                                        ident[0:CAP, 0:CAP])
                last.then_inc(done, 1)

            def step(e, k):
                last_k = (k - 1) % RING
                if known(e, None, E - 1):
                    pe.wait_ge(x_lo_ready, e + 1)
                    gate_up(e, k, 0)
                if known(e, None, E - 2):
                    turn_x(e + 1, (k + 1) % RING)
                if known(e, 1):
                    pe.wait_ge(h_ready, e * NCH)
                    turn_hidden(e - 1, last_k, range(4, FK), 4, turn_b)
                if known(e, None, E - 1):
                    gate_up(e, k, 1)
                if known(e, 1):
                    pe.wait_ge(wd_in[last_k], (e - 1 - last_k) * (16 // RING) + 16)
                    pe.wait_ge(turned_a, e)
                    pe.wait_ge(turned_b, e)
                    if known(e, 2):
                        pe.wait_ge(out_ready, e - 1)
                    for c in range(FK):
                        last = pe.matmul(bank[5][0:CAP, 0:D], hidT[:, c, :], wd_sb[:, last_k, c, :],
                                         start=(c == 0), stop=(c == FK - 1))
                    last.then_inc(down_done, 1)
                if known(e, None, E - 1):
                    gate_up(e, k, 2)
                    pe.wait_ge(h_ready, e * NCH + 2)
                    turn_hidden(e, k, range(4), 3, turn_a)

            pe.wait_ge(base_ready, NT)
            turn_x(0, 0)
            pe.wait_ge(w_lo0_ready, 1)
            pe.wait_ge(row_ready, 1)
            over_experts(pe, step)

        @block.scalar
        def _(act):
            act.dma_start(cst[:, :], consts).then_inc(consts_in, 16)
            act.dma_start(par[:, :], params).then_inc(consts_in, 16)
            def copy_qkT(j):
                act.wait_ge(qkT_psum, j + 1)
                if j >= 2:
                    act.wait_ge(score_done, 4 * (j - 1))
                act.copy(qkT[:, j % 2, :], bank[3][0:DK, 0:4 * TT]).then_inc(qkT_ready, 1)

            act.wait_ge(tau_clip, 1)
            act.activation(tau[:, 1, :], tau[:, 0, :], ACT.Exp).then_inc(tau_exp, 1)

            def upper_h0T(j):
                act.wait_ge(h0T_psum, j + 1)
                if j >= 2:
                    act.wait_ge(vug_psum, j - 1)
                act.copy(h0T_hi[:, j % 2, :], bank[2][0:DK, 0:2 * TT]).then_inc(h0T_hi_ready, 1)

            def projected(j):
                act.wait_ge(vug_psum, j + 1)
                act.copy(vug[:, j, :], bank[4 + 3 * (j % 2)][0:TT, 0:VU]).then_inc(vug_ready, 1)
                act.wait_ge(qk_ready, j + 1)
                if j >= 2:
                    act.wait_ge(n2_ready, j - 1)
                act.activation(squares[:, j % 2, :], qk[:, j, :], ACT.Square).then_inc(sq_ready, 1)

            act.wait_ge(wv_ready, 2)
            act.copy(wproj_hi[:, :, :], wproj_sb[:, :, :]).then_inc(wproj_hi_ready, 1)
            for j in range(NT):
                upper_h0T(j)
                if j >= 1:
                    projected(j - 1)
            projected(NT - 1)
            act.wait_ge(qk_ready, NT)
            act.wait_ge(n2_ready, NT)
            act.wait_ge(s_ready, NT)
            copy_qkT(0)
            act.wait_ge(vug_ready, NT)
            act.activation(gates[:, 0, :, :], vug[:, :, 2 * D:VU], ACT.Exp, scale=-1.0).then_inc(gate_exp, 1)
            act.wait_ge(sT_sub, 1)
            act.activation(sT[:, 2, :], sT[:, 1, :], ACT.Exp).then_inc(sT_exp, 1)
            copy_qkT(1)
            act.wait_ge(n2_ready, NT)
            act.activation(rnorm[:, :, :], norm2[:, :, :], ACT.Sqrt).then_inc(norm_sqrt, 1)

            def square_o(j):
                act.wait_ge(att_ready, j + 1)
                if j >= 2:
                    act.wait_ge(ovar_ready, j - 1)
                act.activation(o_sq[:, j % 2, :], o_att[:, j % SMALL, :], ACT.Square).then_inc(osq_ready, 1)

            def root_o(j):
                act.wait_ge(ovar_ready, j + 1)
                act.activation(o_var[:, j % SMALL, H:2 * H], o_var[:, j % SMALL, 0:H], ACT.Sqrt).then_inc(ostd_ready, 1)

            def copy_oT(j):
                act.wait_ge(oT_psum, j + 1)
                if j >= 2:
                    act.wait_ge(wo_done, j - 1)
                act.copy(oT[:, j % 2, :], bank[6][0:DK, 0:2 * TT]).then_inc(oT_ready, 1)

            def root_r(j):
                act.wait_ge(r1_var, j + 1)
                act.activation(mv1[:, j % SMALL, 2:3], mv1[:, j % SMALL, 1:2], ACT.Sqrt).then_inc(r1_std, 1)

            def copy_h1T(j):
                act.wait_ge(h1T_psum, j + 1)
                act.copy(h1T[:, :, j * TT:(j + 1) * TT],
                         bank[2][0:DK, 0:2 * TT].rearrange("p (c t) -> p c t", c=2)).then_inc(h1T_ready, 1)

            def silu_shared(m):
                act.wait_ge(shared_gu, m + 1)
                if m >= 2:
                    act.wait_ge(hs_ready, m - 1)
                act.activation(silu_s[:, m % 2, :], bank[m % 2][:, 0:HALF], ACT.Silu).then_inc(silu_s_ready, 1)

            copy_qkT(2)
            for i in range(1, NT + 7):
                if 3 <= i + 2 < NT:
                    copy_qkT(i + 2)
                if 0 <= i - 1 < NT:
                    square_o(i - 1)
                if 0 <= i - 2 < NT:
                    root_o(i - 2)
                if 0 <= i - 5 < NT:
                    root_r(i - 5)
                if 0 <= i - 3 < NT:
                    copy_oT(i - 3)
                if 0 <= i - 6 < NT:
                    copy_h1T(i - 6)
            act.wait_ge(logit_psum, 1)
            act.copy(rank_in[:, :], bank[5][0:64, 0:HALF]).then_inc(logit_ready, 1)

            def split_hi(e, k, c):
                if known(e, 2):
                    act.wait_ge(gu_done, (e - 2) * NCH + c + 1)
                cols = slice(c * 2 * CH, (c + 1) * 2 * CH)
                act.copy(w_hi[:, k % 2, :, cols], wgu_sb[:, k % 2, :, cols]).then_inc(w_hi_ready, 1)

            act.wait_ge(wgu_in[0], 16)
            for m in range(2 * FSK):
                silu_shared(m)
                if m < NCH:
                    split_hi(0, 0, m)
            for j in range(NT):
                act.wait_ge(shared_y, j + 1)
                act.copy(y_base[:, 0, j, :], bank[6 + j % 2][0:TT, 0:D]).then_inc(base_ready, 1)
            act.wait_ge(top_psum, 1)
            act.copy(top_T[:, :, :].rearrange("p a b -> p (a b)"), bank[5][0:CAP, 0:96]).then_inc(topT_ready, 1)
            act.wait_ge(pick_ready, 1)
            act.activation(score[:, :], pick[:, 0, :], ACT.Sigmoid).then_inc(score_ready, 1)

            def x_upper(e, k):
                act.wait_ge(x_psum, e + 1)
                if known(e, 2):
                    act.wait_ge(gu_done, (e - 1) * NCH)
                act.copy(x_hi[:, k % 2, :], bank[6][0:DK, 0:2 * CAP]).then_inc(x_hi_ready, 1)

            def silu_gate(e, k, c):
                act.wait_ge(gu_done, e * NCH + c + 1)
                if known(e, 1):
                    act.wait_ge(h_ready, e * NCH - NCH + c + 1)
                act.activation(silu_g[:, c, :], bank[c][0:CAP, 0:CH], ACT.Silu).then_inc(silu_ready, 1)

            def step(e, k):
                nxt = (k + 1) % RING
                if known(e, None, E - 1):
                    silu_gate(e, k, 0)
                if known(e, None, E - 2):
                    x_upper(e + 1, nxt)
                    act.wait_ge(wgu_in[nxt % 2], (e + 1 - nxt % 2) * 8 + 16)
                if known(e, 1):
                    act.wait_ge(turn_b, e)
                    act.copy(hidT[:, 4:FK, :].rearrange("p a b -> p (a b)"), bank[4][:, 0:2 * CAP]).then_inc(turned_b, 1)
                if known(e, None, E - 2):
                    split_hi(e + 1, nxt, 0)
                if known(e, None, E - 1):
                    silu_gate(e, k, 1)
                if known(e, None, E - 2):
                    split_hi(e + 1, nxt, 1)
                if known(e, None, E - 1):
                    silu_gate(e, k, 2)
                    act.wait_ge(turn_a, e + 1)
                    if known(e, 1):
                        act.wait_ge(down_done, e)
                    act.copy(hidT[:, 0:4, :].rearrange("p a b -> p (a b)"), bank[3][:, 0:4 * CAP]).then_inc(turned_a, 1)
                if known(e, None, E - 2):
                    split_hi(e + 1, nxt, 2)

            x_upper(0, 0)
            over_experts(act, step)
            act.wait_ge(y_var, 1)
            act.activation(std2[:, 1, :], std2[:, 0, :], ACT.Sqrt).then_inc(y_std, 1)

        @block.gpsimd
        def _(pool):
            pool.wait_ge(wproj_hi_ready, 1)
            pool.tensor_tensor(wproj_lo[:, :, :], wproj_sb[:, :, :], wproj_hi[:, :, :].bitcast(F32), ALU.subtract)\
                .then_inc(wproj_lo_ready, 1)
            for j in range(NT):
                pool.wait_ge(qk_read, j + 1)
                pool.tensor_tensor(qk[:, j, :], rope_a[:, j % 2, :], rope_b[:, j % 2, :], ALU.add)\
                    .then_inc(qk_ready, 1)

            def spread_v(j):
                if j >= 2:
                    pool.wait_ge(att_psum, 2 * (j - 1))
                v = heads(vug[:, j, 0:D])
                for c in range(3):
                    last = pool.tensor_tensor(
                        v3[:, j % 2, 0:H * 3 * DH].rearrange("p (h c e) -> p h c e", h=H, c=3)[:, :, c, :], v,
                        vcoef[:, j * H:(j + 1) * H, c:c + 1].broadcast_to([TT, H, DH]), ALU.mult)
                last.then_inc(v3_ready, 1)

            def sum_mix(j):
                pool.wait_ge(mix_ready, 2 * (j + 1))
                m = mix[:, j % 2, :].rearrange("p (h c e) -> p h c e", h=H, c=3)
                pool.tensor_tensor(heads(o_sum[:, j % 2, :]), m[:, :, 0, :], m[:, :, 1, :], ALU.add)\
                    .then_inc(p_order, 1)
                pool.wait_ge(p_order, j + 1)
                if j >= SMALL:
                    pool.wait_ge(on_ready, j - SMALL + 1)
                pool.tensor_tensor(heads(o_att[:, j % SMALL, :]), heads(o_sum[:, j % 2, :]), m[:, :, 2, :], ALU.add)\
                    .then_inc(att_ready, 1)

            def expand_q(j):
                spread_q(pool, j, 1).then_inc(q_exp_pool, 1)

            expand_q(0)
            pool.memset(v3[:, :, H * 3 * DH:], 0.0).then_inc(v3_zero, 1)
            expand_q(1)
            pool.wait_ge(vcoef_ready, 1)
            spread_v(0)
            spread_v(1)
            for j in range(NT):
                if j + 2 < NT:
                    expand_q(j + 2)
                sum_mix(j)
                if j + 2 < NT:
                    spread_v(j + 2)

            pool.wait_ge(w_hi_ready, NCH)
            pool.tensor_tensor(w_lo[:, 0, :, :], wgu_sb[:, 0, :, :], w_hi[:, 0, :, :].bitcast(F32), ALU.subtract)\
                .then_inc(w_lo0_ready, 1)
            pool.wait_ge(h1_out, 16 * NT)
            pool.wait_ge(row_ready, 1)

            def gather(e):
                k = e % RING
                pool.indirect_dma_start(xg[:, k, :], None, h1_dram,
                                        bass.IndirectOffsetOnAxis(ap=row_i[:, e:e + 1], axis=0)).then_inc(xg_in[k], 16)

            for e in range(RING):
                gather(e)
            pool.wait_ge(base_ready, NT)
            pool.tensor_tensor(y_base[:, 1, :, :], y_base[:, 0, :, :], h1[:, :, :], ALU.add).then_inc(base_added, 1)
            pool.wait_ge(base_out, 16)
            for e in range(E):
                if e + RING < E:
                    pool.wait_ge(x_psum, e + 1)
                    gather(e + RING)
                pool.wait_ge(out_ready, e + 1)
                if e >= 1:
                    pool.wait_ge(y_add, 16 * e)
                pool.indirect_dma_start(y_dram, bass.IndirectOffsetOnAxis(ap=row_i[:, e:e + 1], axis=0),
                                        o_exp[:, e % 2, :], None, compute_op=ALU.add).then_inc(y_add, 16)

        @block.vector
        def _(dve):
            order = [0]

            def link(ins):
                order[0] += 1
                ins.then_inc(v_order, 1)
                dve.wait_ge(v_order, order[0])

            dve.wait_ge(consts_in, 32)
            dve.tensor_scalar(tau[:, 0, :], par[:, P_TAU:P_TAU + H], -50.0, 30.0, ALU.max, ALU.min)\
                .then_inc(tau_clip, 1)
            dve.wait_ge(tau_exp, 1)
            link(dve.tensor_tensor(heads(mu_row[:, :]), heads(par[0:1, P_MU:P_MU + D]),
                                   tau[0:1, 1, :].rearrange("p (h o) -> p h o", o=1).broadcast_to([1, H, DH]), ALU.mult))
            link(dve.tensor_scalar(tau[:, 0, :], tau[:, 1, :], cst[0:TT, C_T:C_T + 1], -float(DH) ** 0.5, ALU.add, ALU.mult))
            dve.reciprocal(tau[:, 2, :], tau[:, 0, :]).then_inc(tau_ready, 1)
            dve.wait_ge(proj_in, 16)
            for c in range(2):
                wv = heads(wproj_sb[:, c, QK:QK + D])
                link(dve.tensor_reduce(wv_mean[:, c, :], wv, AX_X, ALU.add))
                link(dve.tensor_scalar(wv_mean[:, c, :], wv_mean[:, c, :], 1.0 / DH, None, ALU.mult))
                dve.tensor_tensor(wv, wv, wv_mean[:, c, :].rearrange("p (h o) -> p h o", o=1)
                                  .broadcast_to([DK, H, DH]), ALU.subtract).then_inc(wv_ready, 1)
            dve.tensor_copy(tau[:, 1, :], tau[:, 1, :]).then_inc(tau_ready, 1)

            def add_bias(j):
                dve.wait_ge(embed_done, j + 1)
                dve.tensor_tensor(h0[:, j, :], bank[j % 2][0:TT, 0:D], par[:, P_B:P_B + D], ALU.add)\
                    .then_inc(h0_ready, 1)

            def lower_h0T(j):
                dve.wait_ge(h0T_hi_ready, j + 1)
                dve.tensor_tensor(h0T_lo[:, j % 2, :], bank[2][0:DK, 0:2 * TT], h0T_hi[:, j % 2, :].bitcast(F32),
                                  ALU.subtract).then_inc(h0T_ready, 1)

            def rope(j):
                dve.wait_ge(qk_psum, j + 1)
                if j >= 2:
                    dve.wait_ge(qk_ready, j - 1)
                src = bank[3 + 3 * (j % 2)][0:TT, 0:QK].rearrange("p (h e) -> p h e", e=DH)
                cos = cst[0:TT, C_COS:C_COS + DH].rearrange("p (o e) -> p o e", o=1)
                sin = cst[0:TT, C_SIN:C_SIN + DH].rearrange("p (o e) -> p o e", o=1)
                a = rope_a[:, j % 2, :].rearrange("p (h e) -> p h e", e=DH)
                b = rope_b[:, j % 2, :].rearrange("p (h e) -> p h e", e=DH)
                hd = DH // 2
                dve.tensor_tensor(a, src, cos.broadcast_to([TT, 2 * H, DH]), ALU.mult)
                dve.tensor_tensor(b[:, :, 0:hd], src[:, :, hd:DH],
                                  sin[:, :, 0:hd].broadcast_to([TT, 2 * H, hd]), ALU.mult)
                dve.tensor_tensor(b[:, :, hd:DH], src[:, :, 0:hd],
                                  sin[:, :, hd:DH].broadcast_to([TT, 2 * H, hd]), ALU.mult).then_inc(qk_read, 1)

            def sum_squares(j):
                dve.wait_ge(sq_ready, j + 1)
                dve.tensor_reduce(norm2[:, j, :], squares[:, j % 2, :].rearrange("p (h e) -> p h e", e=DH),
                                  AX_X, ALU.add).then_inc(n2_ready, 1)

            def dot_u(j):
                dve.wait_ge(usum_done, j + 1)
                link(dve.tensor_tensor(u_bar[:, j % 2, :], bank[5][0:TT, 0:D], vug[:, j, D:2 * D], ALU.mult))
                dve.tensor_reduce(s_raw[:, j, :], heads(u_bar[:, j % 2, :]), AX_X, ALU.add).then_inc(s_ready, 1)

            add_bias(0)
            add_bias(1)
            lower_h0T(0)
            for j in range(NT):
                if j + 2 < NT:
                    add_bias(j + 2)
                if j + 1 < NT:
                    lower_h0T(j + 1)
                rope(j)
                if j >= 1:
                    sum_squares(j - 1)
                    dot_u(j - 1)
            sum_squares(NT - 1)
            dot_u(NT - 1)
            dve.wait_ge(s_ready, NT)
            dve.tensor_tensor(es_s[:, 1, :].rearrange("p (j h) -> p j h", j=NT), s_raw[:, :, :],
                              tau[:, 2, :].rearrange("p (o h) -> p o h", o=1).broadcast_to([TT, NT, H]), ALU.mult)\
                .then_inc(s_all, 1)
            def expand_q(j):
                spread_q(dve, j, 0).then_inc(q_exp_ready, 1)

            def mask(j):
                if j >= 2:
                    dve.wait_ge(att_psum, 2 * (j - 1))
                for g in range(4):
                    n = 4 * j + g
                    dve.wait_ge(score_done, n + 1)
                    dve.tensor_tensor(pT[:, j % 2, g * 3 * TT:(g + 1) * 3 * TT].rearrange("p (h t) -> p h t", h=3),
                                      bank[n % 2][0:TT, 0:3 * TT].rearrange("p (h t) -> p h t", h=3),
                                      tri.rearrange("p (o t) -> p o t", o=1).broadcast_to([TT, 3, TT]),
                                      ALU.mult).then_inc(p_ready, 1)

            expand_q(0)
            dve.wait_ge(gate_exp, 1)
            link(dve.tensor_scalar(gates[:, 1, :, :], gates[:, 0, :, :], 1.0, None, ALU.add))
            link(dve.reciprocal(gates[:, 2, :, :], gates[:, 1, :, :]))
            dve.wait_ge(sT_psum, 1)
            sT_ps = bank[5][0:NT * H, 0:TT].rearrange("p (i l) -> p i l", i=2)
            link(dve.tensor_reduce(s_max[:, :], sT_ps, AX_X, ALU.max))
            dve.tensor_tensor(sT[:, 1, :].rearrange("p (i l) -> p i l", i=2), sT_ps,
                              s_max[:, :].rearrange("p (i o) -> p i o", o=1).broadcast_to([NT * H, 2, L]),
                              ALU.subtract).then_inc(sT_sub, 1)
            mask(0)
            expand_q(1)
            dve.wait_ge(norm_sqrt, 1)
            link(dve.tensor_scalar(norm2[:, :, :], rnorm[:, :, :], 1e-12, None, ALU.max))
            link(dve.reciprocal(rnorm[:, :, :], norm2[:, :, :]))
            rq, rk = rnorm[:, :, 0:H], rnorm[:, :, H:2 * H]
            dve.wait_ge(es_psum, 1)
            dve.tensor_copy(es_s[:, 0, :], bank[7][0:TT, 0:NT * H]).then_inc(es_ready, 1)
            dve.wait_ge(es_ready, 1)

            def by_tile(ap):
                return ap.rearrange("p (j h) -> p j h", j=NT)

            dve.tensor_tensor(by_tile(vcoef[:, :, 0]), by_tile(es_s[:, 0, :]), rk, ALU.mult)
            dve.tensor_tensor(by_tile(vcoef[:, :, 1]), by_tile(es_s[:, 1, :]), rk, ALU.mult)
            dve.tensor_copy(by_tile(vcoef[:, :, 2]), rk).then_inc(vcoef_ready, 1)
            mask(1)
            expand_q(2)
            sig1, sigh = gates[:, 2, :, 0:H], gates[:, 2, :, H:2 * H]
            rt = cst[0:TT, C_RT:C_RT + 1]
            a, b, c, d = (small[:, n, :] for n in range(4))
            dve.wait_ge(cum_done, 1)
            link(dve.tensor_scalar(a, bank[6][0:TT, 0:NT * H], 1e-12, None, ALU.add))
            link(dve.reciprocal(b, a))
            dve.tensor_tensor(by_tile(c), sig1, sigh, ALU.subtract)
            link(dve.tensor_tensor(by_tile(a), by_tile(b), sigh, ALU.mult))
            dve.tensor_tensor(by_tile(coef[:, :, 0]), by_tile(a), rq, ALU.mult)
            link(dve.tensor_scalar(d, c, rt, None, ALU.mult))
            link(dve.tensor_tensor(b, d, bank[6][0:TT, NT * H:2 * NT * H], ALU.mult))
            dve.tensor_tensor(by_tile(coef[:, :, 1]), by_tile(d), rq, ALU.mult)
            link(dve.tensor_tensor(by_tile(a), by_tile(b), sigh, ALU.add))
            link(dve.tensor_scalar(b, a, rt, -1.0, ALU.mult, ALU.mult))
            dve.tensor_tensor(by_tile(coef[:, :, 2]), by_tile(b), rq, ALU.mult).then_inc(coef_ready, 1)
            dve.wait_ge(coef_ready, 1)

            def combine(j):
                if j >= 2:
                    dve.wait_ge(att_ready, j - 1)
                for g in range(2):
                    dve.wait_ge(att_psum, 2 * j + g + 1)
                    n = G6 * 3
                    dve.tensor_tensor(mix[:, j % 2, g * n * DH:(g + 1) * n * DH].rearrange("p (h e) -> p h e", e=DH),
                                      bank[4 + g][0:TT, 0:n * DH].rearrange("p (h e) -> p h e", e=DH),
                                      coef[:, j * H + g * G6:j * H + (g + 1) * G6, :].rearrange("p h (c o) -> p (h c) o", o=1)
                                      .broadcast_to([TT, n, DH]), ALU.mult).then_inc(mix_ready, 1)

            def variance_o(j):
                dve.wait_ge(osq_ready, j + 1)
                link(dve.tensor_reduce(o_var[:, j % SMALL, 2 * H:3 * H], heads(o_sq[:, j % 2, :]), AX_X, ALU.add))
                dve.tensor_scalar(o_var[:, j % SMALL, 0:H], o_var[:, j % SMALL, 2 * H:3 * H], 1.0 / DH, EPS, ALU.mult, ALU.add)\
                    .then_inc(ovar_ready, 1)

            def normalise_o(j):
                dve.wait_ge(ostd_ready, j + 1)
                link(dve.reciprocal(o_var[:, j % SMALL, 2 * H:3 * H], o_var[:, j % SMALL, H:2 * H]))
                if j >= SMALL:
                    dve.wait_ge(oT_psum, j - SMALL + 1)
                dve.tensor_tensor(heads(o_n[:, j % SMALL, :]), heads(o_att[:, j % SMALL, :]),
                                  o_var[:, j % SMALL, 2 * H:3 * H].rearrange("p (h o) -> p h o", o=1)
                                  .broadcast_to([TT, H, DH]), ALU.mult).then_inc(on_ready, 1)

            def residual(j):
                dve.wait_ge(wo_done, j + 1)
                dve.tensor_tensor(r1[:, j % SMALL, :], bank[7][0:TT, 0:D], h0[:, j, :], ALU.add).then_inc(r1_ready, 1)
                dve.wait_ge(r1_ready, j + 1)
                link(dve.bn_stats(bn1[:, j % SMALL, :], r1[:, j % SMALL, :]))
                link(dve.bn_aggr(mv1[:, j % SMALL, 0:2], bn1[:, j % SMALL, :]))
                dve.tensor_scalar(mv1[:, j % SMALL, 1:2], mv1[:, j % SMALL, 1:2], EPS, None, ALU.add).then_inc(r1_var, 1)

            def normalise_r(j):
                dve.wait_ge(r1_std, j + 1)
                link(dve.reciprocal(mv1[:, j % SMALL, 3:4], mv1[:, j % SMALL, 2:3]))
                dve.tensor_scalar(h1[:, j, :], r1[:, j % SMALL, :], mv1[:, j % SMALL, 0:1], mv1[:, j % SMALL, 3:4],
                                  ALU.subtract, ALU.mult).then_inc(h1_ready, 1)

            def hidden_s(m):
                n, f = divmod(m, FSK)
                dve.wait_ge(silu_s_ready, m + 1)
                dve.tensor_tensor(hsT[:, f, n * HALF:(n + 1) * HALF], silu_s[:, m % 2, :], bank[3 + m % 2][:, 0:HALF],
                                  ALU.mult).then_inc(hs_ready, 1)

            for i in range(1, NT + 7):
                if 0 <= i - 3 < NT:
                    normalise_o(i - 3)
                if 0 <= i - 6 < NT:
                    normalise_r(i - 6)
                if 2 <= i < NT:
                    mask(i)
                if 3 <= i + 1 < NT:
                    expand_q(i + 1)
                if 0 <= i - 1 < NT:
                    combine(i - 1)
                if 0 <= i - 2 < NT:
                    variance_o(i - 2)
                if 0 <= i - 5 < NT:
                    residual(i - 5)
            dve.wait_ge(logit_ready, 1)
            for n in range(ROUNDS):
                eight = slice(8 * n, 8 * n + 8)
                link(dve.max(top_val[:, eight], rank_in[0:48, :]))
                link(dve.max_index(top_idx[:, eight], top_val[:, eight], rank_in[0:48, :]))
                if n < ROUNDS - 1:
                    link(dve.match_replace(rank_in[0:48, :], top_val[:, eight], rank_in[0:48, :], -3e38))
                if 1 <= n <= 2 * FSK:
                    hidden_s(n - 1)
            link(dve.tensor_copy(top_row[:, :], top_idx[:, 0:CAP]))
            dve.tensor_scalar(top_row[32:48, :], top_row[32:48, :], float(HALF), None, ALU.add).then_inc(top_ready, 1)
            dve.wait_ge(rev_psum, 1)
            va, ia = top_T[:, 0, 0:E], top_T[:, 1, 0:E]
            vb, ib = bank[2][0:CAP, 0:E], bank[2][0:CAP, E:2 * E]
            dve.tensor_tensor(pick[:, 0, :], va, vb, ALU.max).then_inc(pick_ready, 1)
            dve.tensor_tensor(pick[:, 1, :], va, vb, ALU.is_ge)
            link(dve.tensor_tensor(pick[:, 2, :], ia, ib, ALU.subtract))
            link(dve.tensor_tensor(pick[:, 3, :], pick[:, 2, :], pick[:, 1, :], ALU.mult))
            link(dve.tensor_tensor(pick[:, 4, :], pick[:, 3, :], ib, ALU.add))
            dve.tensor_copy(row_i[:, :], pick[:, 4, :]).then_inc(row_ready, 1)
            dve.wait_ge(score_ready, 1)

            def x_lower(e, k):
                dve.wait_ge(x_hi_ready, e + 1)
                dve.tensor_tensor(x_lo[:, k % 2, :], bank[6][0:DK, 0:2 * CAP], x_hi[:, k % 2, :].bitcast(F32),
                                  ALU.subtract).then_inc(x_lo_ready, 1)

            def split_lo(e, k, c):
                dve.wait_ge(w_hi_ready, e * NCH + c + 1)
                cols = slice(c * 2 * CH, (c + 1) * 2 * CH)
                dve.tensor_tensor(w_lo[:, k % 2, :, cols], wgu_sb[:, k % 2, :, cols],
                                  w_hi[:, k % 2, :, cols].bitcast(F32), ALU.subtract).then_inc(w_lo_ready, 1)

            def gated(e, k, c):
                dve.wait_ge(silu_ready, e * NCH + c + 1)
                if c == 0 and known(e, 2):
                    dve.wait_ge(turn_b, e - 1)
                dve.tensor_tensor(hid[:, k % 2, c * CH:(c + 1) * CH], silu_g[:, c, :], bank[c][0:CAP, CH:2 * CH],
                                  ALU.mult).then_inc(h_ready, 1)

            def step(e, k):
                nxt = (k + 1) % RING
                if known(e, None, E - 1):
                    gated(e, k, 0)
                if known(e, None, E - 2):
                    x_lower(e + 1, nxt)
                    split_lo(e + 1, nxt, 0)
                if known(e, None, E - 1):
                    gated(e, k, 1)
                if known(e, None, E - 2):
                    split_lo(e + 1, nxt, 1)
                if known(e, 1):
                    dve.wait_ge(down_done, e)
                    if known(e, 3):
                        dve.wait_ge(y_add, 16 * (e - 2))
                    dve.tensor_scalar(o_exp[:, (k - 1) % 2, :], bank[5][0:CAP, 0:D], score[:, bass.ds(e - 1, 1)], None,
                                      ALU.mult).then_inc(out_ready, 1)
                if known(e, None, E - 1):
                    gated(e, k, 2)
                if known(e, None, E - 2):
                    split_lo(e + 1, nxt, 2)

            x_lower(0, 0)
            over_experts(dve, step)
            dve.wait_ge(y_in, 16)
            for t in range(NY):
                last = dve.bn_stats(bn2[:, t, :], y[:, t, :])
            link(last)
            for t in range(NY):
                last = dve.bn_aggr(mv2[:, t, :], bn2[:, t, :])
            link(last)
            dve.tensor_scalar(std2[:, 0, :], mv2[:, :, 1], EPS, None, ALU.add).then_inc(y_var, 1)
            dve.wait_ge(y_std, 1)
            link(dve.reciprocal(std2[:, 2, :], std2[:, 1, :]))
            for t in range(NY):
                dve.tensor_scalar(y_n[:, t, :], y[:, t, :], mv2[:, t, 0:1], std2[:, 2, t:t + 1],
                                  ALU.subtract, ALU.mult).then_inc(y_norm, 1)


def constants():
    import numpy as np
    c = np.zeros((128, C_N), np.float32)
    c[:, C_ID:C_ID + 128] = np.eye(128)
    m, l = np.arange(TT)[:, None], np.arange(TT)[None, :]
    c[:TT, C_TRI:C_TRI + TT] = (m // L == l // L) & (m <= l)
    c[:CAP, C_REV:C_REV + CAP] = np.eye(CAP)[::-1]
    pos = (np.arange(TT) % L).astype(np.float32)
    inv = (1.0 / 10000.0 ** (np.arange(0, DH, 2, dtype=np.float32) / DH)).astype(np.float32)
    ang = pos[:, None] * inv[None, :]
    c[:TT, C_COS:C_COS + DH] = np.repeat(np.cos(ang), 2, axis=-1)
    sin = np.repeat(np.sin(ang), 2, axis=-1)
    c[:TT, C_SIN:C_SIN + DH // 2] = -sin[:, :DH // 2]
    c[:TT, C_SIN + DH // 2:C_SIN + DH] = sin[:, DH // 2:]
    c[:DK, C_HM:C_HM + G6] = np.arange(DK)[:, None] // DH == np.arange(G6)[None, :]
    c[:TT, C_T] = pos + 1
    c[:TT, C_RT] = 1.0 / (pos + 1)
    c[0, C_ONE:C_ONE + 128] = 1.0
    return c


def layouts(i):
    import numpy as np

    def halves(w):
        return w.reshape(2, DK, -1).transpose(1, 0, 2)

    a = {}
    p = i["x"].reshape(IMAGES, 3, SIDE, PATCH, SIDE, PATCH).transpose(0, 2, 4, 3, 5, 1).reshape(NT, TT, KX, 128)
    a["x"] = p.transpose(0, 3, 2, 1).reshape(NT, 128, KX * TT)
    a["w_patch"] = i["L0_tok_W"].T.reshape(KX, 128, D).transpose(1, 0, 2).reshape(128, KX * D)
    wg = i["L0_attn_Wg"].reshape(H, 3, D)
    a["w_proj"] = halves(np.concatenate([i["L0_attn_Wq"], i["L0_attn_Wk"], i["L0_attn_Wv"], i["L0_attn_Wu"],
                                         wg[:, 0], wg[:, 1]]).T)
    a["w_o"] = halves(i["L0_attn_Wo"].T)
    row = np.concatenate([i["L0_tok_b"], i["L0_attn_prior_mu"].reshape(-1), i["L0_attn_prior_log_tau"].reshape(-1)])
    a["params"] = np.broadcast_to(row, (TT, P_N))
    a["consts"] = constants()
    gate = i["L0_ffn_gate_weight"]
    a["w_gate"] = halves(np.concatenate([gate, gate]).T)
    wgu = np.stack([i["L0_ffn_Wg"].reshape(E, NCH, CH, D), i["L0_ffn_Wu"].reshape(E, NCH, CH, D)], axis=2)
    a["w_gu"] = wgu.reshape(E, 2 * F, 2, DK).transpose(0, 3, 2, 1)
    a["w_d"] = i["L0_ffn_Wd"].reshape(E, D, FK, 128).transpose(0, 3, 2, 1)
    a["ws_gu"] = halves(np.concatenate([i["L0_ffn_Ws_g"], i["L0_ffn_Ws_u"]]).T)
    a["ws_d"] = i["L0_ffn_Ws_d"].reshape(D, FSK, 128).transpose(2, 1, 0)
    return {k: np.ascontiguousarray(v) for k, v in a.items()}


def kernel(**inputs):
    import numpy as np
    from concourse import bacc
    from concourse.bass_utils import run_bass_kernel_spmd

    arrays = layouts({k: np.asarray(v) for k, v in inputs.items()})
    nc = bacc.Bacc("TRN2", target_bir_lowering=False, num_devices=1)
    args = [nc.dram_tensor(k, v.shape, mybir.dt.from_np(v.dtype), kind="ExternalInput").ap() for k, v in arrays.items()]
    out = nc.dram_tensor("out", (TOKENS, D), F32, kind="ExternalOutput").ap()
    build(nc, *args, out)
    r = run_bass_kernel_spmd(nc, [arrays], core_ids=[0])
    return r.results[0]["out"].reshape(IMAGES, L, D)
```

```python
from contextlib import ExitStack

import concourse.bass as bass
from concourse import mybir

ALU = mybir.AluOpType
ACT = mybir.ActivationFunctionType
AX_X = mybir.AxisListType.X
F32 = mybir.dt.float32
I32 = mybir.dt.int32
U32 = mybir.dt.uint32
F32R = mybir.dt.float32r

IMAGES, PATCH, SIDE = 16, 16, 7
L = SIDE * SIDE
TOKENS = IMAGES * L
PIX = 3 * PATCH * PATCH
D = 192
H, DH = 12, 16
TT = 2 * L
NT = TOKENS // TT
KX = PIX // 128
DK = D // 2
KA, KB = 128, D - 128
E = 16
CAP = -(-TOKENS * 2 // E)
F = 4 * D
FK = F // 128
FS = F // 2
FSK = FS // 128
HALF = TOKENS // 2
ROUNDS = -(-CAP // 8)
YT = 112
NY = TOKENS // YT
CH = 256
NCH = F // CH
G6 = 6
EPS = 1e-5
XRING = 4
RING = 4
SMALL = 4

C_ID, C_TRI, C_REV = 0, 128, 128 + TT
C_COS = C_REV + CAP
C_SIN = C_COS + DH
C_HM = C_SIN + DH
C_T = C_HM + G6
C_RT = C_T + 1
C_ONE = C_RT + 1
C_N = C_ONE + 128
P_B, P_MU, P_TAU, P_N = 0, D, 2 * D, 2 * D + H
QK, VU = 2 * D, 2 * D + 2 * H


def build(nc, x, w_patch, w_proj, w_o, params, consts, w_gate, w_gu, w_d, ws_gu, ws_d, out):
    h1_dram = nc.dram_tensor("h1_rows", (TOKENS, D + KB), F32, kind="Internal").ap()
    y_dram = nc.dram_tensor("y_rows", (TOKENS, D), F32, kind="Internal").ap()
    with ExitStack() as ctx:
        def sb(name, shape, dt=F32):
            return ctx.enter_context(nc.sbuf_tensor(name, shape, dt))

        def sem(name):
            return ctx.enter_context(nc.semaphore(name))

        bank = [ctx.enter_context(nc.psum_tensor(f"bank{i}", [128, 512], F32)) for i in range(8)]

        cst = sb("cst", [128, C_N])
        wgate_sb = sb("wgate_sb", [DK, 2, 2 * E])
        h1 = sb("h1", [TT, NT, D])
        h1T = sb("h1T", [DK, 2, TOKENS])
        wgu_sb = sb("wgu_sb", [KA, 2, 2 * F])
        wgu_b = sb("wgu_b", [KB, 2, 2 * F])
        wd_sb = sb("wd_sb", [128, RING, FK, D])
        wsgu_sb = sb("wsgu_sb", [DK, 2, 2 * FS])
        wsd_sb = sb("wsd_sb", [128, FSK, D])
        silu_s = sb("silu_s", [128, 2, HALF])
        hsT = sb("hsT", [128, FSK, TOKENS])

        attention = ctx.enter_context(ExitStack())

        def sa(name, shape, dt=F32):
            return attention.enter_context(nc.sbuf_tensor(name, shape, dt))

        par = sa("par", [TT, P_N])
        wo_sb = sa("wo_sb", [DK, 2, D])
        h0 = sa("h0", [TT, NT, D + KB])
        qk = sa("qk", [TT, NT, QK])
        norm2 = sa("norm2", [TT, NT, 2 * H])
        rnorm = sa("rnorm", [TT, NT, 2 * H])
        vug = sa("vug", [TT, NT, VU])
        s_raw = sa("s_raw", [TT, NT, H])
        es_s = sa("es_s", [TT, 2, NT * H])
        tau = sa("tau", [TT, 3, H])
        mu_row = sa("mu_row", [1, D])
        wv_mean = sa("wv_mean", [KA, 2, H])
        sT = sa("sT", [NT * H, 3, TT])
        s_max = sa("s_max", [NT * H, 2])
        gates = sa("gates", [TT, 3, NT, 2 * H])
        coef = sa("coef", [TT, NT * H, 3])
        vcoef = sa("vcoef", [TT, NT * H, 3])
        small = sa("small", [TT, 4, NT * H])

        projections = attention.enter_context(ExitStack())

        def sproj(name, shape, dt=F32):
            return projections.enter_context(nc.sbuf_tensor(name, shape, dt))

        x_sb = sproj("x_sb", [128, XRING, KX * TT])
        x_hi0 = sproj("x_hi0", [128, 2, KX * TT], F32R)
        x_lo0 = sproj("x_lo0", [128, 2, KX * TT], F32R)
        wp_sb = sproj("wp_sb", [128, KX * D])
        wp_hi = sproj("wp_hi", [128, KX * D], F32R)
        wp_lo = sproj("wp_lo", [128, KX * D], F32R)
        wproj_sb = sproj("wproj_sb", [KA, 2, QK + VU])
        wproj_hi = sproj("wproj_hi", [KA, QK + VU], F32R)
        wproj_lo = sproj("wproj_lo", [KA, QK + VU], F32R)
        wproj_b = sproj("wproj_b", [2 * KB, QK + VU], F32R)
        h0T_hi = sproj("h0T_hi", [KA, 2, 2 * TT], F32R)
        h0T_lo = sproj("h0T_lo", [KA, 2, 2 * TT], F32R)
        tri_r = sproj("tri_r", [TT, TT], F32R)
        ones_r = sproj("ones_r", [1, TT], F32R)
        mu_hi = sproj("mu_hi", [1, D], F32R)
        mu_lo = sproj("mu_lo", [1, D], F32R)
        u_hi = sproj("u_hi", [TT, 2, D], F32R)
        u_lo = sproj("u_lo", [TT, 2, D], F32R)
        rope_a = sproj("rope_a", [TT, 2, QK])
        rope_b = sproj("rope_b", [TT, 2, QK])
        squares = sproj("squares", [TT, 2, QK])
        u_bar = sproj("u_bar", [TT, 2, D])
        projections.close()

        v3 = sa("v3", [TT, 2, (H + 1) * 3 * DH])
        qkT = sa("qkT", [DK, 2, 4 * TT])
        q_exp = sa("q_exp", [DK, 2, 2, G6 * TT])
        pT = sa("pT", [TT, 2, H * TT])
        mix = sa("mix", [TT, 2, H * 3 * DH])
        o_sum = sa("o_sum", [TT, 2, D])
        o_att = sa("o_att", [TT, SMALL, D])
        o_sq = sa("o_sq", [TT, 2, D])
        o_var = sa("o_var", [TT, SMALL, 3 * H])
        o_n = sa("o_n", [TT, SMALL, D])
        oT = sa("oT", [DK, 2, 2 * TT])
        r1 = sa("r1", [TT, SMALL, D])
        bn1 = sa("bn1", [TT, SMALL, 6])
        mv1 = sa("mv1", [TT, SMALL, 4])
        attention.close()

        w_hi = sb("w_hi", [KA, 2, 2 * F], F32R)
        w_lo = sb("w_lo", [KA, 2, 2 * F], F32R)
        w_b = sb("w_b", [2 * KB, 2, 2 * F], F32R)
        rank_in = sb("rank_in", [64, 3, HALF])
        top_val = sb("top_val", [48, 8 * ROUNDS])
        top_idx = sb("top_idx", [48, 8 * ROUNDS], U32)
        top_row = sb("top_row", [48, CAP])
        top_T = sb("top_T", [CAP, 2, 48])
        pick = sb("pick", [CAP, 5, E])
        row_i = sb("row_i", [CAP, E], I32)
        score = sb("score", [CAP, E])
        xg = sb("xg", [CAP, RING, D + KB])
        x_hi = sb("x_hi", [KA, 2, 2 * CAP], F32R)
        x_lo = sb("x_lo", [KA, 2, 2 * CAP], F32R)
        silu_g = sb("silu_g", [CAP, NCH, CH])
        hid = sb("hid", [CAP, 2, F])
        hidT = sb("hidT", [128, FK, CAP])
        o_exp = sb("o_exp", [CAP, 2, D])
        y_base = sb("y_base", [TT, 2, NT, D])
        y = sb("y", [YT, NY, D])
        bn2 = sb("bn2", [YT, NY, 6])
        mv2 = sb("mv2", [YT, NY, 2])
        std2 = sb("std2", [YT, 3, NY])
        y_n = sb("y_n", [YT, NY, D])

        consts_in, wp_in, proj_in, rest_in = (sem(n) for n in ("consts_in", "wp_in", "proj_in", "rest_in"))
        x_in = [sem(f"x_in{j}") for j in range(NT)]
        h1_out = sem("h1_out")
        embed_done, h0_ready, h0T_psum, h0T_ready = (sem(n) for n in (
            "embed_done", "h0_ready", "h0T_psum", "h0T_ready"))
        qk_psum, vug_psum, qk_ready, qk_read, vug_ready, usum_done, s_ready, sq_ready, n2_ready = (sem(n) for n in (
            "qk_psum", "vug_psum", "qk_ready", "qk_read", "vug_ready", "usum_done", "s_ready", "sq_ready", "n2_ready"))
        tau_clip, tau_exp, tau_ready, wv_ready = (sem(n) for n in ("tau_clip", "tau_exp", "tau_ready", "wv_ready"))
        s_all, sT_psum, sT_sub, sT_exp, es_psum, es_ready, cum_done, coef_ready, gate_exp, norm_sqrt, vcoef_ready = (
            sem(n) for n in ("s_all", "sT_psum", "sT_sub", "sT_exp", "es_psum", "es_ready", "cum_done",
                             "coef_ready", "gate_exp", "norm_sqrt", "vcoef_ready"))
        qkT_psum, qkT_ready, q_exp_ready, score_done, p_ready, v3_ready, att_psum, mix_ready, osum_ready = (
            sem(n) for n in ("qkT_psum", "qkT_ready", "q_exp_ready", "score_done", "p_ready", "v3_ready",
                             "att_psum", "mix_ready", "osum_ready"))
        att_ready, osq_ready, ovar_ready, ostd_ready, on_ready, oT_psum, oT_ready, wo_done = (sem(n) for n in (
            "att_ready", "osq_ready", "ovar_ready", "ostd_ready", "on_ready", "oT_psum", "oT_ready", "wo_done"))
        r1_var, r1_std, r1_ready, h1_ready, h1T_psum, h1T_ready = (sem(n) for n in (
            "r1_var", "r1_std", "r1_ready", "h1_ready", "h1T_psum", "h1T_ready"))
        wo_in, wproj_hi_ready, wproj_lo_ready, h0T_hi_ready, q_exp_pool, v3_zero = (sem(n) for n in (
            "wo_in", "wproj_hi_ready", "wproj_lo_ready", "h0T_hi_ready", "q_exp_pool", "v3_zero"))
        ws_in = sem("ws_in")
        x_hi_made, x_lo_made, wp_hi_ready, wp_lo_ready, tri_ready, mu_hi_ready, mu_lo_ready, u_hi_ready, u_lo_ready = (
            sem(n) for n in ("x_hi_made", "x_lo_made", "wp_hi_ready", "wp_lo_ready", "tri_ready", "mu_hi_ready",
                             "mu_lo_ready", "u_hi_ready", "u_lo_ready"))
        norm_ready, gate_ready = sem("norm_ready"), sem("gate_ready")
        top_max, top_left = sem("top_max"), sem("top_left")
        wgu_in = [sem(f"wgu_in{n}") for n in range(2)]
        wd_in = [sem(f"wd_in{n}") for n in range(RING)]
        xg_in = [sem(f"xg_in{n}") for n in range(RING)]
        logit_psum, logit_ready, shared_gu, silu_s_ready, hs_ready, top_ready, top_psum, topT_ready, rev_psum = (
            sem(n) for n in ("logit_psum", "logit_ready", "shared_gu", "silu_s_ready", "hs_ready", "top_ready",
                             "top_psum", "topT_ready", "rev_psum"))
        pick_ready, row_ready, score_ready, shared_y, base_ready, base_added, base_out, y_add, y_in = (
            sem(n) for n in ("pick_ready", "row_ready", "score_ready", "shared_y", "base_ready", "base_added",
                             "base_out", "y_add", "y_in"))
        x_psum, x_hi_ready, x_lo_ready, w_hi_ready, w_lo_ready, w_lo0_ready = (sem(n) for n in (
            "x_psum", "x_hi_ready", "x_lo_ready", "w_hi_ready", "w_lo_ready", "w_lo0_ready"))
        gu_done, silu_ready, h_ready, turn_a, turn_b, turned_a, turned_b, down_done, out_ready = (
            sem(n) for n in ("gu_done", "silu_ready", "h_ready", "turn_a", "turn_b", "turned_a", "turned_b",
                             "down_done", "out_ready"))
        y_var, y_std, y_norm, y_out = (sem(n) for n in ("y_var", "y_std", "y_norm", "y_out"))
        v_order, p_order = sem("v_order"), sem("p_order")

        ident = cst[:, C_ID:C_ID + 128]
        tri = cst[0:TT, C_TRI:C_TRI + TT]
        rev = cst[0:CAP, C_REV:C_REV + CAP]
        ones_row = cst[0:1, C_ONE:C_ONE + TT]

        def heads(ap, n=H):
            return ap.rearrange("p (h e) -> p h e", h=n)

        def spread_q(eng, j, g):
            eng.wait_ge(qkT_ready, j + 1)
            if j >= 2:
                eng.wait_ge(score_done, 3 * (j - 1))
            return eng.tensor_tensor(q_exp[:, j % 2, g, :].rearrange("p (h t) -> p h t", h=G6),
                                     qkT[:, j % 2, g * TT:(g + 1) * TT].rearrange("p (o t) -> p o t", o=1)
                                     .broadcast_to([DK, G6, TT]),
                                     cst[0:DK, C_HM:C_HM + G6].rearrange("p (h o) -> p h o", o=1)
                                     .broadcast_to([DK, G6, TT]), ALU.mult)

        def over_experts(eng, step):
            for e in range(RING - 1):
                step(e, e)
            with eng.Fori(0, E // RING - 1) as i:
                for k in range(RING - 1, 2 * RING - 1):
                    step(i * RING + k, k % RING)
            for e in range(E - 1, E + 1):
                step(e, e % RING)

        def known(e, least=None, most=None):
            return not isinstance(e, int) or ((least is None or e >= least) and (most is None or e <= most))

        block = ctx.enter_context(nc.Block())

        @block.sync
        def _(sp):
            sp.dma_start(wp_sb[:, :], w_patch).then_inc(wp_in, 16)
            for j in range(NT):
                if j >= XRING:
                    sp.wait_ge(x_lo_made, j - XRING)
                    if j == XRING:
                        sp.wait_ge(embed_done, 1)
                sp.dma_start(x_sb[:, j % XRING, :], x[j]).then_inc(x_in[j], 16)
                if j == 1:
                    sp.dma_start(wproj_sb[:, 0, :], w_proj[0:KA, :]).then_inc(proj_in, 16)
                    sp.dma_start(wproj_sb[0:KB, 1, :], w_proj[KA:D, :]).then_inc(proj_in, 16)
            sp.dma_start(wo_sb[:, :, :], w_o).then_inc(wo_in, 16)
            sp.dma_start(wgate_sb[:, :, :], w_gate).then_inc(rest_in, 16)
            sp.dma_start(wsgu_sb[:, :, :], ws_gu).then_inc(ws_in, 16)
            sp.dma_start(wsd_sb[:, :, :], ws_d).then_inc(ws_in, 16)
            for e in range(2):
                sp.dma_start(wgu_sb[:, e, :], w_gu[e, 0:KA, :]).then_inc(wgu_in[e], 16)
                sp.dma_start(wgu_b[:, e, :], w_gu[e, KA:D, :]).then_inc(wgu_in[e], 16)
            for e in range(RING):
                sp.dma_start(wd_sb[:, e, :, :], w_d[e]).then_inc(wd_in[e], 16)
            for j in range(NT):
                sp.wait_ge(h1_ready, j + 1)
                sp.dma_start(h1_dram[j * TT:(j + 1) * TT, 0:D], h1[:, j, :]).then_inc(h1_out, 16)
                sp.dma_start(h1_dram[j * TT:(j + 1) * TT, D:D + KB], h1[:, j, KA:D]).then_inc(h1_out, 16)
            sp.wait_ge(w_lo0_ready, 2)
            sp.dma_start(wgu_sb[:, 0, :], w_gu[2, 0:KA, :]).then_inc(wgu_in[0], 16)
            sp.dma_start(wgu_b[:, 0, :], w_gu[2, KA:D, :]).then_inc(wgu_in[0], 16)
            sp.wait_ge(base_added, 1)
            sp.dma_start(y_dram.rearrange("(j p) d -> p j d", j=NT), y_base[:, 1, :, :]).then_inc(base_out, 16)

            def load_gu(e, k):
                sp.wait_ge(w_lo_ready, (e - 2) * 2 * NCH)
                sp.dma_start(wgu_sb[:, k % 2, :], w_gu[e, 0:KA, :] if isinstance(e, int) else
                             w_gu[bass.ds(e, 1), 0:KA, :].rearrange("o p n -> (o p) n")).then_inc(wgu_in[k % 2], 16)
                sp.dma_start(wgu_b[:, k % 2, :], w_gu[e, KA:D, :] if isinstance(e, int) else
                             w_gu[bass.ds(e, 1), KA:D, :].rearrange("o p n -> (o p) n")).then_inc(wgu_in[k % 2], 16)

            def load_d(e, k):
                sp.wait_ge(down_done, e - RING + 1)
                sp.dma_start(wd_sb[:, k, :, :], w_d[e]).then_inc(wd_in[k], 16)

            load_gu(3, 3)
            with sp.Fori(0, E // RING - 1) as i:
                for k in range(RING):
                    load_gu(i * RING + RING + k, k)
                    load_d(i * RING + RING + k, k)
            sp.wait_ge(y_add, 16 * E)
            sp.dma_start(y[:, :, :], y_dram.rearrange("(p t) d -> p t d", t=NY)).then_inc(y_in, 16)
            out_rows = out.rearrange("(p t) d -> p t d", t=NY)
            for part in (slice(0, 4), slice(4, NY)):
                sp.wait_ge(y_norm, part.stop)
                sp.dma_start(out_rows[:, part, :], y_n[:, part, :]).then_inc(y_out, 16)
            sp.wait_ge(y_out, 32)

        @block.tensor
        def _(pe):
            def embed(j):
                if j == 0:
                    pe.wait_ge(x_in[0], 16)
                    parts = [(x_sb, wp_sb)]
                else:
                    pe.wait_ge(x_lo_made, j)
                    parts = [(x_hi0, wp_hi), (x_lo0, wp_hi), (x_hi0, wp_lo)]
                if j == 1:
                    pe.wait_ge(wp_lo_ready, 1)
                if j >= 2:
                    pe.wait_ge(h0_ready, 2 * (j - 1))
                for m, (x_part, w_part) in enumerate(parts):
                    for c in range(KX):
                        last = pe.matmul(bank[j % 2][0:TT, 0:D], x_part[:, j % 2, c * TT:(c + 1) * TT],
                                         w_part[:, c * D:(c + 1) * D], start=(m == 0 and c == 0),
                                         stop=(m == len(parts) - 1 and c == KX - 1))
                last.then_inc(embed_done, 1)

            def turn_h0(j):
                pe.wait_ge(h0_ready, 2 * (j + 1))
                if j >= 1:
                    pe.wait_ge(h0T_ready, j)
                for c in range(2):
                    last = pe.transpose(bank[2][0:KA, c * TT:(c + 1) * TT], h0[:, j, c * KA:(c + 1) * KA],
                                        ident[0:TT, 0:TT])
                last.then_inc(h0T_psum, 1)

            def project(j):
                pe.wait_ge(h0T_ready, j + 1)
                if j >= 2:
                    pe.wait_ge(qk_read, j - 1)
                    pe.wait_ge(u_hi_ready, j - 1)
                for b, c0, n, done in ((3, 0, QK, qk_psum), (4, QK, VU, vug_psum)):
                    b += 3 * (j % 2)
                    parts = ((h0T_hi, 0, wproj_hi), (h0T_lo, 0, wproj_hi), (h0T_hi, TT, wproj_b),
                             (h0T_lo, TT, wproj_b), (h0T_hi, 0, wproj_lo))
                    for m, (x, x0, w) in enumerate(parts):
                        last = pe.matmul(bank[b][0:TT, 0:n], x[:, j % 2, x0:x0 + TT], w[:, c0:c0 + n],
                                         start=(m == 0), stop=(m == len(parts) - 1))
                    last.then_inc(done, 1)

            def sum_u(j):
                pe.wait_ge(u_lo_ready, j + 1)
                if j >= 1:
                    pe.wait_ge(s_ready, j)
                pe.matmul(bank[5][0:TT, 0:D], tri_r[:, :], u_hi[:, j % 2, :], start=True, stop=False)
                pe.matmul(bank[5][0:TT, 0:D], tri_r[:, :], u_lo[:, j % 2, :], start=False, stop=False)
                pe.matmul(bank[5][0:TT, 0:D], ones_r[:, :], mu_hi[:, :], start=False, stop=False)
                pe.matmul(bank[5][0:TT, 0:D], ones_r[:, :], mu_lo[:, :], start=False, stop=True).then_inc(usum_done, 1)

            pe.wait_ge(consts_in, 32)
            pe.wait_ge(wp_in, 16)
            embed(0)
            embed(1)
            turn_h0(0)
            for j in range(NT):
                if j + 2 < NT:
                    embed(j + 2)
                if j + 1 < NT:
                    turn_h0(j + 1)
                if j == 0:
                    pe.wait_ge(wproj_lo_ready, 2)
                project(j)
                if j == 0:
                    pe.wait_ge(tri_ready, 1)
                    pe.wait_ge(mu_lo_ready, 1)
                if j >= 1:
                    sum_u(j - 1)
            sum_u(NT - 1)

            def turn_qk(j):
                if j < 1:
                    pe.wait_ge(qk_read, NT)
                pe.wait_ge(qk_ready, j + 1)
                if j >= 1:
                    pe.wait_ge(qkT_ready, j)
                for c in range(4):
                    last = pe.transpose(bank[3][0:DK, c * TT:(c + 1) * TT], qk[:, j, c * DK:(c + 1) * DK],
                                        ident[0:TT, 0:TT])
                last.then_inc(qkT_psum, 1)

            def scores(j):
                pe.wait_ge(qkT_ready, j + 1)
                if j == 0:
                    pe.wait_ge(h0_ready, 2 * NT)
                    pe.wait_ge(h0T_ready, NT)
                for g, heads_of in enumerate((((0, 0, 4),), ((0, 4, 6), (1, 0, 2)), ((1, 2, 6),))):
                    if j >= 1:
                        pe.wait_ge(p_ready, 3 * (j - 1) + g + 1)
                    at = 0
                    for rows, first, end in heads_of:
                        pe.wait_ge((q_exp_ready, q_exp_pool)[rows], j + 1)
                        n = (end - first) * TT
                        last = pe.matmul(bank[g][0:TT, at:at + n], qkT[:, j % 2, (2 + rows) * TT:(3 + rows) * TT],
                                         q_exp[:, j % 2, rows, first * TT:end * TT], start=True, stop=True)
                        at += n
                    last.then_inc(score_done, 1)

            def attend(j):
                pe.wait_ge(p_ready, 3 * (j + 1))
                pe.wait_ge(v3_ready, j + 1)
                if j == 0:
                    pe.wait_ge(s_ready, NT)
                if j >= 1:
                    pe.wait_ge(mix_ready, 2 * j)
                for h in range(H):
                    at = (h % G6) * 3 * DH
                    last = pe.matmul(bank[4 + h // G6][0:TT, at:at + 6 * DH],
                                     pT[:, j % 2, h * TT:(h + 1) * TT], v3[:, j % 2, h * 3 * DH:(h + 2) * 3 * DH],
                                     start=True, stop=True)
                    if h % G6 == G6 - 1:
                        last.then_inc(att_psum, 1)

            def turn_o(j):
                pe.wait_ge(on_ready, j + 1)
                if j >= 1:
                    pe.wait_ge(oT_ready, j)
                for c in range(2):
                    last = pe.transpose(bank[6][0:DK, c * TT:(c + 1) * TT], o_n[:, j % SMALL, c * DK:(c + 1) * DK],
                                        ident[0:TT, 0:TT])
                last.then_inc(oT_psum, 1)

            def project_o(j):
                pe.wait_ge(oT_ready, j + 1)
                if j >= 1:
                    pe.wait_ge(r1_ready, j)
                for c in range(2):
                    last = pe.matmul(bank[7][0:TT, 0:D], oT[:, j % 2, c * TT:(c + 1) * TT], wo_sb[:, c, :],
                                     start=(c == 0), stop=(c == 1))
                last.then_inc(wo_done, 1)

            def turn_h1(j):
                pe.wait_ge(h1_ready, j + 1)
                if j == 0:
                    pe.wait_ge(qkT_ready, NT)
                    pe.wait_ge(p_ready, 3 * NT)
                if j >= 2:
                    pe.wait_ge(h1T_ready, j - 1)
                for c in range(2):
                    last = pe.transpose(bank[3 * (j % 2)][0:DK, c * TT:(c + 1) * TT], h1[:, j, c * DK:(c + 1) * DK],
                                        ident[0:TT, 0:TT])
                last.then_inc(h1T_psum, 1)

            def logits(j):
                pe.wait_ge(h1T_ready, j + 1)
                half, at = divmod(j * TT, HALF)
                for c in range(2):
                    last = pe.matmul(bank[2][32 * half:32 * half + 32, at:at + TT], wgate_sb[:, c, :],
                                     h1T[:, c, j * TT:(j + 1) * TT], start=(c == 0), stop=(c == 1))
                last.then_inc(logit_psum, 1)

            def shared(m):
                n, f = divmod(m, FSK)
                if m >= 2:
                    pe.wait_ge(hs_ready, m - 1)
                for b, f0 in ((0, f * 128), (3, FS + f * 128)):
                    for c in range(2):
                        last = pe.matmul(bank[b + m % 2][:, 0:HALF], wsgu_sb[:, c, f0:f0 + 128],
                                         h1T[:, c, n * HALF:(n + 1) * HALF], start=(c == 0), stop=(c == 1))
                last.then_inc(shared_gu, 1)

            turn_qk(0)
            pe.wait_ge(s_all, 1)
            pe.transpose(bank[5][0:NT * H, 0:TT], es_s[:, 1, :], ident[0:TT, 0:TT]).then_inc(sT_psum, 1)
            pe.wait_ge(sT_exp, 1)
            pe.transpose(bank[7][0:TT, 0:NT * H], sT[:, 2, :], ident[0:NT * H, 0:NT * H]).then_inc(es_psum, 1)
            scores(0)
            pe.wait_ge(es_ready, 1)
            pe.matmul(bank[6][0:TT, 0:2 * NT * H], tri, es_s[:, :, :].rearrange("p a b -> p (a b)"),
                      start=True, stop=True).then_inc(cum_done, 1)
            turn_qk(1)
            scores(1)
            turn_qk(2)
            pe.wait_ge(wo_in, 16)
            for i in range(1, NT):
                if i >= 2:
                    scores(i)
                attend(i - 1)
                if 3 <= i + 2 < NT:
                    turn_qk(i + 2)
                if i >= 3:
                    if i == 3:
                        pe.wait_ge(coef_ready, 1)
                    turn_o(i - 3)
                if i >= 4:
                    project_o(i - 4)
            attend(NT - 1)
            turn_h1(0)
            turn_o(NT - 3)
            project_o(NT - 4)
            turn_h1(1)
            pe.wait_ge(rest_in, 16)
            logits(0)
            project_o(NT - 3)
            turn_h1(2)
            logits(1)
            turn_o(NT - 2)
            turn_h1(3)
            logits(2)
            project_o(NT - 2)
            turn_h1(4)
            logits(3)
            turn_o(NT - 1)
            turn_h1(5)
            logits(4)
            project_o(NT - 1)
            logits(5)
            turn_h1(6)
            logits(6)
            turn_h1(7)
            logits(7)
            pe.wait_ge(ws_in, 32)
            for m in range(2 * FSK):
                shared(m)
            pe.wait_ge(hs_ready, 2 * FSK)

            def shared_down(j):
                if j >= 2:
                    pe.wait_ge(base_ready, j - 1)
                for f in range(FSK):
                    last = pe.matmul(bank[6 + j % 2][0:TT, 0:D], hsT[:, f, j * TT:(j + 1) * TT], wsd_sb[:, f, :],
                                     start=(f == 0), stop=(f == FSK - 1))
                last.then_inc(shared_y, 1)

            for j in range(NT - 3):
                shared_down(j)
            pe.wait_ge(top_ready, 1)
            pe.transpose(bank[5][0:CAP, 0:48], top_val[:, 0:CAP], ident[0:48, 0:48])
            pe.transpose(bank[5][0:CAP, 48:96], top_row[:, :], ident[0:48, 0:48]).then_inc(top_psum, 1)
            shared_down(NT - 3)
            pe.wait_ge(topT_ready, 1)
            pe.matmul(bank[2][0:CAP, 0:2 * E], rev, top_T[:, :, 32:48], start=True, stop=True).then_inc(rev_psum, 1)
            shared_down(NT - 2)
            shared_down(NT - 1)

            def turn_x(e, k):
                pe.wait_ge(xg_in[k], (e - k) * (16 // RING) + 16)
                if known(e, 1):
                    pe.wait_ge(x_lo_ready, e)
                for c in range(2):
                    last = pe.transpose(bank[6][0:KA, c * CAP:(c + 1) * CAP], xg[:, k, c * KA:(c + 1) * KA],
                                        ident[0:CAP, 0:CAP])
                last.then_inc(x_psum, 1)

            def gate_up(e, k, c):
                if known(e, 1):
                    pe.wait_ge(h_ready, e * NCH - NCH + c + 1)
                    pe.wait_ge(w_lo_ready, (e * NCH - NCH + c + 1) * 2)
                parts = ((x_hi, 0, w_hi), (x_hi, 0, w_lo), (x_lo, 0, w_hi), (x_hi, CAP, w_b), (x_lo, CAP, w_b))
                for m, (x, x0, w) in enumerate(parts):
                    last = pe.matmul(bank[c][0:CAP, 0:2 * CH], x[:, k % 2, x0:x0 + CAP],
                                     w[:, k % 2, c * 2 * CH:(c + 1) * 2 * CH],
                                     start=(m == 0), stop=(m == len(parts) - 1))
                last.then_inc(gu_done, 1)

            def turn_hidden(e, k, tiles, b, done):
                for n, c in enumerate(tiles):
                    last = pe.transpose(bank[b][:, n * CAP:(n + 1) * CAP], hid[:, k % 2, c * 128:(c + 1) * 128],
                                        ident[0:CAP, 0:CAP])
                last.then_inc(done, 1)

            def step(e, k):
                last_k = (k - 1) % RING
                if known(e, None, E - 1):
                    pe.wait_ge(x_lo_ready, e + 1)
                    gate_up(e, k, 0)
                if known(e, None, E - 2):
                    turn_x(e + 1, (k + 1) % RING)
                if known(e, 1):
                    pe.wait_ge(h_ready, e * NCH)
                    turn_hidden(e - 1, last_k, range(4, FK), 4, turn_b)
                if known(e, None, E - 1):
                    gate_up(e, k, 1)
                if known(e, 1):
                    pe.wait_ge(wd_in[last_k], (e - 1 - last_k) * (16 // RING) + 16)
                    pe.wait_ge(turned_a, e)
                    pe.wait_ge(turned_b, e)
                    if known(e, 2):
                        pe.wait_ge(out_ready, e - 1)
                    for c in range(FK):
                        last = pe.matmul(bank[5][0:CAP, 0:D], hidT[:, c, :], wd_sb[:, last_k, c, :],
                                         start=(c == 0), stop=(c == FK - 1))
                    last.then_inc(down_done, 1)
                if known(e, None, E - 1):
                    gate_up(e, k, 2)
                    pe.wait_ge(h_ready, e * NCH + 2)
                    turn_hidden(e, k, range(4), 3, turn_a)

            pe.wait_ge(base_ready, NT)
            turn_x(0, 0)
            pe.wait_ge(w_lo0_ready, 2)
            pe.wait_ge(row_ready, 1)
            over_experts(pe, step)

        @block.scalar
        def _(act):
            act.dma_start(cst[:, :], consts).then_inc(consts_in, 16)
            act.dma_start(par[:, :], params).then_inc(consts_in, 16)
            def copy_qkT(j):
                act.wait_ge(qkT_psum, j + 1)
                if j >= 2:
                    act.wait_ge(score_done, 3 * (j - 1))
                act.copy(qkT[:, j % 2, :], bank[3][0:DK, 0:4 * TT]).then_inc(qkT_ready, 1)

            act.wait_ge(tau_clip, 1)
            act.activation(tau[:, 1, :], tau[:, 0, :], ACT.Exp).then_inc(tau_exp, 1)

            def upper_h0T(j):
                act.wait_ge(h0T_psum, j + 1)
                if j >= 2:
                    act.wait_ge(vug_psum, j - 1)
                act.copy(h0T_hi[:, j % 2, :], bank[2][0:KA, 0:2 * TT]).then_inc(h0T_hi_ready, 1)

            def upper_x(j):
                act.wait_ge(x_in[j], 16)
                if j >= 3:
                    act.wait_ge(embed_done, j - 1)
                act.copy(x_hi0[:, j % 2, :], x_sb[:, j % XRING, :]).then_inc(x_hi_made, 1)

            def projected(j):
                act.wait_ge(vug_psum, j + 1)
                act.copy(vug[:, j, :], bank[4 + 3 * (j % 2)][0:TT, 0:VU]).then_inc(vug_ready, 1)
                if j >= 2:
                    act.wait_ge(usum_done, j - 1)
                act.copy(u_hi[:, j % 2, :], bank[4 + 3 * (j % 2)][0:TT, D:2 * D]).then_inc(u_hi_ready, 1)
                act.wait_ge(qk_ready, j + 1)
                if j >= 2:
                    act.wait_ge(n2_ready, j - 1)
                act.activation(squares[:, j % 2, :], qk[:, j, :], ACT.Square).then_inc(sq_ready, 1)

            def root_norm(j):
                act.wait_ge(n2_ready, j + 1)
                act.activation(rnorm[:, j, :], norm2[:, j, :], ACT.Sqrt).then_inc(norm_sqrt, 1)

            act.wait_ge(wp_in, 16)
            act.copy(wp_hi[:, :], wp_sb[:, :]).then_inc(wp_hi_ready, 1)
            upper_x(1)
            upper_x(2)
            act.wait_ge(wv_ready, 2)
            act.copy(wproj_hi[:, :], wproj_sb[:, 0, :])
            act.copy(wproj_b[0:KB, :], wproj_sb[0:KB, 1, :]).then_inc(wproj_hi_ready, 1)
            act.copy(tri_r[:, :], tri)
            act.copy(ones_r[:, :], ones_row).then_inc(tri_ready, 1)
            act.wait_ge(tau_ready, 2)
            act.copy(mu_hi[:, :], mu_row[:, :]).then_inc(mu_hi_ready, 1)
            for j in range(NT):
                upper_h0T(j)
                if j + 3 < NT:
                    upper_x(j + 3)
                if j >= 1:
                    projected(j - 1)
                if j >= 2:
                    root_norm(j - 2)
            projected(NT - 1)
            root_norm(NT - 2)
            act.wait_ge(vug_ready, NT)
            act.activation(gates[:, 0, :, :], vug[:, :, 2 * D:VU], ACT.Exp, scale=-1.0).then_inc(gate_exp, 1)
            act.wait_ge(qk_ready, NT)
            act.wait_ge(n2_ready, NT)
            act.wait_ge(s_ready, NT)
            copy_qkT(0)
            act.wait_ge(sT_sub, 1)
            act.activation(sT[:, 2, :], sT[:, 1, :], ACT.Exp).then_inc(sT_exp, 1)
            root_norm(NT - 1)
            copy_qkT(1)

            def square_o(j):
                act.wait_ge(att_ready, j + 1)
                if j >= 2:
                    act.wait_ge(ovar_ready, j - 1)
                act.activation(o_sq[:, j % 2, :], o_att[:, j % SMALL, :], ACT.Square).then_inc(osq_ready, 1)

            def root_o(j):
                act.wait_ge(ovar_ready, j + 1)
                act.activation(o_var[:, j % SMALL, H:2 * H], o_var[:, j % SMALL, 0:H], ACT.Sqrt).then_inc(ostd_ready, 1)

            def copy_oT(j):
                act.wait_ge(oT_psum, j + 1)
                if j >= 2:
                    act.wait_ge(wo_done, j - 1)
                act.copy(oT[:, j % 2, :], bank[6][0:DK, 0:2 * TT]).then_inc(oT_ready, 1)

            def root_r(j):
                act.wait_ge(r1_var, j + 1)
                act.activation(mv1[:, j % SMALL, 2:3], mv1[:, j % SMALL, 1:2], ACT.Sqrt).then_inc(r1_std, 1)

            def copy_h1T(j):
                act.wait_ge(h1T_psum, j + 1)
                act.copy(h1T[:, :, j * TT:(j + 1) * TT],
                         bank[3 * (j % 2)][0:DK, 0:2 * TT].rearrange("p (c t) -> p c t", c=2)).then_inc(h1T_ready, 1)

            def silu_shared(m):
                act.wait_ge(shared_gu, m + 1)
                if m >= 2:
                    act.wait_ge(hs_ready, m - 1)
                act.activation(silu_s[:, m % 2, :], bank[m % 2][:, 0:HALF], ACT.Silu).then_inc(silu_s_ready, 1)

            copy_qkT(2)
            for i in range(1, NT):
                if 3 <= i + 2 < NT:
                    copy_qkT(i + 2)
                if i >= 3:
                    copy_oT(i - 3)
                if i >= 5:
                    root_r(i - 5)
                if i >= 2:
                    root_o(i - 2)
                square_o(i - 1)
            copy_h1T(0)
            copy_oT(NT - 3)
            copy_h1T(1)
            root_r(NT - 5)
            root_o(NT - 2)
            copy_h1T(2)
            root_r(NT - 4)
            copy_oT(NT - 2)
            square_o(NT - 1)
            copy_h1T(3)
            root_r(NT - 3)
            root_o(NT - 1)
            copy_h1T(4)
            copy_oT(NT - 1)
            root_r(NT - 2)
            copy_h1T(5)
            copy_h1T(6)
            root_r(NT - 1)
            copy_h1T(7)
            act.wait_ge(logit_psum, NT)
            act.copy(rank_in[:, 0, :], bank[2][0:64, 0:HALF]).then_inc(logit_ready, 1)

            def split_hi(e, k, c):
                if known(e, 2):
                    act.wait_ge(gu_done, (e - 2) * NCH + c + 1)
                cols = slice(c * 2 * CH, (c + 1) * 2 * CH)
                act.copy(w_hi[:, k % 2, cols], wgu_sb[:, k % 2, cols])
                act.copy(w_b[0:KB, k % 2, cols], wgu_b[:, k % 2, cols]).then_inc(w_hi_ready, 1)

            act.wait_ge(wgu_in[0], 32)
            for m in range(2 * FSK):
                silu_shared(m)
                if m < NCH:
                    split_hi(0, 0, m)
            for j in range(NT):
                if j == NT - 3:
                    act.wait_ge(top_psum, 1)
                    act.copy(top_T[:, :, :].rearrange("p a b -> p (a b)"), bank[5][0:CAP, 0:96]).then_inc(topT_ready, 1)
                act.wait_ge(shared_y, j + 1)
                act.copy(y_base[:, 0, j, :], bank[6 + j % 2][0:TT, 0:D]).then_inc(base_ready, 1)
            act.wait_ge(pick_ready, 1)
            act.activation(score[:, :], pick[:, 0, :], ACT.Sigmoid).then_inc(score_ready, 1)

            def x_upper(e, k):
                act.wait_ge(x_psum, e + 1)
                if known(e, 2):
                    act.wait_ge(gu_done, (e - 1) * NCH)
                act.copy(x_hi[:, k % 2, :], bank[6][0:KA, 0:2 * CAP]).then_inc(x_hi_ready, 1)

            def silu_gate(e, k, c):
                act.wait_ge(gu_done, e * NCH + c + 1)
                if known(e, 1):
                    act.wait_ge(h_ready, e * NCH - NCH + c + 1)
                act.activation(silu_g[:, c, :], bank[c][0:CAP, 0:CH], ACT.Silu).then_inc(silu_ready, 1)

            def step(e, k):
                nxt = (k + 1) % RING
                if known(e, None, E - 1):
                    silu_gate(e, k, 0)
                if known(e, None, E - 2):
                    x_upper(e + 1, nxt)
                    act.wait_ge(wgu_in[nxt % 2], (e + 1 - nxt % 2) * 16 + 32)
                if known(e, 1):
                    act.wait_ge(turn_b, e)
                    act.copy(hidT[:, 4:FK, :].rearrange("p a b -> p (a b)"), bank[4][:, 0:2 * CAP]).then_inc(turned_b, 1)
                if known(e, None, E - 2):
                    split_hi(e + 1, nxt, 0)
                if known(e, None, E - 1):
                    silu_gate(e, k, 1)
                if known(e, None, E - 2):
                    split_hi(e + 1, nxt, 1)
                if known(e, None, E - 1):
                    silu_gate(e, k, 2)
                    act.wait_ge(turn_a, e + 1)
                    if known(e, 1):
                        act.wait_ge(down_done, e)
                    act.copy(hidT[:, 0:4, :].rearrange("p a b -> p (a b)"), bank[3][:, 0:4 * CAP]).then_inc(turned_a, 1)
                if known(e, None, E - 2):
                    split_hi(e + 1, nxt, 2)

            x_upper(0, 0)
            over_experts(act, step)
            act.wait_ge(y_var, 1)
            act.activation(std2[:, 1, :], std2[:, 0, :], ACT.Sqrt).then_inc(y_std, 1)

        @block.gpsimd
        def _(pool):
            def lower_x(j):
                pool.wait_ge(x_hi_made, j)
                if j >= 3:
                    pool.wait_ge(embed_done, j - 1)
                pool.tensor_tensor(x_lo0[:, j % 2, :], x_sb[:, j % XRING, :], x_hi0[:, j % 2, :].bitcast(F32),
                                   ALU.subtract).then_inc(x_lo_made, 1)

            lower_x(1)
            pool.wait_ge(x_lo_made, 1)
            lower_x(2)
            pool.wait_ge(wproj_hi_ready, 1)
            pool.tensor_tensor(wproj_lo[:, :], wproj_sb[:, 0, :], wproj_hi[:, :].bitcast(F32), ALU.subtract)\
                .then_inc(wproj_lo_ready, 1)
            for j in range(NT):
                if j + 3 < NT:
                    lower_x(j + 3)
                pool.wait_ge(qk_read, j + 1)
                pool.tensor_tensor(qk[:, j, :], rope_a[:, j % 2, :], rope_b[:, j % 2, :], ALU.add)\
                    .then_inc(qk_ready, 1)

            def spread_v(j):
                if j >= 2:
                    pool.wait_ge(att_psum, 2 * (j - 1))
                v = heads(vug[:, j, 0:D])
                for c in range(3):
                    last = pool.tensor_tensor(
                        v3[:, j % 2, 0:H * 3 * DH].rearrange("p (h c e) -> p h c e", h=H, c=3)[:, :, c, :], v,
                        vcoef[:, j * H:(j + 1) * H, c:c + 1].broadcast_to([TT, H, DH]), ALU.mult)
                last.then_inc(v3_ready, 1)

            def sum_mix(j):
                pool.wait_ge(mix_ready, 2 * (j + 1))
                m = mix[:, j % 2, :].rearrange("p (h c e) -> p h c e", h=H, c=3)
                pool.tensor_tensor(heads(o_sum[:, j % 2, :]), m[:, :, 0, :], m[:, :, 1, :], ALU.add)\
                    .then_inc(p_order, 1)
                pool.wait_ge(p_order, j + 1)
                if j >= SMALL:
                    pool.wait_ge(on_ready, j - SMALL + 1)
                pool.tensor_tensor(heads(o_att[:, j % SMALL, :]), heads(o_sum[:, j % 2, :]), m[:, :, 2, :], ALU.add)\
                    .then_inc(att_ready, 1)

            def expand_q(j):
                spread_q(pool, j, 1).then_inc(q_exp_pool, 1)

            expand_q(0)
            pool.memset(v3[:, :, H * 3 * DH:], 0.0).then_inc(v3_zero, 1)
            expand_q(1)
            pool.wait_ge(vcoef_ready, 1)
            spread_v(0)
            spread_v(1)
            for j in range(NT):
                if j + 2 < NT:
                    expand_q(j + 2)
                sum_mix(j)
                if j + 2 < NT:
                    spread_v(j + 2)

            pool.wait_ge(w_hi_ready, NCH)
            pool.tensor_tensor(w_b[KB:2 * KB, 0, :], wgu_b[:, 0, :], w_b[0:KB, 0, :].bitcast(F32), ALU.subtract)\
                .then_inc(w_lo0_ready, 1)
            pool.wait_ge(w_lo0_ready, 1)
            pool.tensor_tensor(w_lo[:, 0, :], wgu_sb[:, 0, :], w_hi[:, 0, :].bitcast(F32), ALU.subtract)\
                .then_inc(w_lo0_ready, 1)
            pool.wait_ge(h1_out, 32 * NT)
            pool.wait_ge(row_ready, 1)

            def gather(e):
                k = e % RING
                pool.indirect_dma_start(xg[:, k, :], None, h1_dram,
                                        bass.IndirectOffsetOnAxis(ap=row_i[:, e:e + 1], axis=0)).then_inc(xg_in[k], 16)

            for e in range(RING):
                gather(e)
            pool.wait_ge(base_ready, NT)
            pool.tensor_tensor(y_base[:, 1, :, :], y_base[:, 0, :, :], h1[:, :, :], ALU.add).then_inc(base_added, 1)
            pool.wait_ge(base_out, 16)
            for e in range(E):
                if e + RING < E:
                    pool.wait_ge(x_psum, e + 1)
                    gather(e + RING)
                pool.wait_ge(out_ready, e + 1)
                if e >= 1:
                    pool.wait_ge(y_add, 16 * e)
                pool.indirect_dma_start(y_dram, bass.IndirectOffsetOnAxis(ap=row_i[:, e:e + 1], axis=0),
                                        o_exp[:, e % 2, :], None, compute_op=ALU.add).then_inc(y_add, 16)

        @block.vector
        def _(dve):
            order = [0]

            def link(ins):
                order[0] += 1
                ins.then_inc(v_order, 1)
                dve.wait_ge(v_order, order[0])

            dve.wait_ge(consts_in, 32)
            dve.tensor_scalar(tau[:, 0, :], par[:, P_TAU:P_TAU + H], -50.0, 30.0, ALU.max, ALU.min)\
                .then_inc(tau_clip, 1)
            dve.wait_ge(tau_exp, 1)
            link(dve.tensor_tensor(heads(mu_row[:, :]), heads(par[0:1, P_MU:P_MU + D]),
                                   tau[0:1, 1, :].rearrange("p (h o) -> p h o", o=1).broadcast_to([1, H, DH]), ALU.mult))
            link(dve.tensor_scalar(tau[:, 0, :], tau[:, 1, :], cst[0:TT, C_T:C_T + 1], -float(DH) ** 0.5, ALU.add, ALU.mult))
            dve.reciprocal(tau[:, 2, :], tau[:, 0, :]).then_inc(tau_ready, 2)
            dve.wait_ge(wp_hi_ready, 1)
            dve.tensor_tensor(wp_lo[:, :], wp_sb[:, :], wp_hi[:, :].bitcast(F32), ALU.subtract).then_inc(wp_lo_ready, 1)
            dve.wait_ge(proj_in, 32)
            for c, rows in enumerate((KA, KB)):
                wv = heads(wproj_sb[0:rows, c, QK:QK + D])
                mean = wv_mean[0:rows, c, :]
                link(dve.tensor_reduce(mean, wv, AX_X, ALU.add))
                link(dve.tensor_scalar(mean, mean, 1.0 / DH, None, ALU.mult))
                dve.tensor_tensor(wv, wv, mean.rearrange("p (h o) -> p h o", o=1)
                                  .broadcast_to([rows, H, DH]), ALU.subtract).then_inc(wv_ready, 1)

            def add_bias(j):
                dve.wait_ge(embed_done, j + 1)
                for to, c0, n in ((0, 0, D), (D, KA, KB)):
                    dve.tensor_tensor(h0[:, j, to:to + n], bank[j % 2][0:TT, c0:c0 + n],
                                      par[:, P_B + c0:P_B + c0 + n], ALU.add).then_inc(h0_ready, 1)

            def lower_h0T(j):
                dve.wait_ge(h0T_hi_ready, j + 1)
                dve.tensor_tensor(h0T_lo[:, j % 2, :], bank[2][0:KA, 0:2 * TT], h0T_hi[:, j % 2, :].bitcast(F32),
                                  ALU.subtract).then_inc(h0T_ready, 1)

            def rope(j):
                dve.wait_ge(qk_psum, j + 1)
                if j >= 2:
                    dve.wait_ge(qk_ready, j - 1)
                src = bank[3 + 3 * (j % 2)][0:TT, 0:QK].rearrange("p (h e) -> p h e", e=DH)
                cos = cst[0:TT, C_COS:C_COS + DH].rearrange("p (o e) -> p o e", o=1)
                sin = cst[0:TT, C_SIN:C_SIN + DH].rearrange("p (o e) -> p o e", o=1)
                a = rope_a[:, j % 2, :].rearrange("p (h e) -> p h e", e=DH)
                b = rope_b[:, j % 2, :].rearrange("p (h e) -> p h e", e=DH)
                hd = DH // 2
                dve.tensor_tensor(a, src, cos.broadcast_to([TT, 2 * H, DH]), ALU.mult)
                dve.tensor_tensor(b[:, :, 0:hd], src[:, :, hd:DH],
                                  sin[:, :, 0:hd].broadcast_to([TT, 2 * H, hd]), ALU.mult)
                dve.tensor_tensor(b[:, :, hd:DH], src[:, :, 0:hd],
                                  sin[:, :, hd:DH].broadcast_to([TT, 2 * H, hd]), ALU.mult).then_inc(qk_read, 1)

            def sum_squares(j):
                dve.wait_ge(sq_ready, j + 1)
                dve.tensor_reduce(norm2[:, j, :], squares[:, j % 2, :].rearrange("p (h e) -> p h e", e=DH),
                                  AX_X, ALU.add).then_inc(n2_ready, 1)

            def invert_norm(j):
                dve.wait_ge(norm_sqrt, j + 1)
                link(dve.tensor_scalar(norm2[:, j, :], rnorm[:, j, :], 1e-12, None, ALU.max))
                dve.reciprocal(rnorm[:, j, :], norm2[:, j, :]).then_inc(norm_ready, 1)

            def dot_u(j):
                dve.wait_ge(usum_done, j + 1)
                link(dve.tensor_tensor(u_bar[:, j % 2, :], bank[5][0:TT, 0:D], vug[:, j, D:2 * D], ALU.mult))
                dve.tensor_reduce(s_raw[:, j, :], heads(u_bar[:, j % 2, :]), AX_X, ALU.add).then_inc(s_ready, 1)

            def lower_u(j):
                dve.wait_ge(u_hi_ready, j + 1)
                dve.tensor_tensor(u_lo[:, j % 2, :], vug[:, j, D:2 * D],
                                  u_hi[:, j % 2, :].bitcast(F32), ALU.subtract).then_inc(u_lo_ready, 1)

            add_bias(0)
            add_bias(1)
            dve.wait_ge(wproj_hi_ready, 1)
            dve.tensor_tensor(wproj_b[KB:2 * KB, :], wproj_sb[0:KB, 1, :], wproj_b[0:KB, :].bitcast(F32),
                              ALU.subtract).then_inc(wproj_lo_ready, 1)
            lower_h0T(0)
            dve.wait_ge(mu_hi_ready, 1)
            dve.tensor_tensor(mu_lo[:, :], mu_row[:, :], mu_hi[:, :].bitcast(F32), ALU.subtract).then_inc(mu_lo_ready, 1)
            for j in range(NT):
                if j + 2 < NT:
                    add_bias(j + 2)
                if j + 1 < NT:
                    lower_h0T(j + 1)
                rope(j)
                lower_u(j)
                if j >= 1:
                    sum_squares(j - 1)
                    dot_u(j - 1)
                if j >= 2:
                    invert_norm(j - 2)
            dot_u(NT - 1)
            dve.wait_ge(s_ready, NT)
            dve.tensor_tensor(es_s[:, 1, :].rearrange("p (j h) -> p j h", j=NT), s_raw[:, :, :],
                              tau[:, 2, :].rearrange("p (o h) -> p o h", o=1).broadcast_to([TT, NT, H]), ALU.mult)\
                .then_inc(s_all, 1)
            sum_squares(NT - 1)
            invert_norm(NT - 2)

            def expand_q(j):
                spread_q(dve, j, 0).then_inc(q_exp_ready, 1)

            def mask(j):
                if j >= 2:
                    dve.wait_ge(att_psum, 2 * (j - 1))
                for g in range(3):
                    dve.wait_ge(score_done, 3 * j + g + 1)
                    dve.tensor_tensor(pT[:, j % 2, g * 4 * TT:(g + 1) * 4 * TT].rearrange("p (h t) -> p h t", h=4),
                                      bank[g][0:TT, 0:4 * TT].rearrange("p (h t) -> p h t", h=4),
                                      tri.rearrange("p (o t) -> p o t", o=1).broadcast_to([TT, 4, TT]),
                                      ALU.mult).then_inc(p_ready, 1)

            dve.wait_ge(sT_psum, 1)
            sT_ps = bank[5][0:NT * H, 0:TT].rearrange("p (i l) -> p i l", i=2)
            link(dve.tensor_reduce(s_max[:, :], sT_ps, AX_X, ALU.max))
            dve.tensor_tensor(sT[:, 1, :].rearrange("p (i l) -> p i l", i=2), sT_ps,
                              s_max[:, :].rearrange("p (i o) -> p i o", o=1).broadcast_to([NT * H, 2, L]),
                              ALU.subtract).then_inc(sT_sub, 1)
            expand_q(0)
            invert_norm(NT - 1)
            dve.wait_ge(norm_ready, NT)
            rq, rk = rnorm[:, :, 0:H], rnorm[:, :, H:2 * H]
            dve.wait_ge(es_psum, 1)
            dve.tensor_copy(es_s[:, 0, :], bank[7][0:TT, 0:NT * H]).then_inc(es_ready, 1)
            dve.wait_ge(es_ready, 1)

            def by_tile(ap):
                return ap.rearrange("p (j h) -> p j h", j=NT)

            dve.tensor_tensor(by_tile(vcoef[:, :, 0]), by_tile(es_s[:, 0, :]), rk, ALU.mult)
            dve.tensor_tensor(by_tile(vcoef[:, :, 1]), by_tile(es_s[:, 1, :]), rk, ALU.mult)
            dve.tensor_copy(by_tile(vcoef[:, :, 2]), rk).then_inc(vcoef_ready, 1)
            mask(0)
            expand_q(1)
            dve.wait_ge(gate_exp, 1)
            link(dve.tensor_scalar(gates[:, 1, :, :], gates[:, 0, :, :], 1.0, None, ALU.add))
            dve.reciprocal(gates[:, 2, :, :], gates[:, 1, :, :]).then_inc(gate_ready, 1)
            sig1, sigh = gates[:, 2, :, 0:H], gates[:, 2, :, H:2 * H]
            rt = cst[0:TT, C_RT:C_RT + 1]
            a, b, c, d = (small[:, n, :] for n in range(4))
            dve.wait_ge(gate_ready, 1)
            dve.wait_ge(cum_done, 1)
            link(dve.tensor_scalar(a, bank[6][0:TT, 0:NT * H], 1e-12, None, ALU.add))
            link(dve.reciprocal(b, a))
            dve.tensor_tensor(by_tile(c), sig1, sigh, ALU.subtract)
            link(dve.tensor_tensor(by_tile(a), by_tile(b), sigh, ALU.mult))
            dve.tensor_tensor(by_tile(coef[:, :, 0]), by_tile(a), rq, ALU.mult)
            link(dve.tensor_scalar(d, c, rt, None, ALU.mult))
            link(dve.tensor_tensor(b, d, bank[6][0:TT, NT * H:2 * NT * H], ALU.mult))
            dve.tensor_tensor(by_tile(coef[:, :, 1]), by_tile(d), rq, ALU.mult)
            link(dve.tensor_tensor(by_tile(a), by_tile(b), sigh, ALU.add))
            link(dve.tensor_scalar(b, a, rt, -1.0, ALU.mult, ALU.mult))
            dve.tensor_tensor(by_tile(coef[:, :, 2]), by_tile(b), rq, ALU.mult).then_inc(coef_ready, 1)
            dve.wait_ge(coef_ready, 1)
            mask(1)
            expand_q(2)

            def combine(j):
                if j >= 2:
                    dve.wait_ge(att_ready, j - 1)
                for g in range(2):
                    dve.wait_ge(att_psum, 2 * j + g + 1)
                    n = G6 * 3
                    dve.tensor_tensor(mix[:, j % 2, g * n * DH:(g + 1) * n * DH].rearrange("p (h e) -> p h e", e=DH),
                                      bank[4 + g][0:TT, 0:n * DH].rearrange("p (h e) -> p h e", e=DH),
                                      coef[:, j * H + g * G6:j * H + (g + 1) * G6, :].rearrange("p h (c o) -> p (h c) o", o=1)
                                      .broadcast_to([TT, n, DH]), ALU.mult).then_inc(mix_ready, 1)

            def variance_o(j):
                dve.wait_ge(osq_ready, j + 1)
                link(dve.tensor_reduce(o_var[:, j % SMALL, 2 * H:3 * H], heads(o_sq[:, j % 2, :]), AX_X, ALU.add))
                dve.tensor_scalar(o_var[:, j % SMALL, 0:H], o_var[:, j % SMALL, 2 * H:3 * H], 1.0 / DH, EPS, ALU.mult, ALU.add)\
                    .then_inc(ovar_ready, 1)

            def normalise_o(j):
                dve.wait_ge(ostd_ready, j + 1)
                link(dve.reciprocal(o_var[:, j % SMALL, 2 * H:3 * H], o_var[:, j % SMALL, H:2 * H]))
                if j >= SMALL:
                    dve.wait_ge(oT_psum, j - SMALL + 1)
                dve.tensor_tensor(heads(o_n[:, j % SMALL, :]), heads(o_att[:, j % SMALL, :]),
                                  o_var[:, j % SMALL, 2 * H:3 * H].rearrange("p (h o) -> p h o", o=1)
                                  .broadcast_to([TT, H, DH]), ALU.mult).then_inc(on_ready, 1)

            def residual(j):
                dve.wait_ge(wo_done, j + 1)
                if j >= SMALL:
                    dve.wait_ge(h1_ready, j - SMALL + 1)
                dve.tensor_tensor(r1[:, j % SMALL, :], bank[7][0:TT, 0:D], h0[:, j, 0:D], ALU.add).then_inc(r1_ready, 1)
                dve.wait_ge(r1_ready, j + 1)
                link(dve.bn_stats(bn1[:, j % SMALL, :], r1[:, j % SMALL, :]))
                link(dve.bn_aggr(mv1[:, j % SMALL, 0:2], bn1[:, j % SMALL, :]))
                dve.tensor_scalar(mv1[:, j % SMALL, 1:2], mv1[:, j % SMALL, 1:2], EPS, None, ALU.add).then_inc(r1_var, 1)

            def normalise_r(j):
                dve.wait_ge(r1_std, j + 1)
                link(dve.reciprocal(mv1[:, j % SMALL, 3:4], mv1[:, j % SMALL, 2:3]))
                dve.tensor_scalar(h1[:, j, :], r1[:, j % SMALL, :], mv1[:, j % SMALL, 0:1], mv1[:, j % SMALL, 3:4],
                                  ALU.subtract, ALU.mult).then_inc(h1_ready, 1)

            def hidden_s(m):
                n, f = divmod(m, FSK)
                dve.wait_ge(silu_s_ready, m + 1)
                dve.tensor_tensor(hsT[:, f, n * HALF:(n + 1) * HALF], silu_s[:, m % 2, :], bank[3 + m % 2][:, 0:HALF],
                                  ALU.mult).then_inc(hs_ready, 1)

            for i in range(1, NT):
                if 3 <= i + 1 < NT:
                    expand_q(i + 1)
                if i >= 3:
                    normalise_o(i - 3)
                if i >= 5:
                    residual(i - 5)
                if i >= 6:
                    normalise_r(i - 6)
                if i >= 2:
                    mask(i)
                combine(i - 1)
                if i >= 2:
                    variance_o(i - 2)
            normalise_o(NT - 3)
            residual(NT - 5)
            normalise_r(NT - 6)
            variance_o(NT - 2)
            combine(NT - 1)
            normalise_r(NT - 5)
            normalise_o(NT - 2)
            residual(NT - 4)
            normalise_r(NT - 4)
            residual(NT - 3)
            variance_o(NT - 1)
            normalise_r(NT - 3)
            normalise_o(NT - 1)
            residual(NT - 2)
            normalise_r(NT - 2)
            residual(NT - 1)
            normalise_r(NT - 1)
            dve.wait_ge(logit_ready, 1)

            def left(n):
                return rank_in[0:48, n % 3, :]

            def find(n):
                eight = slice(8 * n, 8 * n + 8)
                return dve.max_index(top_idx[:, eight], top_val[:, eight], left(n))

            for n in range(ROUNDS):
                eight = slice(8 * n, 8 * n + 8)
                dve.max(top_val[:, eight], left(n)).then_inc(top_max, 1)
                if n >= 1:
                    find(n - 1)
                if n < ROUNDS - 1:
                    dve.wait_ge(top_max, n + 1)
                    dve.match_replace(left(n + 1), top_val[:, eight], left(n), -3e38).then_inc(top_left, 1)
                    if n >= 4 and n - 4 < 2 * FSK:
                        hidden_s(n - 4)
                    dve.wait_ge(top_left, n + 1)
            dve.wait_ge(top_max, ROUNDS)
            link(find(ROUNDS - 1))
            link(dve.tensor_copy(top_row[:, :], top_idx[:, 0:CAP]))
            dve.tensor_scalar(top_row[32:48, :], top_row[32:48, :], float(HALF), None, ALU.add).then_inc(top_ready, 1)
            dve.wait_ge(rev_psum, 1)
            va, ia = top_T[:, 0, 0:E], top_T[:, 1, 0:E]
            vb, ib = bank[2][0:CAP, 0:E], bank[2][0:CAP, E:2 * E]
            dve.tensor_tensor(pick[:, 0, :], va, vb, ALU.max).then_inc(pick_ready, 1)
            dve.tensor_tensor(pick[:, 1, :], va, vb, ALU.is_ge)
            link(dve.tensor_tensor(pick[:, 2, :], ia, ib, ALU.subtract))
            link(dve.tensor_tensor(pick[:, 3, :], pick[:, 2, :], pick[:, 1, :], ALU.mult))
            link(dve.tensor_tensor(pick[:, 4, :], pick[:, 3, :], ib, ALU.add))
            dve.tensor_copy(row_i[:, :], pick[:, 4, :]).then_inc(row_ready, 1)
            dve.wait_ge(score_ready, 1)

            def x_lower(e, k):
                dve.wait_ge(x_hi_ready, e + 1)
                dve.tensor_tensor(x_lo[:, k % 2, :], bank[6][0:KA, 0:2 * CAP], x_hi[:, k % 2, :].bitcast(F32),
                                  ALU.subtract).then_inc(x_lo_ready, 1)

            def split_lo(e, k, c):
                dve.wait_ge(w_hi_ready, e * NCH + c + 1)
                cols = slice(c * 2 * CH, (c + 1) * 2 * CH)
                dve.tensor_tensor(w_lo[:, k % 2, cols], wgu_sb[:, k % 2, cols],
                                  w_hi[:, k % 2, cols].bitcast(F32), ALU.subtract).then_inc(w_lo_ready, 1)
                dve.tensor_tensor(w_b[KB:2 * KB, k % 2, cols], wgu_b[:, k % 2, cols],
                                  w_b[0:KB, k % 2, cols].bitcast(F32), ALU.subtract).then_inc(w_lo_ready, 1)

            def gated(e, k, c):
                dve.wait_ge(silu_ready, e * NCH + c + 1)
                if c == 0 and known(e, 2):
                    dve.wait_ge(turn_b, e - 1)
                dve.tensor_tensor(hid[:, k % 2, c * CH:(c + 1) * CH], silu_g[:, c, :], bank[c][0:CAP, CH:2 * CH],
                                  ALU.mult).then_inc(h_ready, 1)

            def step(e, k):
                nxt = (k + 1) % RING
                if known(e, None, E - 1):
                    gated(e, k, 0)
                if known(e, None, E - 2):
                    x_lower(e + 1, nxt)
                    split_lo(e + 1, nxt, 0)
                if known(e, None, E - 1):
                    gated(e, k, 1)
                if known(e, None, E - 2):
                    split_lo(e + 1, nxt, 1)
                if known(e, 1):
                    dve.wait_ge(down_done, e)
                    if known(e, 3):
                        dve.wait_ge(y_add, 16 * (e - 2))
                    dve.tensor_scalar(o_exp[:, (k - 1) % 2, :], bank[5][0:CAP, 0:D], score[:, bass.ds(e - 1, 1)], None,
                                      ALU.mult).then_inc(out_ready, 1)
                if known(e, None, E - 1):
                    gated(e, k, 2)
                if known(e, None, E - 2):
                    split_lo(e + 1, nxt, 2)

            x_lower(0, 0)
            over_experts(dve, step)
            dve.wait_ge(y_in, 16)
            for t in range(NY):
                last = dve.bn_stats(bn2[:, t, :], y[:, t, :])
            link(last)
            for t in range(NY):
                last = dve.bn_aggr(mv2[:, t, :], bn2[:, t, :])
            link(last)
            dve.tensor_scalar(std2[:, 0, :], mv2[:, :, 1], EPS, None, ALU.add).then_inc(y_var, 1)
            dve.wait_ge(y_std, 1)
            link(dve.reciprocal(std2[:, 2, :], std2[:, 1, :]))
            for t in range(NY):
                dve.tensor_scalar(y_n[:, t, :], y[:, t, :], mv2[:, t, 0:1], std2[:, 2, t:t + 1],
                                  ALU.subtract, ALU.mult).then_inc(y_norm, 1)


def constants():
    import numpy as np
    c = np.zeros((128, C_N), np.float32)
    c[:, C_ID:C_ID + 128] = np.eye(128)
    m, l = np.arange(TT)[:, None], np.arange(TT)[None, :]
    c[:TT, C_TRI:C_TRI + TT] = (m // L == l // L) & (m <= l)
    c[:CAP, C_REV:C_REV + CAP] = np.eye(CAP)[::-1]
    pos = (np.arange(TT) % L).astype(np.float32)
    inv = (1.0 / 10000.0 ** (np.arange(0, DH, 2, dtype=np.float32) / DH)).astype(np.float32)
    ang = pos[:, None] * inv[None, :]
    c[:TT, C_COS:C_COS + DH] = np.repeat(np.cos(ang), 2, axis=-1)
    sin = np.repeat(np.sin(ang), 2, axis=-1)
    c[:TT, C_SIN:C_SIN + DH // 2] = -sin[:, :DH // 2]
    c[:TT, C_SIN + DH // 2:C_SIN + DH] = sin[:, DH // 2:]
    c[:DK, C_HM:C_HM + G6] = np.arange(DK)[:, None] // DH == np.arange(G6)[None, :]
    c[:TT, C_T] = pos + 1
    c[:TT, C_RT] = 1.0 / (pos + 1)
    c[0, C_ONE:C_ONE + 128] = 1.0
    return c


def layouts(i):
    import numpy as np

    def halves(w):
        return w.reshape(2, DK, -1).transpose(1, 0, 2)

    a = {}
    p = i["x"].reshape(IMAGES, 3, SIDE, PATCH, SIDE, PATCH).transpose(0, 2, 4, 3, 5, 1).reshape(NT, TT, KX, 128)
    a["x"] = p.transpose(0, 3, 2, 1).reshape(NT, 128, KX * TT)
    a["w_patch"] = i["L0_tok_W"].T.reshape(KX, 128, D).transpose(1, 0, 2).reshape(128, KX * D)
    wg = i["L0_attn_Wg"].reshape(H, 3, D)
    a["w_proj"] = np.concatenate([i["L0_attn_Wq"], i["L0_attn_Wk"], i["L0_attn_Wv"], i["L0_attn_Wu"],
                                         wg[:, 0], wg[:, 1]]).T
    a["w_o"] = halves(i["L0_attn_Wo"].T)
    row = np.concatenate([i["L0_tok_b"], i["L0_attn_prior_mu"].reshape(-1), i["L0_attn_prior_log_tau"].reshape(-1)])
    a["params"] = np.broadcast_to(row, (TT, P_N))
    a["consts"] = constants()
    gate = i["L0_ffn_gate_weight"]
    a["w_gate"] = halves(np.concatenate([gate, gate]).T)
    wgu = np.stack([i["L0_ffn_Wg"].reshape(E, NCH, CH, D), i["L0_ffn_Wu"].reshape(E, NCH, CH, D)], axis=2)
    a["w_gu"] = wgu.reshape(E, 2 * F, D).transpose(0, 2, 1)
    a["w_d"] = i["L0_ffn_Wd"].reshape(E, D, FK, 128).transpose(0, 3, 2, 1)
    a["ws_gu"] = halves(np.concatenate([i["L0_ffn_Ws_g"], i["L0_ffn_Ws_u"]]).T)
    a["ws_d"] = i["L0_ffn_Ws_d"].reshape(D, FSK, 128).transpose(2, 1, 0)
    return {k: np.ascontiguousarray(v) for k, v in a.items()}


def kernel(**inputs):
    import numpy as np
    from concourse import bacc
    from concourse.bass_utils import run_bass_kernel_spmd

    arrays = layouts({k: np.asarray(v) for k, v in inputs.items()})
    nc = bacc.Bacc("TRN2", target_bir_lowering=False, num_devices=1)
    args = [nc.dram_tensor(k, v.shape, mybir.dt.from_np(v.dtype), kind="ExternalInput").ap() for k, v in arrays.items()]
    out = nc.dram_tensor("out", (TOKENS, D), F32, kind="ExternalOutput").ap()
    build(nc, *args, out)
    r = run_bass_kernel_spmd(nc, [arrays], core_ids=[0])
    return r.results[0]["out"].reshape(IMAGES, L, D)
```

```python
from contextlib import ExitStack

import concourse.bass as bass
from concourse import mybir

ALU = mybir.AluOpType
ACT = mybir.ActivationFunctionType
AX_X = mybir.AxisListType.X
F32 = mybir.dt.float32
I32 = mybir.dt.int32
U32 = mybir.dt.uint32
F32R = mybir.dt.float32r

IMAGES, PATCH, SIDE = 16, 16, 7
L = SIDE * SIDE
TOKENS = IMAGES * L
PIX = 3 * PATCH * PATCH
D = 192
H, DH = 12, 16
TT = 2 * L
NT = TOKENS // TT
KX = PIX // 128
DK = D // 2
KA, KB = 128, D - 128
E = 16
CAP = -(-TOKENS * 2 // E)
F = 4 * D
FK = F // 128
FS = F // 2
FSK = FS // 128
HALF = TOKENS // 2
ROUNDS = -(-CAP // 8)
YT = 112
NY = TOKENS // YT
NY_DVE = 4
CH = 256
NCH = F // CH
G6 = 6
EPS = 1e-5
Y_BANKS = (0, 1, 2, 6, 7, 3, 4)
WP1 = KX // 2 * D
XRING = 4
RING = 4
SBUFS = 3
SMALL = 4

C_ID, C_TRI, C_REV = 0, 128, 128 + TT
C_COS = C_REV + CAP
C_SIN = C_COS + DH
C_HM = C_SIN + DH
C_T = C_HM + G6
C_RT = C_T + 1
C_N = C_RT + 1
P_B, P_TAU, P_N = 0, D, D + H
QK, VU = 2 * D, 2 * D + 2 * H


def build(nc, x, w_patch, w_proj, w_o, params, mu, consts, token_no, w_gate, w_gu, w_d, ws_gu, ws_d, out):
    h1_dram = nc.dram_tensor("h1_rows", (TOKENS, D + KB), F32, kind="Internal").ap()
    y_dram = nc.dram_tensor("y_rows", (TOKENS, D), F32, kind="Internal").ap()
    with ExitStack() as ctx:
        def sb(name, shape, dt=F32):
            return ctx.enter_context(nc.sbuf_tensor(name, shape, dt))

        def sem(name):
            return ctx.enter_context(nc.semaphore(name))

        bank = [ctx.enter_context(nc.psum_tensor(f"bank{i}", [128, 512], F32)) for i in range(8)]

        cst = sb("cst", [128, C_N])
        token_sb = sb("token_sb", [CAP, TOKENS])
        wgate_sb = sb("wgate_sb", [DK, 2, 2 * E])
        h1 = sb("h1", [TT, NT, D])
        h1T = sb("h1T", [DK, 2, TOKENS])
        wgu_sb = sb("wgu_sb", [KA, 2, 2 * F])
        wgu_b = sb("wgu_b", [KB, 2, 2 * F])
        wd_sb = sb("wd_sb", [128, RING, FK, D])
        wsgu_sb = sb("wsgu_sb", [DK, 2, 2 * FS])
        wsd_sb = sb("wsd_sb", [128, FSK, D])
        hsT = sb("hsT", [128, FSK, TOKENS])

        attention = ctx.enter_context(ExitStack())

        def sa(name, shape, dt=F32):
            return attention.enter_context(nc.sbuf_tensor(name, shape, dt))

        par = sa("par", [TT, P_N])
        wo_sb = sa("wo_sb", [DK, 2, D])
        h0 = sa("h0", [TT, NT, D + KB])
        qk = sa("qk", [TT, NT, QK])
        norm2 = sa("norm2", [TT, NT, 2 * H])
        rnorm = sa("rnorm", [TT, NT, 2 * H])
        vug = sa("vug", [TT, NT, VU])
        s_raw = sa("s_raw", [TT, NT, H])
        es_s = sa("es_s", [TT, 2, NT * H])
        tau = sa("tau", [TT, 3, H])
        mu_in = sa("mu_in", [1, D])
        mu_row = sa("mu_row", [1, D])
        ones = sa("ones", [1, TT])
        wv_mean = sa("wv_mean", [KA, 2, H])
        sT = sa("sT", [NT * H, 3, TT])
        s_max = sa("s_max", [NT * H, 2])
        gates = sa("gates", [TT, 3, NT, 2 * H])
        coef = sa("coef", [TT, NT * H, 3])
        vcoef = sa("vcoef", [TT, NT * H, 3])
        small = sa("small", [TT, 6, NT * H])

        projections = attention.enter_context(ExitStack())

        def sproj(name, shape, dt=F32):
            return projections.enter_context(nc.sbuf_tensor(name, shape, dt))

        x_sb = sproj("x_sb", [128, XRING, KX * TT])
        x_hi0 = sproj("x_hi0", [128, 2, KX * TT], F32R)
        x_lo0 = sproj("x_lo0", [128, 2, KX * TT], F32R)
        wp_sb = sproj("wp_sb", [128, KX * D])
        wp_hi = sproj("wp_hi", [128, KX * D], F32R)
        wp_lo = sproj("wp_lo", [128, KX * D], F32R)
        wproj_sb = sproj("wproj_sb", [KA, 2, QK + VU])
        wproj_hi = sproj("wproj_hi", [KA, QK + VU], F32R)
        wproj_lo = sproj("wproj_lo", [KA, QK + VU], F32R)
        wproj_b = sproj("wproj_b", [2 * KB, QK + VU], F32R)
        h0T_hi = sproj("h0T_hi", [KA, 2, 2 * TT], F32R)
        h0T_lo = sproj("h0T_lo", [KA, 2, 2 * TT], F32R)
        tri_r = sproj("tri_r", [TT, TT], F32R)
        ones_r = sproj("ones_r", [1, TT], F32R)
        mu_hi = sproj("mu_hi", [1, D], F32R)
        mu_lo = sproj("mu_lo", [1, D], F32R)
        u_hi = sproj("u_hi", [TT, 2, D], F32R)
        u_lo = sproj("u_lo", [TT, 2, D], F32R)
        rope_a = sproj("rope_a", [TT, 2, QK])
        rope_b = sproj("rope_b", [TT, 2, QK])
        squares = sproj("squares", [TT, 2, QK])
        u_bar = sproj("u_bar", [TT, 2, D])
        projections.close()

        v3 = sa("v3", [TT, 2, (H + 1) * 3 * DH])
        qkT = sa("qkT", [DK, 2, 4 * TT])
        q_exp = sa("q_exp", [DK, 2, 2, G6 * TT])
        pT = sa("pT", [TT, 2, H * TT])
        mix = sa("mix", [TT, 2, H * 3 * DH])
        o_sum = sa("o_sum", [TT, 2, D])
        o_att = sa("o_att", [TT, SMALL, D])
        o_sq = sa("o_sq", [TT, 2, D])
        o_var = sa("o_var", [TT, SMALL, 3 * H])
        o_n = sa("o_n", [TT, SMALL, D])
        oT = sa("oT", [DK, 2, 2 * TT])
        r1 = sa("r1", [TT, SMALL, D])
        bn1 = sa("bn1", [TT, SMALL, 6])
        mv1 = sa("mv1", [TT, SMALL, 4])
        attention.close()

        w_hi = sb("w_hi", [KA, 2, 2 * F], F32R)
        w_lo = sb("w_lo", [KA, 2, 2 * F], F32R)
        w_b = sb("w_b", [2 * KB, 2, 2 * F], F32R)
        silu_s = sb("silu_s", [128, SBUFS, HALF])
        up_s = sb("up_s", [128, SBUFS, HALF])
        rank_in = sb("rank_in", [64, 3, HALF])
        top_val = sb("top_val", [48, 8 * ROUNDS])
        top_idx = sb("top_idx", [48, 8 * ROUNDS], U32)
        top_row = sb("top_row", [48, CAP])
        top_T = sb("top_T", [CAP, 2, 48])
        pick = sb("pick", [CAP, 5, E])
        place = sb("place", [CAP, TOKENS])
        row_i = sb("row_i", [CAP, E], I32)
        score = sb("score", [CAP, E])
        xg = sb("xg", [CAP, RING, D + KB])
        x_hi = sb("x_hi", [KA, 2, 2 * CAP], F32R)
        x_lo = sb("x_lo", [KA, 2, 2 * CAP], F32R)
        silu_g = sb("silu_g", [CAP, NCH, CH])
        hid = sb("hid", [CAP, 2, F])
        hidT = sb("hidT", [128, FK, CAP])
        o_exp = sb("o_exp", [CAP, 2, D])
        y_base = sb("y_base", [TT, 2, NT, D])
        y = sb("y", [YT, NY, D])
        bn2 = sb("bn2", [YT, NY, 6])
        mv2 = sb("mv2", [YT, NY, 2])
        std2 = sb("std2", [YT, 4, NY])
        y_n = sb("y_n", [YT, NY, D])

        consts_in, wp_in, proj_in, rest_in = (sem(n) for n in ("consts_in", "wp_in", "proj_in", "rest_in"))
        x_in = [sem(f"x_in{j}") for j in range(NT)]
        h1_out = sem("h1_out")
        embed_done, h0_ready, h0T_psum, h0T_ready = (sem(n) for n in (
            "embed_done", "h0_ready", "h0T_psum", "h0T_ready"))
        qk_psum, vug_psum, qk_ready, qk_read, vug_ready, usum_done, s_ready, sq_ready, n2_ready = (sem(n) for n in (
            "qk_psum", "vug_psum", "qk_ready", "qk_read", "vug_ready", "usum_done", "s_ready", "sq_ready", "n2_ready"))
        tau_clip, tau_exp, tau_ready, wv_ready = (sem(n) for n in ("tau_clip", "tau_exp", "tau_ready", "wv_ready"))
        s_all, sT_psum, sT_sub, sT_exp, es_psum, es_ready, cum_done, coef_ready, gate_exp, norm_sqrt, vcoef_ready = (
            sem(n) for n in ("s_all", "sT_psum", "sT_sub", "sT_exp", "es_psum", "es_ready", "cum_done",
                             "coef_ready", "gate_exp", "norm_sqrt", "vcoef_ready"))
        qkT_psum, qkT_ready, q_exp_ready, score_done, p_ready, v3_ready, att_psum, mix_ready = (
            sem(n) for n in ("qkT_psum", "qkT_ready", "q_exp_ready", "score_done", "p_ready", "v3_ready",
                             "att_psum", "mix_ready"))
        att_ready, osq_ready, ovar_ready, ostd_ready, on_ready, oT_psum, oT_ready, wo_done = (sem(n) for n in (
            "att_ready", "osq_ready", "ovar_ready", "ostd_ready", "on_ready", "oT_psum", "oT_ready", "wo_done"))
        r1_var, r1_std, r1_ready, h1_ready, h1T_psum, h1T_ready = (sem(n) for n in (
            "r1_var", "r1_std", "r1_ready", "h1_ready", "h1T_psum", "h1T_ready"))
        wo_in, wproj_hi_ready, wproj_lo_ready, h0T_hi_ready, q_exp_pool, v3_zero = (sem(n) for n in (
            "wo_in", "wproj_hi_ready", "wproj_lo_ready", "h0T_hi_ready", "q_exp_pool", "v3_zero"))
        ws_in, wp2_in, ones_ready = sem("ws_in"), sem("wp2_in"), sem("ones_ready")
        x_hi_made, x_lo_made, wp_hi_ready, wp_lo_ready, tri_ready, mu_hi_ready, mu_lo_ready, u_hi_ready, u_lo_ready = (
            sem(n) for n in ("x_hi_made", "x_lo_made", "wp_hi_ready", "wp_lo_ready", "tri_ready", "mu_hi_ready",
                             "mu_lo_ready", "u_hi_ready", "u_lo_ready"))
        norm_ready, gate_ready = sem("norm_ready"), sem("gate_ready")
        top_max, top_left, up_s_ready = sem("top_max"), sem("top_left"), sem("up_s_ready")
        wgu_in = [sem(f"wgu_in{n}") for n in range(2)]
        wd_in = [sem(f"wd_in{n}") for n in range(RING)]
        xg_in = [sem(f"xg_in{n}") for n in range(RING)]
        logit_psum, logit_ready, shared_gu, silu_s_ready, hs_ready, top_ready, top_psum, topT_ready, rev_psum = (
            sem(n) for n in ("logit_psum", "logit_ready", "shared_gu", "silu_s_ready", "hs_ready", "top_ready",
                             "top_psum", "topT_ready", "rev_psum"))
        pick_ready, row_ready, score_ready, shared_y, base_ready, base_added, base_out, y_add, y_in = (
            sem(n) for n in ("pick_ready", "row_ready", "score_ready", "shared_y", "base_ready", "base_added",
                             "base_out", "y_add", "y_in"))
        x_psum, x_hi_ready, x_lo_ready, w_hi_ready, w_lo_ready, w_lo0_ready = (sem(n) for n in (
            "x_psum", "x_hi_ready", "x_lo_ready", "w_hi_ready", "w_lo_ready", "w_lo0_ready"))
        gu_done, silu_ready, h_ready, turn_a, turn_b, turned_a, turned_b, down_done, out_ready = (
            sem(n) for n in ("gu_done", "silu_ready", "h_ready", "turn_a", "turn_b", "turned_a", "turned_b",
                             "down_done", "out_ready"))
        tokens_in, hs_last, place_ready, last_psum, y_sum = (sem(n) for n in (
            "tokens_in", "hs_last", "place_ready", "last_psum", "y_sum"))
        y_var, y_std, y_rstd, y_norm, y_norm_act, y_out = (sem(n) for n in (
            "y_var", "y_std", "y_rstd", "y_norm", "y_norm_act", "y_out"))
        v_order, p_order = sem("v_order"), sem("p_order")

        ident = cst[:, C_ID:C_ID + 128]
        tri = cst[0:TT, C_TRI:C_TRI + TT]
        rev = cst[0:CAP, C_REV:C_REV + CAP]

        def heads(ap, n=H):
            return ap.rearrange("p (h e) -> p h e", h=n)

        def spread_q(eng, j, g):
            eng.wait_ge(qkT_ready, j + 1)
            if j >= 2:
                eng.wait_ge(score_done, 3 * (j - 1))
            return eng.tensor_tensor(q_exp[:, j % 2, g, :].rearrange("p (h t) -> p h t", h=G6),
                                     qkT[:, j % 2, g * TT:(g + 1) * TT].rearrange("p (o t) -> p o t", o=1)
                                     .broadcast_to([DK, G6, TT]),
                                     cst[0:DK, C_HM:C_HM + G6].rearrange("p (h o) -> p h o", o=1)
                                     .broadcast_to([DK, G6, TT]), ALU.mult)

        def over_experts(eng, step):
            for e in range(RING - 1):
                step(e, e)
            with eng.Fori(0, E // RING - 1) as i:
                for k in range(RING - 1, 2 * RING - 1):
                    step(i * RING + k, k % RING)
            for e in range(E - 1, E + 1):
                step(e, e % RING)

        def known(e, least=None, most=None):
            return not isinstance(e, int) or ((least is None or e >= least) and (most is None or e <= most))

        block = ctx.enter_context(nc.Block())

        @block.sync
        def _(sp):
            sp.dma_start(wp_sb[:, 0:WP1], w_patch[:, 0:WP1]).then_inc(wp_in, 16)
            sp.dma_start(wp_sb[:, WP1:], w_patch[:, WP1:]).then_inc(wp2_in, 16)
            for j in range(1, NT):
                if j >= XRING:
                    sp.wait_ge(x_lo_made, j - XRING)
                    if j == XRING:
                        sp.wait_ge(embed_done, 1)
                sp.dma_start(x_sb[:, j % XRING, :], x[j]).then_inc(x_in[j], 16)
                if j == 1:
                    sp.dma_start(wproj_sb[:, 0, :], w_proj[0:KA, :]).then_inc(proj_in, 16)
                    sp.dma_start(wproj_sb[0:KB, 1, :], w_proj[KA:D, :]).then_inc(proj_in, 16)
            sp.dma_start(wo_sb[:, :, :], w_o).then_inc(wo_in, 16)
            sp.dma_start(wgate_sb[:, :, :], w_gate).then_inc(rest_in, 16)
            sp.dma_start(wsgu_sb[:, :, :], ws_gu).then_inc(ws_in, 16)
            sp.dma_start(wsd_sb[:, :, :], ws_d).then_inc(ws_in, 16)
            sp.dma_start(token_sb[:, :], token_no).then_inc(tokens_in, 16)
            for e in range(2):
                sp.dma_start(wgu_sb[:, e, :], w_gu[e, 0:KA, :]).then_inc(wgu_in[e], 16)
                sp.dma_start(wgu_b[:, e, :], w_gu[e, KA:D, :]).then_inc(wgu_in[e], 16)
            for e in range(RING):
                sp.dma_start(wd_sb[:, e, :, :], w_d[e]).then_inc(wd_in[e], 16)
            for j in range(NT):
                sp.wait_ge(h1_ready, j + 1)
                sp.dma_start(h1_dram[j * TT:(j + 1) * TT, 0:D], h1[:, j, :]).then_inc(h1_out, 16)
                sp.dma_start(h1_dram[j * TT:(j + 1) * TT, D:D + KB], h1[:, j, KA:D]).then_inc(h1_out, 16)
            sp.wait_ge(w_lo0_ready, 2 * NCH)
            sp.dma_start(wgu_sb[:, 0, :], w_gu[2, 0:KA, :]).then_inc(wgu_in[0], 16)
            sp.dma_start(wgu_b[:, 0, :], w_gu[2, KA:D, :]).then_inc(wgu_in[0], 16)
            sp.wait_ge(base_added, 1)
            sp.dma_start(y_dram.rearrange("(j p) d -> p j d", j=NT), y_base[:, 1, :, :]).then_inc(base_out, 16)

            def load_gu(e, k):
                sp.wait_ge(w_lo_ready, (e - 2) * 2 * NCH)
                sp.dma_start(wgu_sb[:, k % 2, :], w_gu[e, 0:KA, :] if isinstance(e, int) else
                             w_gu[bass.ds(e, 1), 0:KA, :].rearrange("o p n -> (o p) n")).then_inc(wgu_in[k % 2], 16)
                sp.dma_start(wgu_b[:, k % 2, :], w_gu[e, KA:D, :] if isinstance(e, int) else
                             w_gu[bass.ds(e, 1), KA:D, :].rearrange("o p n -> (o p) n")).then_inc(wgu_in[k % 2], 16)

            def load_d(e, k):
                sp.wait_ge(down_done, e - RING + 1)
                sp.dma_start(wd_sb[:, k, :, :], w_d[e]).then_inc(wd_in[k], 16)

            load_gu(3, 3)
            with sp.Fori(0, E // RING - 1) as i:
                for k in range(RING):
                    load_gu(i * RING + RING + k, k)
                    load_d(i * RING + RING + k, k)
            sp.wait_ge(y_add, 16 * (E - 1))
            sp.dma_start(y[:, :, :], y_dram.rearrange("(p t) d -> p t d", t=NY)).then_inc(y_in, 16)
            out_rows = out.rearrange("(p t) d -> p t d", t=NY)
            for part, done in ((slice(0, NY_DVE), y_norm), (slice(NY_DVE, NY), y_norm_act)):
                sp.wait_ge(done, part.stop - part.start)
                sp.dma_start(out_rows[:, part, :], y_n[:, part, :]).then_inc(y_out, 16)
            sp.wait_ge(y_out, 32)

        @block.tensor
        def _(pe):
            def embed(j):
                if j == 0:
                    pe.wait_ge(x_in[0], 16)
                    parts = [(x_sb, wp_sb)]
                else:
                    pe.wait_ge(x_lo_made, j)
                    parts = [(x_hi0, wp_hi), (x_lo0, wp_hi), (x_hi0, wp_lo)]
                if j == 1:
                    pe.wait_ge(wp_lo_ready, 2)
                if j >= 2:
                    pe.wait_ge(h0_ready, 2 * (j - 1))
                for m, (x_part, w_part) in enumerate(parts):
                    for c in range(KX):
                        if j == 0 and c == KX // 2:
                            pe.wait_ge(wp2_in, 16)
                        last = pe.matmul(bank[j % 2][0:TT, 0:D], x_part[:, j % 2, c * TT:(c + 1) * TT],
                                         w_part[:, c * D:(c + 1) * D], start=(m == 0 and c == 0),
                                         stop=(m == len(parts) - 1 and c == KX - 1))
                last.then_inc(embed_done, 1)

            def turn_h0(j):
                pe.wait_ge(h0_ready, 2 * (j + 1))
                if j >= 1:
                    pe.wait_ge(h0T_ready, j)
                for c in range(2):
                    last = pe.transpose(bank[2][0:KA, c * TT:(c + 1) * TT], h0[:, j, c * KA:(c + 1) * KA],
                                        ident[0:TT, 0:TT])
                last.then_inc(h0T_psum, 1)

            def project(j):
                pe.wait_ge(h0T_ready, j + 1)
                if j >= 2:
                    pe.wait_ge(qk_read, j - 1)
                    pe.wait_ge(u_hi_ready, j - 1)
                for b, c0, n, done in ((3, 0, QK, qk_psum), (4, QK, VU, vug_psum)):
                    b += 3 * (j % 2)
                    parts = ((h0T_hi, 0, wproj_hi), (h0T_lo, 0, wproj_hi), (h0T_hi, TT, wproj_b),
                             (h0T_lo, TT, wproj_b), (h0T_hi, 0, wproj_lo))
                    for m, (x, x0, w) in enumerate(parts):
                        last = pe.matmul(bank[b][0:TT, 0:n], x[:, j % 2, x0:x0 + TT], w[:, c0:c0 + n],
                                         start=(m == 0), stop=(m == len(parts) - 1))
                    last.then_inc(done, 1)

            def sum_u(j):
                pe.wait_ge(u_lo_ready, j + 1)
                if j >= 1:
                    pe.wait_ge(s_ready, j)
                pe.matmul(bank[5][0:TT, 0:D], tri_r[:, :], u_hi[:, j % 2, :], start=True, stop=False)
                pe.matmul(bank[5][0:TT, 0:D], tri_r[:, :], u_lo[:, j % 2, :], start=False, stop=False)
                pe.matmul(bank[5][0:TT, 0:D], ones_r[:, :], mu_hi[:, :], start=False, stop=False)
                pe.matmul(bank[5][0:TT, 0:D], ones_r[:, :], mu_lo[:, :], start=False, stop=True).then_inc(usum_done, 1)

            pe.wait_ge(wp_in, 16)
            embed(0)
            embed(1)
            pe.wait_ge(consts_in, 48)
            turn_h0(0)
            for j in range(NT):
                if j + 2 < NT:
                    embed(j + 2)
                if j + 1 < NT:
                    turn_h0(j + 1)
                if j == 0:
                    pe.wait_ge(wproj_lo_ready, 2)
                project(j)
                if j == 0:
                    pe.wait_ge(tri_ready, 1)
                    pe.wait_ge(mu_lo_ready, 1)
                if j >= 1:
                    sum_u(j - 1)
            sum_u(NT - 1)

            def turn_qk(j):
                if j < 1:
                    pe.wait_ge(qk_read, NT)
                pe.wait_ge(qk_ready, j + 1)
                if j >= 1:
                    pe.wait_ge(qkT_ready, j)
                for c in range(4):
                    last = pe.transpose(bank[3][0:DK, c * TT:(c + 1) * TT], qk[:, j, c * DK:(c + 1) * DK],
                                        ident[0:TT, 0:TT])
                last.then_inc(qkT_psum, 1)

            def scores(j):
                pe.wait_ge(qkT_ready, j + 1)
                if j == 0:
                    pe.wait_ge(h0_ready, 2 * NT)
                    pe.wait_ge(h0T_ready, NT)
                for g, heads_of in enumerate((((0, 0, 4),), ((0, 4, 6), (1, 0, 2)), ((1, 2, 6),))):
                    if j >= 1:
                        pe.wait_ge(p_ready, 3 * (j - 1) + g + 1)
                    at = 0
                    for rows, first, end in heads_of:
                        pe.wait_ge((q_exp_ready, q_exp_pool)[rows], j + 1)
                        n = (end - first) * TT
                        last = pe.matmul(bank[g][0:TT, at:at + n], qkT[:, j % 2, (2 + rows) * TT:(3 + rows) * TT],
                                         q_exp[:, j % 2, rows, first * TT:end * TT], start=True, stop=True)
                        at += n
                    last.then_inc(score_done, 1)

            def attend(j):
                pe.wait_ge(p_ready, 3 * (j + 1))
                pe.wait_ge(v3_ready, j + 1)
                if j == 0:
                    pe.wait_ge(v3_zero, 1)
                    pe.wait_ge(s_ready, NT)
                if j >= 1:
                    pe.wait_ge(mix_ready, 2 * j)
                for h in range(H):
                    at = (h % G6) * 3 * DH
                    last = pe.matmul(bank[4 + h // G6][0:TT, at:at + 6 * DH],
                                     pT[:, j % 2, h * TT:(h + 1) * TT], v3[:, j % 2, h * 3 * DH:(h + 2) * 3 * DH],
                                     start=True, stop=True)
                    if h % G6 == G6 - 1:
                        last.then_inc(att_psum, 1)

            def turn_o(j):
                pe.wait_ge(on_ready, j + 1)
                if j >= 1:
                    pe.wait_ge(oT_ready, j)
                for c in range(2):
                    last = pe.transpose(bank[6][0:DK, c * TT:(c + 1) * TT], o_n[:, j % SMALL, c * DK:(c + 1) * DK],
                                        ident[0:TT, 0:TT])
                last.then_inc(oT_psum, 1)

            def project_o(j):
                pe.wait_ge(oT_ready, j + 1)
                if j >= 1:
                    pe.wait_ge(r1_ready, j)
                for c in range(2):
                    last = pe.matmul(bank[7][0:TT, 0:D], oT[:, j % 2, c * TT:(c + 1) * TT], wo_sb[:, c, :],
                                     start=(c == 0), stop=(c == 1))
                last.then_inc(wo_done, 1)

            def turn_h1(j):
                pe.wait_ge(h1_ready, j + 1)
                if j == 0:
                    pe.wait_ge(p_ready, 3 * NT)
                if j >= 2:
                    pe.wait_ge(h1T_ready, j - 1)
                for c in range(2):
                    last = pe.transpose(bank[1 + j % 2][0:DK, c * TT:(c + 1) * TT], h1[:, j, c * DK:(c + 1) * DK],
                                        ident[0:TT, 0:TT])
                last.then_inc(h1T_psum, 1)

            def logits(j):
                pe.wait_ge(h1T_ready, j + 1)
                if j == 0:
                    pe.wait_ge(mix_ready, 2 * NT)
                half, at = divmod(j * TT, HALF)
                for c in range(2):
                    last = pe.matmul(bank[5][32 * half:32 * half + 32, at:at + TT], wgate_sb[:, c, :],
                                     h1T[:, c, j * TT:(j + 1) * TT], start=(c == 0), stop=(c == 1))
                last.then_inc(logit_psum, 1)

            def shared_part(m, part, c):
                n, f = divmod(m, FSK)
                f0 = part * FS + f * 128
                return pe.matmul(bank[3 * part + m % 2][:, 0:HALF], wsgu_sb[:, c, f0:f0 + 128],
                                 h1T[:, c, n * HALF:(n + 1) * HALF], start=(c == 0), stop=(c == 1))

            def shared(m):
                if m == 1:
                    pe.wait_ge(h1T_ready, NT)
                if m >= 2:
                    pe.wait_ge(up_s_ready, m - 1)
                if m >= 1:
                    shared_part(m, 0, 0)
                    shared_part(m, 0, 1)
                shared_part(m, 1, 0)
                shared_part(m, 1, 1).then_inc(shared_gu, 1)

            def shared_down(j):
                pe.wait_ge(hs_ready, FSK if j < NT // 2 else 2 * FSK - 1)
                if j >= NT // 2:
                    pe.wait_ge(hs_last, 1)
                if j >= 2:
                    pe.wait_ge(base_ready, j - 1)
                for f in range(FSK):
                    last = pe.matmul(bank[6 + j % 2][0:TT, 0:D], hsT[:, f, j * TT:(j + 1) * TT], wsd_sb[:, f, :],
                                     start=(f == 0), stop=(f == FSK - 1))
                last.then_inc(shared_y, 1)

            turn_qk(0)
            pe.wait_ge(s_all, 1)
            pe.transpose(bank[5][0:NT * H, 0:TT], es_s[:, 1, :], ident[0:TT, 0:TT]).then_inc(sT_psum, 1)
            turn_qk(1)
            pe.wait_ge(sT_exp, 1)
            pe.transpose(bank[7][0:TT, 0:NT * H], sT[:, 2, :], ident[0:NT * H, 0:NT * H]).then_inc(es_psum, 1)
            scores(0)
            pe.wait_ge(es_ready, 1)
            pe.matmul(bank[6][0:TT, 0:2 * NT * H], tri, es_s[:, :, :].rearrange("p a b -> p (a b)"),
                      start=True, stop=True).then_inc(cum_done, 1)
            scores(1)
            turn_qk(2)
            pe.wait_ge(wo_in, 16)
            for i in range(1, NT):
                if i >= 2:
                    scores(i)
                attend(i - 1)
                if 3 <= i + 2 < NT:
                    turn_qk(i + 2)
                if i >= 3:
                    if i == 3:
                        pe.wait_ge(coef_ready, 1)
                    turn_o(i - 3)
                if i >= 4:
                    project_o(i - 4)
            attend(NT - 1)
            turn_h1(0)
            turn_o(NT - 3)
            project_o(NT - 4)
            turn_h1(1)
            pe.wait_ge(rest_in, 16)
            logits(0)
            project_o(NT - 3)
            turn_o(NT - 2)
            turn_h1(2)
            logits(1)
            project_o(NT - 2)
            turn_h1(3)
            logits(2)
            turn_o(NT - 1)
            turn_h1(NT - 4)
            logits(3)
            project_o(NT - 1)
            turn_h1(NT - 3)
            logits(NT - 4)
            pe.wait_ge(ws_in, 32)
            shared_part(0, 0, 0)
            logits(NT - 3)
            turn_h1(NT - 2)
            turn_h1(NT - 1)
            logits(NT - 2)
            logits(NT - 1)
            shared_part(0, 0, 1)
            for m in range(2 * FSK - 2):
                shared(m)
            shared_down(0)
            shared_down(1)
            shared(2 * FSK - 2)
            shared_down(2)
            shared_down(3)
            shared(2 * FSK - 1)
            pe.wait_ge(top_ready, 1)
            pe.transpose(bank[5][0:CAP, 0:48], top_val[:, 0:CAP], ident[0:48, 0:48])
            pe.transpose(bank[5][0:CAP, 48:96], top_row[:, :], ident[0:48, 0:48]).then_inc(top_psum, 1)
            pe.wait_ge(topT_ready, 1)
            pe.matmul(bank[2][0:CAP, 0:2 * E], rev, top_T[:, :, 32:48], start=True, stop=True).then_inc(rev_psum, 1)
            for j in range(NT // 2, NT - 1):
                shared_down(j)

            def turn_x(e, k):
                pe.wait_ge(xg_in[k], (e - k) * (16 // RING) + 16)
                if known(e, 1):
                    pe.wait_ge(x_lo_ready, e)
                for c in range(2):
                    last = pe.transpose(bank[6][0:KA, c * CAP:(c + 1) * CAP], xg[:, k, c * KA:(c + 1) * KA],
                                        ident[0:CAP, 0:CAP])
                last.then_inc(x_psum, 1)

            def gate_up(e, k, c):
                if known(e, 1):
                    pe.wait_ge(h_ready, e * NCH - NCH + c + 1)
                    pe.wait_ge(w_lo_ready, (e * NCH - NCH + c + 1) * 2)
                parts = ((x_hi, 0, w_hi), (x_hi, 0, w_lo), (x_lo, 0, w_hi), (x_hi, CAP, w_b), (x_lo, CAP, w_b))
                for m, (x, x0, w) in enumerate(parts):
                    last = pe.matmul(bank[c][0:CAP, 0:2 * CH], x[:, k % 2, x0:x0 + CAP],
                                     w[:, k % 2, c * 2 * CH:(c + 1) * 2 * CH],
                                     start=(m == 0), stop=(m == len(parts) - 1))
                last.then_inc(gu_done, 1)

            def turn_hidden(e, k, tiles, b, done):
                for n, c in enumerate(tiles):
                    last = pe.transpose(bank[b][:, n * CAP:(n + 1) * CAP], hid[:, k % 2, c * 128:(c + 1) * 128],
                                        ident[0:CAP, 0:CAP])
                last.then_inc(done, 1)

            def step(e, k):
                last_k = (k - 1) % RING
                if known(e, None, E - 1):
                    pe.wait_ge(x_lo_ready, e + 1)
                    gate_up(e, k, 0)
                if known(e, None, E - 2):
                    turn_x(e + 1, (k + 1) % RING)
                if known(e, 1):
                    pe.wait_ge(h_ready, e * NCH)
                    turn_hidden(e - 1, last_k, range(4, FK), 4, turn_b)
                if known(e, None, E - 1):
                    gate_up(e, k, 1)
                if known(e, 1):
                    pe.wait_ge(wd_in[last_k], (e - 1 - last_k) * (16 // RING) + 16)
                    pe.wait_ge(turned_a, e)
                    pe.wait_ge(turned_b, e)
                    if known(e, 2):
                        pe.wait_ge(out_ready, e - 1)
                    for c in range(FK):
                        last = pe.matmul(bank[5][0:CAP, 0:D], hidT[:, c, :], wd_sb[:, last_k, c, :],
                                         start=(c == 0), stop=(c == FK - 1))
                    last.then_inc(down_done, 1)
                if known(e, None, E - 1):
                    gate_up(e, k, 2)
                    pe.wait_ge(h_ready, e * NCH + 2)
                    turn_hidden(e, k, range(4), 3, turn_a)

            pe.wait_ge(base_ready, NT - 1)
            turn_x(0, 0)
            shared_down(NT - 1)
            pe.wait_ge(w_lo0_ready, 2 * NCH)
            pe.wait_ge(row_ready, 1)
            over_experts(pe, step)
            pe.wait_ge(place_ready, 1)
            pe.wait_ge(out_ready, E)
            pe.wait_ge(base_ready, NT)
            for t in range(NY):
                pe.matmul(bank[Y_BANKS[t]][0:YT, 0:D], place[:, t * YT:(t + 1) * YT], o_exp[:, (E - 1) % 2, :],
                          start=True, stop=True).then_inc(last_psum, 1)

        @block.scalar
        def _(act):
            act.dma_start(x_sb[:, 0, :], x[0]).then_inc(x_in[0], 16)
            act.dma_start(cst[:, :], consts).then_inc(consts_in, 16)
            act.dma_start(par[:, :], params).then_inc(consts_in, 16)
            act.dma_start(mu_in[:, :], mu).then_inc(consts_in, 16)

            def copy_qkT(j):
                act.wait_ge(qkT_psum, j + 1)
                if j >= 2:
                    act.wait_ge(score_done, 3 * (j - 1))
                act.copy(qkT[:, j % 2, :], bank[3][0:DK, 0:4 * TT]).then_inc(qkT_ready, 1)

            def upper_h0T(j):
                act.wait_ge(h0T_psum, j + 1)
                if j >= 2:
                    act.wait_ge(vug_psum, j - 1)
                act.copy(h0T_hi[:, j % 2, :], bank[2][0:KA, 0:2 * TT]).then_inc(h0T_hi_ready, 1)

            def upper_x(j):
                act.wait_ge(x_in[j], 16)
                if j >= 3:
                    act.wait_ge(embed_done, j - 1)
                act.copy(x_hi0[:, j % 2, :], x_sb[:, j % XRING, :]).then_inc(x_hi_made, 1)

            def projected(j):
                act.wait_ge(vug_psum, j + 1)
                act.copy(vug[:, j, :], bank[4 + 3 * (j % 2)][0:TT, 0:VU]).then_inc(vug_ready, 1)
                if j >= 2:
                    act.wait_ge(usum_done, j - 1)
                act.copy(u_hi[:, j % 2, :], bank[4 + 3 * (j % 2)][0:TT, D:2 * D]).then_inc(u_hi_ready, 1)
                act.wait_ge(qk_ready, j + 1)
                if j >= 2:
                    act.wait_ge(n2_ready, j - 1)
                act.activation(squares[:, j % 2, :], qk[:, j, :], ACT.Square).then_inc(sq_ready, 1)

            def root_norm(j):
                act.wait_ge(n2_ready, j + 1)
                act.activation(rnorm[:, j, :], norm2[:, j, :], ACT.Sqrt).then_inc(norm_sqrt, 1)

            act.wait_ge(wp_in, 16)
            act.copy(wp_hi[:, 0:WP1], wp_sb[:, 0:WP1]).then_inc(wp_hi_ready, 1)
            act.wait_ge(wp2_in, 16)
            act.copy(wp_hi[:, WP1:], wp_sb[:, WP1:]).then_inc(wp_hi_ready, 1)
            upper_x(1)
            act.wait_ge(tau_clip, 1)
            act.activation(tau[:, 1, :], tau[:, 0, :], ACT.Exp).then_inc(tau_exp, 1)
            upper_x(2)
            act.wait_ge(wv_ready, 2)
            act.copy(wproj_hi[:, :], wproj_sb[:, 0, :])
            act.copy(wproj_b[0:KB, :], wproj_sb[0:KB, 1, :]).then_inc(wproj_hi_ready, 1)
            act.copy(tri_r[:, :], tri)
            act.wait_ge(ones_ready, 1)
            act.copy(ones_r[:, :], ones[:, :]).then_inc(tri_ready, 1)
            act.wait_ge(tau_ready, 2)
            act.copy(mu_hi[:, :], mu_row[:, :]).then_inc(mu_hi_ready, 1)
            for j in range(NT):
                upper_h0T(j)
                if j + 3 < NT:
                    upper_x(j + 3)
                if j >= 1:
                    projected(j - 1)
                if j >= 2:
                    root_norm(j - 2)
            projected(NT - 1)
            root_norm(NT - 2)
            root_norm(NT - 1)
            act.wait_ge(qk_ready, NT)
            act.wait_ge(n2_ready, NT)
            act.wait_ge(s_ready, NT)
            copy_qkT(0)
            act.wait_ge(vug_ready, NT)
            act.activation(gates[:, 0, :, :], vug[:, :, 2 * D:VU], ACT.Exp, scale=-1.0).then_inc(gate_exp, 1)
            act.wait_ge(sT_sub, 1)
            act.activation(sT[:, 2, :], sT[:, 1, :], ACT.Exp).then_inc(sT_exp, 1)
            copy_qkT(1)

            def square_o(j):
                act.wait_ge(att_ready, j + 1)
                if j >= 2:
                    act.wait_ge(ovar_ready, j - 1)
                act.activation(o_sq[:, j % 2, :], o_att[:, j % SMALL, :], ACT.Square).then_inc(osq_ready, 1)

            def root_o(j):
                act.wait_ge(ovar_ready, j + 1)
                act.activation(o_var[:, j % SMALL, H:2 * H], o_var[:, j % SMALL, 0:H], ACT.Sqrt).then_inc(ostd_ready, 1)

            def copy_oT(j):
                act.wait_ge(oT_psum, j + 1)
                if j >= 2:
                    act.wait_ge(wo_done, j - 1)
                act.copy(oT[:, j % 2, :], bank[6][0:DK, 0:2 * TT]).then_inc(oT_ready, 1)

            def root_r(j):
                act.wait_ge(r1_var, j + 1)
                act.activation(mv1[:, j % SMALL, 2:3], mv1[:, j % SMALL, 1:2], ACT.Sqrt).then_inc(r1_std, 1)

            def copy_h1T(j):
                act.wait_ge(h1T_psum, j + 1)
                act.copy(h1T[:, :, j * TT:(j + 1) * TT],
                         bank[1 + j % 2][0:DK, 0:2 * TT].rearrange("p (c t) -> p c t", c=2)).then_inc(h1T_ready, 1)

            def silu_shared(m):
                act.wait_ge(shared_gu, m + 1)
                if m >= SBUFS:
                    act.wait_ge(hs_ready, m - SBUFS + 1)
                act.activation(silu_s[:, m % SBUFS, :], bank[m % 2][:, 0:HALF], ACT.Silu).then_inc(silu_s_ready, 1)
                act.copy(up_s[:, m % SBUFS, :], bank[3 + m % 2][:, 0:HALF]).then_inc(up_s_ready, 1)

            copy_qkT(2)
            for i in range(1, NT):
                if 3 <= i + 2 < NT:
                    copy_qkT(i + 2)
                if i >= 3:
                    copy_oT(i - 3)
                if i >= 5:
                    root_r(i - 5)
                if i >= 2:
                    root_o(i - 2)
                square_o(i - 1)
            copy_h1T(0)
            copy_oT(NT - 3)
            copy_h1T(1)
            root_r(NT - 5)
            root_o(NT - 2)
            root_r(NT - 4)
            square_o(NT - 1)
            copy_oT(NT - 2)
            copy_h1T(2)
            root_o(NT - 1)
            root_r(NT - 3)
            copy_h1T(3)
            copy_oT(NT - 1)
            copy_h1T(NT - 4)
            root_r(NT - 2)
            copy_h1T(NT - 3)
            root_r(NT - 1)
            copy_h1T(NT - 2)
            copy_h1T(NT - 1)
            act.wait_ge(logit_psum, NT)
            act.copy(rank_in[:, 0, :], bank[5][0:64, 0:HALF]).then_inc(logit_ready, 1)

            def split_hi(e, k, c):
                if known(e, 2):
                    act.wait_ge(gu_done, (e - 2) * NCH + c + 1)
                cols = slice(c * 2 * CH, (c + 1) * 2 * CH)
                act.copy(w_hi[:, k % 2, cols], wgu_sb[:, k % 2, cols])
                act.copy(w_b[0:KB, k % 2, cols], wgu_b[:, k % 2, cols]).then_inc(w_hi_ready, 1)

            def copy_base(j):
                act.wait_ge(shared_y, j + 1)
                act.copy(y_base[:, 0, j, :], bank[6 + j % 2][0:TT, 0:D]).then_inc(base_ready, 1)

            act.wait_ge(wgu_in[0], 32)
            for m in range(2 * FSK):
                silu_shared(m)
                if m < NCH:
                    split_hi(0, 0, m)
                elif m < 2 * FSK - 1:
                    if m == NCH:
                        act.wait_ge(wgu_in[1], 32)
                        split_hi(1, 1, 0)
                    copy_base(2 * (m - NCH))
                    copy_base(2 * (m - NCH) + 1)
            act.wait_ge(top_psum, 1)
            act.copy(top_T[:, :, :].rearrange("p a b -> p (a b)"), bank[5][0:CAP, 0:96]).then_inc(topT_ready, 1)
            act.wait_ge(pick_ready, 1)
            act.activation(score[:, :], pick[:, 0, :], ACT.Sigmoid).then_inc(score_ready, 1)
            for j in range(NT // 2, NT - 1):
                if j + 1 - NT // 2 < NCH:
                    split_hi(1, 1, j + 1 - NT // 2)
                copy_base(j)

            def x_upper(e, k):
                act.wait_ge(x_psum, e + 1)
                if known(e, 2):
                    act.wait_ge(gu_done, (e - 1) * NCH)
                act.copy(x_hi[:, k % 2, :], bank[6][0:KA, 0:2 * CAP]).then_inc(x_hi_ready, 1)

            def silu_gate(e, k, c):
                act.wait_ge(gu_done, e * NCH + c + 1)
                if known(e, 1):
                    act.wait_ge(h_ready, e * NCH - NCH + c + 1)
                act.activation(silu_g[:, c, :], bank[c][0:CAP, 0:CH], ACT.Silu).then_inc(silu_ready, 1)

            def step(e, k):
                nxt = (k + 1) % RING
                if known(e, None, E - 1):
                    silu_gate(e, k, 0)
                if known(e, 1):
                    act.wait_ge(turn_b, e)
                    act.copy(hidT[:, 4:FK, :].rearrange("p a b -> p (a b)"), bank[4][:, 0:2 * CAP]).then_inc(turned_b, 1)
                if known(e, None, E - 2):
                    x_upper(e + 1, nxt)
                if known(e, 1, E - 2):
                    act.wait_ge(wgu_in[nxt % 2], (e + 1 - nxt % 2) * 16 + 32)
                    split_hi(e + 1, nxt, 0)
                if known(e, None, E - 1):
                    silu_gate(e, k, 1)
                if known(e, 1, E - 2):
                    split_hi(e + 1, nxt, 1)
                if known(e, None, E - 1):
                    silu_gate(e, k, 2)
                    act.wait_ge(turn_a, e + 1)
                    if known(e, 1):
                        act.wait_ge(down_done, e)
                    act.copy(hidT[:, 0:4, :].rearrange("p a b -> p (a b)"), bank[3][:, 0:4 * CAP]).then_inc(turned_a, 1)
                if known(e, 1, E - 2):
                    split_hi(e + 1, nxt, 2)

            x_upper(0, 0)
            copy_base(NT - 1)
            over_experts(act, step)
            act.wait_ge(y_var, 1)
            act.activation(std2[:, 1, :], std2[:, 0, :], ACT.Sqrt).then_inc(y_std, 1)
            act.wait_ge(y_rstd, 1)
            for t in range(NY_DVE, NY):
                act.activation(y_n[:, t, :], y[:, t, :], ACT.Identity, bias=std2[:, 3, t:t + 1],
                               scale=std2[:, 2, t:t + 1]).then_inc(y_norm_act, 1)

        @block.gpsimd
        def _(pool):
            def lower_x(j):
                pool.wait_ge(x_hi_made, j)
                if j >= 3:
                    pool.wait_ge(embed_done, j - 1)
                pool.tensor_tensor(x_lo0[:, j % 2, :], x_sb[:, j % XRING, :], x_hi0[:, j % 2, :].bitcast(F32),
                                   ALU.subtract).then_inc(x_lo_made, 1)

            lower_x(1)
            pool.wait_ge(x_lo_made, 1)
            lower_x(2)
            pool.wait_ge(wproj_hi_ready, 1)
            pool.tensor_tensor(wproj_lo[:, :], wproj_sb[:, 0, :], wproj_hi[:, :].bitcast(F32), ALU.subtract)\
                .then_inc(wproj_lo_ready, 1)
            for j in range(NT):
                if j + 3 < NT:
                    lower_x(j + 3)
                pool.wait_ge(qk_read, j + 1)
                pool.tensor_tensor(qk[:, j, :], rope_a[:, j % 2, :], rope_b[:, j % 2, :], ALU.add)\
                    .then_inc(qk_ready, 1)

            def spread_v(j):
                if j >= 2:
                    pool.wait_ge(att_psum, 2 * (j - 1))
                v = heads(vug[:, j, 0:D])
                for c in range(3):
                    last = pool.tensor_tensor(
                        v3[:, j % 2, 0:H * 3 * DH].rearrange("p (h c e) -> p h c e", h=H, c=3)[:, :, c, :], v,
                        vcoef[:, j * H:(j + 1) * H, c:c + 1].broadcast_to([TT, H, DH]), ALU.mult)
                last.then_inc(v3_ready, 1)

            def sum_mix(j):
                pool.wait_ge(mix_ready, 2 * (j + 1))
                m = mix[:, j % 2, :].rearrange("p (h c e) -> p h c e", h=H, c=3)
                pool.tensor_tensor(heads(o_sum[:, j % 2, :]), m[:, :, 0, :], m[:, :, 1, :], ALU.add)\
                    .then_inc(p_order, 1)
                pool.wait_ge(p_order, j + 1)
                if j >= SMALL:
                    pool.wait_ge(on_ready, j - SMALL + 1)
                pool.tensor_tensor(heads(o_att[:, j % SMALL, :]), heads(o_sum[:, j % 2, :]), m[:, :, 2, :], ALU.add)\
                    .then_inc(att_ready, 1)

            def expand_q(j):
                spread_q(pool, j, 1).then_inc(q_exp_pool, 1)

            expand_q(0)
            pool.memset(v3[:, :, H * 3 * DH:], 0.0).then_inc(v3_zero, 1)
            expand_q(1)
            pool.wait_ge(vcoef_ready, 1)
            spread_v(0)
            spread_v(1)
            for j in range(NT):
                if j + 2 < NT:
                    expand_q(j + 2)
                sum_mix(j)
                if j + 2 < NT:
                    spread_v(j + 2)

            for m in range(2 * FSK - 1):
                n, f = divmod(m, FSK)
                pool.wait_ge(silu_s_ready, m + 1)
                pool.wait_ge(up_s_ready, m + 1)
                pool.tensor_tensor(hsT[:, f, n * HALF:(n + 1) * HALF], silu_s[:, m % SBUFS, :], up_s[:, m % SBUFS, :],
                                   ALU.mult).then_inc(hs_ready, 1)
                if 2 <= m < NCH + 2:
                    c = m - 2
                    cols = slice(c * 2 * CH, (c + 1) * 2 * CH)
                    pool.wait_ge(w_hi_ready, c + 1)
                    pool.tensor_tensor(w_lo[:, 0, cols], wgu_sb[:, 0, cols], w_hi[:, 0, cols].bitcast(F32),
                                       ALU.subtract).then_inc(w_lo0_ready, 1)
                    pool.wait_ge(hs_ready, m + 1)
                    pool.wait_ge(w_lo0_ready, 2 * c + 1)
                    pool.tensor_tensor(w_b[KB:2 * KB, 0, cols], wgu_b[:, 0, cols], w_b[0:KB, 0, cols].bitcast(F32),
                                       ALU.subtract).then_inc(w_lo0_ready, 1)
                    pool.wait_ge(w_lo0_ready, 2 * c + 2)
            pool.wait_ge(h1_out, 32 * NT)
            pool.wait_ge(row_ready, 1)

            def gather(e):
                k = e % RING
                pool.indirect_dma_start(xg[:, k, :], None, h1_dram,
                                        bass.IndirectOffsetOnAxis(ap=row_i[:, e:e + 1], axis=0)).then_inc(xg_in[k], 16)

            for e in range(RING):
                gather(e)
            pool.wait_ge(base_ready, NT)
            pool.tensor_tensor(y_base[:, 1, :, :], y_base[:, 0, :, :], h1[:, :, :], ALU.add).then_inc(base_added, 1)
            pool.wait_ge(base_out, 16)
            for e in range(E - 1):
                if e + RING < E:
                    pool.wait_ge(x_psum, e + 1)
                    gather(e + RING)
                pool.wait_ge(out_ready, e + 1)
                if e >= 1:
                    pool.wait_ge(y_add, 16 * e)
                pool.indirect_dma_start(y_dram, bass.IndirectOffsetOnAxis(ap=row_i[:, e:e + 1], axis=0),
                                        o_exp[:, e % 2, :], None, compute_op=ALU.add).then_inc(y_add, 16)

        @block.vector
        def _(dve):
            order = [0]

            def link(ins):
                order[0] += 1
                ins.then_inc(v_order, 1)
                dve.wait_ge(v_order, order[0])

            dve.memset(ones[:, :], 1.0).then_inc(ones_ready, 1)
            for n, cols in enumerate((slice(0, WP1), slice(WP1, KX * D))):
                dve.wait_ge(wp_hi_ready, n + 1)
                dve.tensor_tensor(wp_lo[:, cols], wp_sb[:, cols], wp_hi[:, cols].bitcast(F32), ALU.subtract)\
                    .then_inc(wp_lo_ready, 1)
            dve.wait_ge(consts_in, 48)
            dve.tensor_scalar(tau[:, 0, :], par[:, P_TAU:P_TAU + H], -50.0, 30.0, ALU.max, ALU.min)\
                .then_inc(tau_clip, 1)
            dve.wait_ge(tau_exp, 1)
            link(dve.tensor_tensor(heads(mu_row[:, :]), heads(mu_in[:, :]),
                                   tau[0:1, 1, :].rearrange("p (h o) -> p h o", o=1).broadcast_to([1, H, DH]), ALU.mult))
            link(dve.tensor_scalar(tau[:, 0, :], tau[:, 1, :], cst[0:TT, C_T:C_T + 1], -float(DH) ** 0.5, ALU.add, ALU.mult))
            dve.reciprocal(tau[:, 2, :], tau[:, 0, :]).then_inc(tau_ready, 2)
            dve.wait_ge(proj_in, 32)
            for c, rows in enumerate((KA, KB)):
                wv = heads(wproj_sb[0:rows, c, QK:QK + D])
                mean = wv_mean[0:rows, c, :]
                link(dve.tensor_reduce(mean, wv, AX_X, ALU.add))
                link(dve.tensor_scalar(mean, mean, 1.0 / DH, None, ALU.mult))
                dve.tensor_tensor(wv, wv, mean.rearrange("p (h o) -> p h o", o=1)
                                  .broadcast_to([rows, H, DH]), ALU.subtract).then_inc(wv_ready, 1)

            def add_bias(j):
                dve.wait_ge(embed_done, j + 1)
                for to, c0, n in ((0, 0, D), (D, KA, KB)):
                    dve.tensor_tensor(h0[:, j, to:to + n], bank[j % 2][0:TT, c0:c0 + n],
                                      par[:, P_B + c0:P_B + c0 + n], ALU.add).then_inc(h0_ready, 1)

            def lower_h0T(j):
                dve.wait_ge(h0T_hi_ready, j + 1)
                dve.tensor_tensor(h0T_lo[:, j % 2, :], bank[2][0:KA, 0:2 * TT], h0T_hi[:, j % 2, :].bitcast(F32),
                                  ALU.subtract).then_inc(h0T_ready, 1)

            def rope(j):
                dve.wait_ge(qk_psum, j + 1)
                if j >= 2:
                    dve.wait_ge(qk_ready, j - 1)
                src = bank[3 + 3 * (j % 2)][0:TT, 0:QK].rearrange("p (h e) -> p h e", e=DH)
                cos = cst[0:TT, C_COS:C_COS + DH].rearrange("p (o e) -> p o e", o=1)
                sin = cst[0:TT, C_SIN:C_SIN + DH].rearrange("p (o e) -> p o e", o=1)
                a = rope_a[:, j % 2, :].rearrange("p (h e) -> p h e", e=DH)
                b = rope_b[:, j % 2, :].rearrange("p (h e) -> p h e", e=DH)
                hd = DH // 2
                dve.tensor_tensor(a, src, cos.broadcast_to([TT, 2 * H, DH]), ALU.mult)
                dve.tensor_tensor(b[:, :, 0:hd], src[:, :, hd:DH],
                                  sin[:, :, 0:hd].broadcast_to([TT, 2 * H, hd]), ALU.mult)
                dve.tensor_tensor(b[:, :, hd:DH], src[:, :, 0:hd],
                                  sin[:, :, hd:DH].broadcast_to([TT, 2 * H, hd]), ALU.mult).then_inc(qk_read, 1)

            def sum_squares(j):
                dve.wait_ge(sq_ready, j + 1)
                dve.tensor_reduce(norm2[:, j, :], squares[:, j % 2, :].rearrange("p (h e) -> p h e", e=DH),
                                  AX_X, ALU.add).then_inc(n2_ready, 1)

            def invert_norm(j):
                dve.wait_ge(norm_sqrt, j + 1)
                link(dve.tensor_scalar(norm2[:, j, :], rnorm[:, j, :], 1e-12, None, ALU.max))
                dve.reciprocal(rnorm[:, j, :], norm2[:, j, :]).then_inc(norm_ready, 1)

            def dot_u(j):
                dve.wait_ge(usum_done, j + 1)
                link(dve.tensor_tensor(u_bar[:, j % 2, :], bank[5][0:TT, 0:D], vug[:, j, D:2 * D], ALU.mult))
                dve.tensor_reduce(s_raw[:, j, :], heads(u_bar[:, j % 2, :]), AX_X, ALU.add).then_inc(s_ready, 1)

            def lower_u(j):
                dve.wait_ge(u_hi_ready, j + 1)
                dve.tensor_tensor(u_lo[:, j % 2, :], vug[:, j, D:2 * D],
                                  u_hi[:, j % 2, :].bitcast(F32), ALU.subtract).then_inc(u_lo_ready, 1)

            add_bias(0)
            add_bias(1)
            dve.wait_ge(wproj_hi_ready, 1)
            dve.tensor_tensor(wproj_b[KB:2 * KB, :], wproj_sb[0:KB, 1, :], wproj_b[0:KB, :].bitcast(F32),
                              ALU.subtract).then_inc(wproj_lo_ready, 1)
            lower_h0T(0)
            dve.wait_ge(mu_hi_ready, 1)
            dve.tensor_tensor(mu_lo[:, :], mu_row[:, :], mu_hi[:, :].bitcast(F32), ALU.subtract).then_inc(mu_lo_ready, 1)
            for j in range(NT):
                if j + 2 < NT:
                    add_bias(j + 2)
                if j + 1 < NT:
                    lower_h0T(j + 1)
                rope(j)
                lower_u(j)
                if j >= 1:
                    sum_squares(j - 1)
                    dot_u(j - 1)
                if j >= 2:
                    invert_norm(j - 2)
            sum_squares(NT - 1)
            dot_u(NT - 1)
            dve.wait_ge(s_ready, NT)
            dve.tensor_tensor(es_s[:, 1, :].rearrange("p (j h) -> p j h", j=NT), s_raw[:, :, :],
                              tau[:, 2, :].rearrange("p (o h) -> p o h", o=1).broadcast_to([TT, NT, H]), ALU.mult)\
                .then_inc(s_all, 1)
            invert_norm(NT - 2)

            def expand_q(j):
                spread_q(dve, j, 0).then_inc(q_exp_ready, 1)

            def mask(j, between=None):
                if j >= 2:
                    dve.wait_ge(att_psum, 2 * (j - 1))
                for g in range(3):
                    dve.wait_ge(score_done, 3 * j + g + 1)
                    dve.tensor_tensor(pT[:, j % 2, g * 4 * TT:(g + 1) * 4 * TT].rearrange("p (h t) -> p h t", h=4),
                                      bank[g][0:TT, 0:4 * TT].rearrange("p (h t) -> p h t", h=4),
                                      tri.rearrange("p (o t) -> p o t", o=1).broadcast_to([TT, 4, TT]),
                                      ALU.mult).then_inc(p_ready, 1)
                    if between and g == 0:
                        between()

            dve.wait_ge(sT_psum, 1)
            sT_ps = bank[5][0:NT * H, 0:TT].rearrange("p (i l) -> p i l", i=2)
            link(dve.tensor_reduce(s_max[:, :], sT_ps, AX_X, ALU.max))
            dve.tensor_tensor(sT[:, 1, :].rearrange("p (i l) -> p i l", i=2), sT_ps,
                              s_max[:, :].rearrange("p (i o) -> p i o", o=1).broadcast_to([NT * H, 2, L]),
                              ALU.subtract).then_inc(sT_sub, 1)
            expand_q(0)
            invert_norm(NT - 1)
            expand_q(1)
            dve.wait_ge(es_psum, 1)
            dve.tensor_copy(es_s[:, 0, :], bank[7][0:TT, 0:NT * H]).then_inc(es_ready, 1)
            dve.wait_ge(norm_ready, NT)
            dve.wait_ge(es_ready, 1)
            rq, rk = rnorm[:, :, 0:H], rnorm[:, :, H:2 * H]

            def by_tile(ap):
                return ap.rearrange("p (j h) -> p j h", j=NT)

            dve.tensor_tensor(by_tile(vcoef[:, :, 0]), by_tile(es_s[:, 0, :]), rk, ALU.mult)
            dve.tensor_tensor(by_tile(vcoef[:, :, 1]), by_tile(es_s[:, 1, :]), rk, ALU.mult)
            dve.tensor_copy(by_tile(vcoef[:, :, 2]), rk).then_inc(vcoef_ready, 1)

            def sigmoid_gates():
                dve.wait_ge(gate_exp, 1)
                link(dve.tensor_scalar(gates[:, 1, :, :], gates[:, 0, :, :], 1.0, None, ALU.add))
                dve.reciprocal(gates[:, 2, :, :], gates[:, 1, :, :]).then_inc(gate_ready, 1)

            mask(0, sigmoid_gates)
            sig1, sigh = gates[:, 2, :, 0:H], gates[:, 2, :, H:2 * H]
            rt = cst[0:TT, C_RT:C_RT + 1]
            a, b, c, d, e, sums = (small[:, n, :] for n in range(6))
            dve.wait_ge(gate_ready, 1)
            dve.tensor_tensor(by_tile(c), sig1, sigh, ALU.subtract)
            dve.tensor_tensor(by_tile(a), sigh, rq, ALU.mult)
            link(dve.tensor_scalar(by_tile(e), rq, rt, -1.0, ALU.mult, ALU.mult))
            link(dve.tensor_scalar(d, c, rt, None, ALU.mult))
            dve.tensor_tensor(by_tile(coef[:, :, 1]), by_tile(d), rq, ALU.mult)
            mask(1)
            expand_q(2)
            dve.wait_ge(cum_done, 1)
            link(dve.tensor_scalar(sums, bank[6][0:TT, 0:NT * H], 1e-12, None, ALU.add))
            dve.reciprocal(b, sums)
            link(dve.tensor_tensor(c, d, bank[6][0:TT, NT * H:2 * NT * H], ALU.mult))
            link(dve.tensor_tensor(by_tile(sums), by_tile(c), sigh, ALU.add))
            dve.tensor_tensor(coef[:, :, 2], sums, e, ALU.mult)
            dve.tensor_tensor(coef[:, :, 0], a, b, ALU.mult).then_inc(coef_ready, 1)
            dve.wait_ge(coef_ready, 1)

            def combine(j):
                if j >= 2:
                    dve.wait_ge(att_ready, j - 1)
                for g in range(2):
                    dve.wait_ge(att_psum, 2 * j + g + 1)
                    n = G6 * 3
                    dve.tensor_tensor(mix[:, j % 2, g * n * DH:(g + 1) * n * DH].rearrange("p (h e) -> p h e", e=DH),
                                      bank[4 + g][0:TT, 0:n * DH].rearrange("p (h e) -> p h e", e=DH),
                                      coef[:, j * H + g * G6:j * H + (g + 1) * G6, :].rearrange("p h (c o) -> p (h c) o", o=1)
                                      .broadcast_to([TT, n, DH]), ALU.mult).then_inc(mix_ready, 1)

            def variance_o(j):
                dve.wait_ge(osq_ready, j + 1)
                link(dve.tensor_reduce(o_var[:, j % SMALL, 2 * H:3 * H], heads(o_sq[:, j % 2, :]), AX_X, ALU.add))
                dve.tensor_scalar(o_var[:, j % SMALL, 0:H], o_var[:, j % SMALL, 2 * H:3 * H], 1.0 / DH, EPS, ALU.mult, ALU.add)\
                    .then_inc(ovar_ready, 1)

            def normalise_o(j):
                dve.wait_ge(ostd_ready, j + 1)
                link(dve.reciprocal(o_var[:, j % SMALL, 2 * H:3 * H], o_var[:, j % SMALL, H:2 * H]))
                if j >= SMALL:
                    dve.wait_ge(oT_psum, j - SMALL + 1)
                dve.tensor_tensor(heads(o_n[:, j % SMALL, :]), heads(o_att[:, j % SMALL, :]),
                                  o_var[:, j % SMALL, 2 * H:3 * H].rearrange("p (h o) -> p h o", o=1)
                                  .broadcast_to([TT, H, DH]), ALU.mult).then_inc(on_ready, 1)

            def residual(j):
                dve.wait_ge(wo_done, j + 1)
                if j >= SMALL:
                    dve.wait_ge(h1_ready, j - SMALL + 1)
                dve.tensor_tensor(r1[:, j % SMALL, :], bank[7][0:TT, 0:D], h0[:, j, 0:D], ALU.add).then_inc(r1_ready, 1)
                dve.wait_ge(r1_ready, j + 1)
                link(dve.bn_stats(bn1[:, j % SMALL, :], r1[:, j % SMALL, :]))
                link(dve.bn_aggr(mv1[:, j % SMALL, 0:2], bn1[:, j % SMALL, :]))
                dve.tensor_scalar(mv1[:, j % SMALL, 1:2], mv1[:, j % SMALL, 1:2], EPS, None, ALU.add).then_inc(r1_var, 1)

            def normalise_r(j):
                dve.wait_ge(r1_std, j + 1)
                link(dve.reciprocal(mv1[:, j % SMALL, 3:4], mv1[:, j % SMALL, 2:3]))
                dve.tensor_scalar(h1[:, j, :], r1[:, j % SMALL, :], mv1[:, j % SMALL, 0:1], mv1[:, j % SMALL, 3:4],
                                  ALU.subtract, ALU.mult).then_inc(h1_ready, 1)

            for i in range(1, NT):
                if 3 <= i + 1 < NT:
                    expand_q(i + 1)
                if i >= 3:
                    normalise_o(i - 3)
                if i >= 5:
                    residual(i - 5)
                if i >= 6:
                    normalise_r(i - 6)
                if i >= 2:
                    mask(i)
                combine(i - 1)
                if i >= 2:
                    variance_o(i - 2)
            normalise_o(NT - 3)
            residual(NT - 5)
            normalise_r(NT - 6)
            variance_o(NT - 2)
            combine(NT - 1)
            residual(NT - 4)
            normalise_o(NT - 2)
            normalise_r(NT - 5)
            variance_o(NT - 1)
            residual(NT - 3)
            normalise_r(NT - 4)
            normalise_o(NT - 1)
            residual(NT - 2)
            normalise_r(NT - 3)
            residual(NT - 1)
            normalise_r(NT - 2)
            normalise_r(NT - 1)
            dve.wait_ge(logit_ready, 1)

            def left(n):
                return rank_in[0:48, n % 3, :]

            def find(n):
                eight = slice(8 * n, 8 * n + 8)
                return dve.max_index(top_idx[:, eight], top_val[:, eight], left(n))

            for n in range(ROUNDS):
                eight = slice(8 * n, 8 * n + 8)
                dve.max(top_val[:, eight], left(n)).then_inc(top_max, 1)
                if n >= 1:
                    find(n - 1)
                if n < ROUNDS - 1:
                    dve.wait_ge(top_max, n + 1)
                    dve.match_replace(left(n + 1), top_val[:, eight], left(n), -3e38).then_inc(top_left, 1)
                    dve.wait_ge(top_left, n + 1)
            dve.wait_ge(top_max, ROUNDS)
            link(find(ROUNDS - 1))
            link(dve.tensor_copy(top_row[:, :], top_idx[:, 0:CAP]))
            dve.tensor_scalar(top_row[32:48, :], top_row[32:48, :], float(HALF), None, ALU.add).then_inc(top_ready, 1)
            dve.wait_ge(silu_s_ready, 2 * FSK)
            dve.wait_ge(up_s_ready, 2 * FSK)
            dve.tensor_tensor(hsT[:, FSK - 1, HALF:TOKENS], silu_s[:, (2 * FSK - 1) % SBUFS, :],
                              up_s[:, (2 * FSK - 1) % SBUFS, :], ALU.mult).then_inc(hs_last, 1)
            dve.wait_ge(rev_psum, 1)
            va, ia = top_T[:, 0, 0:E], top_T[:, 1, 0:E]
            vb, ib = bank[2][0:CAP, 0:E], bank[2][0:CAP, E:2 * E]
            dve.tensor_tensor(pick[:, 0, :], va, vb, ALU.max).then_inc(pick_ready, 1)
            dve.tensor_tensor(pick[:, 1, :], va, vb, ALU.is_ge)
            link(dve.tensor_tensor(pick[:, 2, :], ia, ib, ALU.subtract))
            link(dve.tensor_tensor(pick[:, 3, :], pick[:, 2, :], pick[:, 1, :], ALU.mult))
            link(dve.tensor_tensor(pick[:, 4, :], pick[:, 3, :], ib, ALU.add))
            dve.tensor_copy(row_i[:, :], pick[:, 4, :]).then_inc(row_ready, 1)
            dve.wait_ge(tokens_in, 16)
            dve.tensor_scalar(place[:, :], token_sb[:, :], pick[:, 4, E - 1:E], None, ALU.is_equal)\
                .then_inc(place_ready, 1)

            def x_lower(e, k):
                dve.wait_ge(x_hi_ready, e + 1)
                dve.tensor_tensor(x_lo[:, k % 2, :], bank[6][0:KA, 0:2 * CAP], x_hi[:, k % 2, :].bitcast(F32),
                                  ALU.subtract).then_inc(x_lo_ready, 1)

            def split_lo(e, k, c):
                dve.wait_ge(w_hi_ready, e * NCH + c + 1)
                cols = slice(c * 2 * CH, (c + 1) * 2 * CH)
                dve.tensor_tensor(w_lo[:, k % 2, cols], wgu_sb[:, k % 2, cols],
                                  w_hi[:, k % 2, cols].bitcast(F32), ALU.subtract).then_inc(w_lo_ready, 1)
                dve.tensor_tensor(w_b[KB:2 * KB, k % 2, cols], wgu_b[:, k % 2, cols],
                                  w_b[0:KB, k % 2, cols].bitcast(F32), ALU.subtract).then_inc(w_lo_ready, 1)

            def gated(e, k, c):
                dve.wait_ge(silu_ready, e * NCH + c + 1)
                if c == 0 and known(e, 2):
                    dve.wait_ge(turn_b, e - 1)
                dve.tensor_tensor(hid[:, k % 2, c * CH:(c + 1) * CH], silu_g[:, c, :], bank[c][0:CAP, CH:2 * CH],
                                  ALU.mult).then_inc(h_ready, 1)

            def step(e, k):
                nxt = (k + 1) % RING
                if known(e, None, E - 1):
                    gated(e, k, 0)
                if known(e, None, E - 2):
                    x_lower(e + 1, nxt)
                if known(e, 1, E - 2):
                    split_lo(e + 1, nxt, 0)
                if known(e, None, E - 1):
                    gated(e, k, 1)
                if known(e, 1, E - 2):
                    split_lo(e + 1, nxt, 1)
                if known(e, 1):
                    dve.wait_ge(down_done, e)
                    if known(e, 3):
                        dve.wait_ge(y_add, 16 * (e - 2))
                    dve.tensor_scalar(o_exp[:, (k - 1) % 2, :], bank[5][0:CAP, 0:D], score[:, bass.ds(e - 1, 1)], None,
                                      ALU.mult).then_inc(out_ready, 1)
                if known(e, None, E - 1):
                    gated(e, k, 2)
                if known(e, 1, E - 2):
                    split_lo(e + 1, nxt, 2)

            for c in range(NCH):
                split_lo(1, 1, c)
            x_lower(0, 0)
            dve.wait_ge(score_ready, 1)
            over_experts(dve, step)
            dve.wait_ge(y_in, 16)
            for t in range(NY + 1):
                if t < NY:
                    dve.wait_ge(last_psum, t + 1)
                    dve.tensor_tensor(y[:, t, :], y[:, t, :], bank[Y_BANKS[t]][0:YT, 0:D], ALU.add).then_inc(y_sum, 1)
                if t >= 1:
                    dve.wait_ge(y_sum, t)
                    last = dve.bn_stats(bn2[:, t - 1, :], y[:, t - 1, :])
            link(last)
            for t in range(NY):
                last = dve.bn_aggr(mv2[:, t, :], bn2[:, t, :])
            link(last)
            dve.tensor_scalar(std2[:, 0, :], mv2[:, :, 1], EPS, None, ALU.add).then_inc(y_var, 1)
            dve.wait_ge(y_std, 1)
            link(dve.reciprocal(std2[:, 2, :], std2[:, 1, :]))
            dve.scalar_tensor_tensor(std2[:, 3, :], mv2[:, :, 0], -1.0, std2[:, 2, :], ALU.mult, ALU.mult)\
                .then_inc(y_rstd, 1)
            for t in range(NY_DVE):
                dve.tensor_scalar(y_n[:, t, :], y[:, t, :], mv2[:, t, 0:1], std2[:, 2, t:t + 1],
                                  ALU.subtract, ALU.mult).then_inc(y_norm, 1)


def constants():
    import numpy as np
    c = np.zeros((128, C_N), np.float32)
    c[:, C_ID:C_ID + 128] = np.eye(128)
    m, l = np.arange(TT)[:, None], np.arange(TT)[None, :]
    c[:TT, C_TRI:C_TRI + TT] = (m // L == l // L) & (m <= l)
    c[:CAP, C_REV:C_REV + CAP] = np.eye(CAP)[::-1]
    pos = (np.arange(TT) % L).astype(np.float32)
    inv = (1.0 / 10000.0 ** (np.arange(0, DH, 2, dtype=np.float32) / DH)).astype(np.float32)
    ang = pos[:, None] * inv[None, :]
    c[:TT, C_COS:C_COS + DH] = np.repeat(np.cos(ang), 2, axis=-1)
    sin = np.repeat(np.sin(ang), 2, axis=-1)
    c[:TT, C_SIN:C_SIN + DH // 2] = -sin[:, :DH // 2]
    c[:TT, C_SIN + DH // 2:C_SIN + DH] = sin[:, DH // 2:]
    c[:DK, C_HM:C_HM + G6] = np.arange(DK)[:, None] // DH == np.arange(G6)[None, :]
    c[:TT, C_T] = pos + 1
    c[:TT, C_RT] = 1.0 / (pos + 1)
    return c


def layouts(i):
    import numpy as np

    def halves(w):
        return w.reshape(2, DK, -1).transpose(1, 0, 2)

    a = {}
    p = i["x"].reshape(IMAGES, 3, SIDE, PATCH, SIDE, PATCH).transpose(0, 2, 4, 3, 5, 1).reshape(NT, TT, KX, 128)
    a["x"] = p.transpose(0, 3, 2, 1).reshape(NT, 128, KX * TT)
    a["w_patch"] = i["L0_tok_W"].T.reshape(KX, 128, D).transpose(1, 0, 2).reshape(128, KX * D)
    wg = i["L0_attn_Wg"].reshape(H, 3, D)
    a["w_proj"] = np.concatenate([i["L0_attn_Wq"], i["L0_attn_Wk"], i["L0_attn_Wv"], i["L0_attn_Wu"],
                                         wg[:, 0], wg[:, 1]]).T
    a["w_o"] = halves(i["L0_attn_Wo"].T)
    row = np.concatenate([i["L0_tok_b"], i["L0_attn_prior_log_tau"].reshape(-1)])
    a["params"] = np.broadcast_to(row, (TT, P_N))
    a["mu"] = i["L0_attn_prior_mu"].reshape(1, D)
    a["consts"] = constants()
    a["token_no"] = np.broadcast_to(np.arange(TOKENS, dtype=np.float32).reshape(YT, NY).T.reshape(-1), (CAP, TOKENS))
    gate = i["L0_ffn_gate_weight"]
    a["w_gate"] = halves(np.concatenate([gate, gate]).T)
    wgu = np.stack([i["L0_ffn_Wg"].reshape(E, NCH, CH, D), i["L0_ffn_Wu"].reshape(E, NCH, CH, D)], axis=2)
    a["w_gu"] = wgu.reshape(E, 2 * F, D).transpose(0, 2, 1)
    a["w_d"] = i["L0_ffn_Wd"].reshape(E, D, FK, 128).transpose(0, 3, 2, 1)
    a["ws_gu"] = halves(np.concatenate([i["L0_ffn_Ws_g"], i["L0_ffn_Ws_u"]]).T)
    a["ws_d"] = i["L0_ffn_Ws_d"].reshape(D, FSK, 128).transpose(2, 1, 0)
    return {k: np.ascontiguousarray(v) for k, v in a.items()}


def kernel(**inputs):
    import numpy as np
    from concourse import bacc
    from concourse.bass_utils import run_bass_kernel_spmd

    arrays = layouts({k: np.asarray(v) for k, v in inputs.items()})
    nc = bacc.Bacc("TRN2", target_bir_lowering=False, num_devices=1)
    args = [nc.dram_tensor(k, v.shape, mybir.dt.from_np(v.dtype), kind="ExternalInput").ap() for k, v in arrays.items()]
    out = nc.dram_tensor("out", (TOKENS, D), F32, kind="ExternalOutput").ap()
    build(nc, *args, out)
    r = run_bass_kernel_spmd(nc, [arrays], core_ids=[0])
    return r.results[0]["out"].reshape(IMAGES, L, D)
```
